# Optimizing a Trainium2 kernel written in Bass

```python
import numpy as np
import jax
import jax.numpy as jnp

def _softmax(x, axis=-1):
    return jax.nn.softmax(x, axis=axis)

def _gelu(x):
    return jax.nn.gelu(x, approximate=True)

def _silu(x):
    return jax.nn.silu(x)

def _sigmoid(x):
    return jax.nn.sigmoid(x)

def _layernorm(x, axis=-1, eps=1e-05):
    m = jnp.mean(x, axis=axis, keepdims=True)
    v = jnp.var(x, axis=axis, keepdims=True)
    return (x - m) / jnp.sqrt(v + eps)

def _scatter_add(tgt, idx, src, axis=0):
    return tgt.at[idx].add(src)

def _segment_sum(src, seg, n):
    return jax.ops.segment_sum(src, seg, n)
kernel_name = 'mk_decoder_preln_d1_seqx_r4_966d47'

def setup_inputs(seed: int=0):
    np.random.seed(seed)
    _w = jnp.asarray

    def _rec_inputs():
        import jax
        import jax.numpy as jnp
        _rk = jax.random.key(seed)
        x = -0.000125 + 0.9999 * jax.random.normal(jax.random.fold_in(_rk, 1), (16, 256, 256), jnp.float32)
        _lenS = 256 - jax.random.randint(jax.random.fold_in(_rk, 7), (16,), 0, max(1, 256 // 4) + 1, jnp.int32)
        _lenS2 = 77 - jax.random.randint(jax.random.fold_in(_rk, 8), (16,), 0, max(1, 77 // 4) + 1, jnp.int32)
        _ctx_768P = jax.random.normal(jax.random.fold_in(_rk, 11), (16, 16, 192), jnp.float32)
        _ctx_768c = jax.random.dirichlet(jax.random.fold_in(_rk, 511), 0.3 * jnp.ones((16,), jnp.float32), (16, 77))
        _ctx_768t = jnp.einsum('bsk,bkd->bsd', _ctx_768c, _ctx_768P)
        _ctx_768t = _ctx_768t * jax.lax.rsqrt(jnp.mean(jnp.square(_ctx_768t)) + 1e-12) * 0.953939
        ctx_768 = 0.00272024 + 0.999456 * (_ctx_768t + 0.3 * jax.random.normal(jax.random.fold_in(_rk, 611), (16, 77, 192), jnp.float32))
        return (x, ctx_768)
    x, ctx_768 = _rec_inputs()

    def _L0_attn_setup():
        import jax, jax.numpy as jnp
        import numpy as np
        WS = 8
        H = 16
        SHIFT = 4

        def _relative_position_index(ws):
            coords = np.stack(np.meshgrid(np.arange(ws), np.arange(ws), indexing='ij'))
            cf = coords.reshape(2, -1)
            rel = cf[:, :, None] - cf[:, None, :]
            rel = rel.transpose(1, 2, 0).astype(np.int64)
            rel[..., 0] += ws - 1
            rel[..., 1] += ws - 1
            rel[..., 0] *= 2 * ws - 1
            return rel.sum(-1)
        key = jax.random.key(seed)
        ks = jax.random.split(key, 5)
        B, N, C = (4, 2048, 256)
        x = jax.random.normal(ks[0], (B, N, C), dtype=jnp.float32)
        w_qkv = jax.random.normal(ks[1], (C, 3 * C), dtype=jnp.float32) * 0.02
        b_qkv = jnp.zeros((3 * C,), dtype=jnp.float32)
        w_proj = jax.random.normal(ks[2], (C, C), dtype=jnp.float32) * 0.02
        b_proj = jnp.zeros((C,), dtype=jnp.float32)
        bias_table = jax.random.normal(ks[3], ((2 * WS - 1) ** 2, H), dtype=jnp.float32) * 0.02
        return {'x': x, 'w_qkv': w_qkv, 'b_qkv': b_qkv, 'w_proj': w_proj, 'b_proj': b_proj, 'bias_table': bias_table}
    _L0_attn_all = _L0_attn_setup()
    _L0_attn_in = {k: v for k, v in _L0_attn_all.items() if k in ('w_qkv', 'b_qkv', 'w_proj', 'b_proj', 'bias_table')}
    del _L0_attn_all

    def _L0_xattn_setup():
        import jax, jax.numpy as jnp
        import numpy as np
        HEADS = 16
        DIM_HEAD = 64
        SCALE = DIM_HEAD ** (-0.5)
        QUERY_DIM = 256
        CONTEXT_DIM = 192
        INNER_DIM = HEADS * DIM_HEAD
        key = jax.random.key(seed)
        ks = jax.random.split(key, 7)
        B, Nq, Nk = (8, 1024, 77)
        x = jax.random.normal(ks[0], (B, Nq, QUERY_DIM), dtype=jnp.float32)
        context = jax.random.normal(ks[1], (B, Nk, CONTEXT_DIM), dtype=jnp.float32)
        Wq = jax.random.normal(ks[2], (QUERY_DIM, INNER_DIM), dtype=jnp.float32) * QUERY_DIM ** (-0.5)
        Wk = jax.random.normal(ks[3], (CONTEXT_DIM, INNER_DIM), dtype=jnp.float32) * CONTEXT_DIM ** (-0.5)
        Wv = jax.random.normal(ks[4], (CONTEXT_DIM, INNER_DIM), dtype=jnp.float32) * CONTEXT_DIM ** (-0.5)
        Wo = jax.random.normal(ks[5], (INNER_DIM, QUERY_DIM), dtype=jnp.float32) * INNER_DIM ** (-0.5)
        bo = jnp.zeros((QUERY_DIM,), dtype=jnp.float32)
        return {'x': x, 'context': context, 'Wq': Wq, 'Wk': Wk, 'Wv': Wv, 'Wo': Wo, 'bo': bo}
    _L0_xattn_all = _L0_xattn_setup()
    _L0_xattn_in = {k: v for k, v in _L0_xattn_all.items() if k in ('Wq', 'Wk', 'Wv', 'Wo', 'bo')}
    del _L0_xattn_all

    def _L0_ffn_setup():
        import jax, jax.numpy as jnp
        import numpy as np
        DIM = 256
        HIDDEN = 1024
        E = 8
        B, S = (2, 1024)
        key = jax.random.key(seed)
        ks = jax.random.split(key, 8)
        sd = 1.0 / np.sqrt(DIM)
        sh = 1.0 / np.sqrt(HIDDEN)
        return {'x': jax.random.normal(ks[0], (B, S, DIM), dtype=jnp.float32), 'router_w': jax.random.uniform(ks[1], (DIM, E), jnp.float32, -sd, sd), 'router_b': jax.random.uniform(ks[2], (E,), jnp.float32, -sd, sd), 'w1': jax.random.uniform(ks[3], (E, DIM, 2 * HIDDEN), jnp.float32, -sd, sd), 'b1': jax.random.uniform(ks[4], (E, 2 * HIDDEN), jnp.float32, -sd, sd), 'w2': jax.random.uniform(ks[5], (E, HIDDEN, DIM), jnp.float32, -sh, sh), 'b2': jax.random.uniform(ks[6], (E, DIM), jnp.float32, -sh, sh)}
    _L0_ffn_all = _L0_ffn_setup()
    _L0_ffn_in = {k: v for k, v in _L0_ffn_all.items() if k in ('router_w', 'router_b', 'w1', 'b1', 'w2', 'b2')}
    del _L0_ffn_all
    return {'x': x, 'ctx_768': ctx_768, 'L0_attn_w_qkv': _L0_attn_in['w_qkv'], 'L0_attn_b_qkv': _L0_attn_in['b_qkv'], 'L0_attn_w_proj': _L0_attn_in['w_proj'], 'L0_attn_b_proj': _L0_attn_in['b_proj'], 'L0_attn_bias_table': _L0_attn_in['bias_table'], 'L0_xattn_Wq': _L0_xattn_in['Wq'], 'L0_xattn_Wk': _L0_xattn_in['Wk'], 'L0_xattn_Wv': _L0_xattn_in['Wv'], 'L0_xattn_Wo': _L0_xattn_in['Wo'], 'L0_xattn_bo': _L0_xattn_in['bo'], 'L0_ffn_router_w': _L0_ffn_in['router_w'], 'L0_ffn_router_b': _L0_ffn_in['router_b'], 'L0_ffn_w1': _L0_ffn_in['w1'], 'L0_ffn_b1': _L0_ffn_in['b1'], 'L0_ffn_w2': _L0_ffn_in['w2'], 'L0_ffn_b2': _L0_ffn_in['b2']}

def reference(x, ctx_768, L0_attn_w_qkv, L0_attn_b_qkv, L0_attn_w_proj, L0_attn_b_proj, L0_attn_bias_table, L0_xattn_Wq, L0_xattn_Wk, L0_xattn_Wv, L0_xattn_Wo, L0_xattn_bo, L0_ffn_router_w, L0_ffn_router_b, L0_ffn_w1, L0_ffn_b1, L0_ffn_w2, L0_ffn_b2):
    import jax
    import jax.numpy as jnp

    def _L0_attn_ref(x, w_qkv, b_qkv, w_proj, b_proj, bias_table):
        import jax, jax.numpy as jnp
        import numpy as np
        WS = 8
        H = 16
        SHIFT = 4

        def _relative_position_index(ws):
            coords = np.stack(np.meshgrid(np.arange(ws), np.arange(ws), indexing='ij'))
            cf = coords.reshape(2, -1)
            rel = cf[:, :, None] - cf[:, None, :]
            rel = rel.transpose(1, 2, 0).astype(np.int64)
            rel[..., 0] += ws - 1
            rel[..., 1] += ws - 1
            rel[..., 0] *= 2 * ws - 1
            return rel.sum(-1)
        B, N, C = x.shape
        D = C // H
        pad_len = -N % WS
        if pad_len:
            x = jnp.pad(x, ((0, 0), (0, pad_len), (0, 0)))
        Np = N + pad_len
        if SHIFT > 0:
            x = jnp.roll(x, -SHIFT, axis=1)
        nw = Np // WS
        xw = x.reshape(B * nw, WS, C)
        qkv = xw @ w_qkv + b_qkv
        q, k, v = jnp.split(qkv, 3, axis=-1)

        def to_heads(t):
            return t.reshape(-1, WS, H, D).transpose(0, 2, 1, 3)
        q, k, v = (to_heads(q), to_heads(k), to_heads(v))
        attn = jnp.einsum('bhqd,bhkd->bhqk', q, k) * D ** (-0.5)
        idx = _relative_position_index(WS)[:WS, :WS]
        bias = bias_table[idx.reshape(-1)].reshape(WS, WS, H)
        bias = bias.transpose(2, 0, 1)
        attn = jax.nn.softmax(attn + bias[None], axis=-1)
        out = jnp.einsum('bhqk,bhkd->bhqd', attn, v)
        out = out.transpose(0, 2, 1, 3).reshape(-1, WS, C)
        out = out @ w_proj + b_proj
        out = out.reshape(B, Np, C)
        if SHIFT > 0:
            out = jnp.roll(out, SHIFT, axis=1)
        return out[:, :N, :]

    def _L0_xattn_ref(x, context, Wq, Wk, Wv, Wo, bo):
        import jax, jax.numpy as jnp
        import numpy as np
        HEADS = 16
        DIM_HEAD = 64
        SCALE = DIM_HEAD ** (-0.5)
        QUERY_DIM = 256
        CONTEXT_DIM = 192
        INNER_DIM = HEADS * DIM_HEAD
        B, Nq, _ = x.shape
        Nk = context.shape[1]
        q = x @ Wq
        k = context @ Wk
        v = context @ Wv
        q = q.reshape(B, Nq, HEADS, DIM_HEAD).transpose(0, 2, 1, 3)
        k = k.reshape(B, Nk, HEADS, DIM_HEAD).transpose(0, 2, 1, 3)
        v = v.reshape(B, Nk, HEADS, DIM_HEAD).transpose(0, 2, 1, 3)
        sim = jnp.einsum('bhid,bhjd->bhij', q, k) * SCALE
        attn = jax.nn.softmax(sim, axis=-1)
        out = jnp.einsum('bhij,bhjd->bhid', attn, v)
        out = out.transpose(0, 2, 1, 3).reshape(B, Nq, INNER_DIM)
        return out @ Wo + bo

    def _L0_ffn_ref(x, router_w, router_b, w1, b1, w2, b2):
        import jax, jax.numpy as jnp
        import numpy as np
        DIM = 256
        HIDDEN = 1024
        E = 8
        B, S = (2, 1024)
        logits = jnp.einsum('bsd,de->bse', x, router_w) + router_b
        probs = jax.nn.softmax(logits, axis=-1)
        top1 = jnp.argmax(probs, axis=-1)
        out = jnp.zeros_like(x)
        for i in range(E):
            h = jnp.einsum('bsd,df->bsf', x, w1[i]) + b1[i]
            a, g = jnp.split(h, 2, axis=-1)
            y = jnp.einsum('bsh,hd->bsd', a * jax.nn.sigmoid(g), w2[i]) + b2[i]
            out = out + jnp.where((top1 == i)[..., None], y, 0.0)
        return out
    x = x + _L0_attn_ref(_layernorm(x, axis=-1), L0_attn_w_qkv, L0_attn_b_qkv, L0_attn_w_proj, L0_attn_b_proj, L0_attn_bias_table)
    x = x + _L0_xattn_ref(_layernorm(x, axis=-1), ctx_768, L0_xattn_Wq, L0_xattn_Wk, L0_xattn_Wv, L0_xattn_Wo, L0_xattn_bo)
    x = x + _L0_ffn_ref(_layernorm(x, axis=-1), L0_ffn_router_w, L0_ffn_router_b, L0_ffn_w1, L0_ffn_b1, L0_ffn_w2, L0_ffn_b2)
    return x

_drawn_inputs = setup_inputs


def setup_inputs(seed=0):
    import zlib

    import numpy as np

    out = dict(_drawn_inputs(seed))
    spreads = {'L0_attn_b_qkv': (0.0, 0.1), 'L0_attn_b_proj': (0.0, 0.1), 'L0_xattn_bo': (0.0, 0.1)}
    factors = {'L0_attn_bias_table': 31.998, 'L0_ffn_b1': 5.971, 'L0_ffn_b2': 3.584}
    for name, (base, spread) in spreads.items():
        noise = np.random.default_rng([zlib.crc32(name.encode()), seed]).standard_normal(out[name].shape)
        drawn = base * np.exp(spread * noise) if base else spread * noise
        out[name] = jnp.asarray(drawn.astype(out[name].dtype))
    for name, factor in factors.items():
        out[name] = (out[name] * factor).astype(out[name].dtype)
    return out
```

```python
from contextlib import ExitStack

import concourse.bass as bass
from concourse import mybir

F32 = mybir.dt.float32
BF16 = mybir.dt.bfloat16
I32 = mybir.dt.int32
U32 = mybir.dt.uint32
ALU = mybir.AluOpType
ACT = mybir.ActivationFunctionType
X = mybir.AxisListType.X

P = 128
B, N, C = 16, 256, 256
KC = C // P
WS, SHIFT = 8, 4
H, D1 = 16, 16
D2 = 64
INNER = H * D2
CH = INNER // P
CTX, CTXD = 77, 192
GB = 4
NG = B // GB
BLK = N // WS
E, HID = 8, 1024
HC = HID // P
ET = 256
NT = B * N // ET + E - 1
TT = B * N // P
EPS = 1e-5

A_ORDER = (["XN2"] + [f"Q{n}" for n in range(4)] + ["NM", "S0", "S1", "S2", "S3", "S4", "S5", "O0", "S6", "S7"]
           + ["O1", "O2", "O3", "CTX'", "K0'", "K1'", "XN3"])
D_ORDER = [f"MAX{n}" for n in range(8)] + [f"PV{v}" for v in range(8)] + ["X2", "PROJ'", "V0'", "V1'", "LOG"]
A_FIRST = ["CTX'", "K0'", "K1'"]
D_FIRST = ["PROJ'", "V0'", "V1'"]
A_BANKS, D_BANKS = 4, 2
assert GB * len(A_ORDER) % A_BANKS == 0 and GB * len(D_ORDER) % D_BANKS == 0
WA_ITEMS, WD_ITEMS = 8, 12
TMP_ITEMS = 2 * WS


def at(order, first, banks, name, j, b):
    if isinstance(j, int) and j < 0:
        return first.index(name), first.index(name) % banks
    k = len(first) + order.index(name)
    return j * len(order) + k, (b * len(order) + k) % banks


class Steps:

    def __init__(self, eng, sem):
        self.eng, self.sem, self.before, self.per_turn, self.turn, self.n = eng, sem, 0, 0, 0, 0

    def loop(self, turn, per_turn):
        self.before, self.n, self.turn, self.per_turn = self.before + self.n, 0, turn, per_turn

    def turned(self):
        assert self.n == self.per_turn, f"{self.sem}: {self.n} steps in a turn"
        self.n = 0

    def done(self, ins):
        ins.then_inc(self.sem, 1)
        self.n += 1
        self.eng.wait_ge(self.sem, self.turn * self.per_turn + (self.before + self.n))


def then(eng, ins, sem, value):
    ins.then_inc(sem, 1)
    eng.wait_ge(sem, value)


def decoder_layer(nc, x, ctx_768, w_qkv, b_qkv, w_proj, b_proj, bias_table, Wq, Wk, Wv, Wo, bo,
                  router_w, router_b, w1, b1, w2, b2, out):
    sorted_x = nc.dram_tensor("sorted_x", (NT * ET, C), F32, kind="Internal").ap()
    sorted_y = nc.dram_tensor("sorted_y", (NT * ET, C), F32, kind="Internal").ap()
    x_flat = x.rearrange("b n c -> b (n c)")

    def half_of(ap, j, half):
        rows = ap[bass.ds(j, 1)].rearrange("a (k r) c -> r (a k) c", r=WS)
        return rows[SHIFT:WS] if half == 0 else rows[0:SHIFT]

    with ExitStack() as whole:
        def keep(name, shape, dt=F32):
            return whole.enter_context(nc.sbuf_tensor(name, shape, dt))

        ident = keep("ident", [P, P])
        identb = keep("identb", [P, P], BF16)
        x2 = keep("x2", [P, B, 2, C])
        logits = keep("logits", [P, B, 2, E])
        ln3 = keep("ln3", [P, B, 2, 2])
        b1T = keep("b1T", [P, E, 2 * HC])

        trunk(nc, whole, locals())
        experts(nc, whole, locals())


def trunk(nc, outer, v):
    x, x_flat, ctx_768, half_of = v["x"], v["x_flat"], v["ctx_768"], v["half_of"]
    ident, identb, x2, logits, ln3, b1T = (v[k] for k in ("ident", "identb", "x2", "logits", "ln3", "b1T"))
    sorted_x = v["sorted_x"]
    with ExitStack() as st:
        def sb(name, shape, dt=F32):
            return st.enter_context(nc.sbuf_tensor(name, shape, dt))

        def sem(name):
            return st.enter_context(nc.semaphore(name))

        psA = st.enter_context(nc.psum_tensor("psA", [P, A_BANKS, 512], F32))
        psD = st.enter_context(nc.psum_tensor("psD", [P, D_BANKS, 512], F32))
        psWA = st.enter_context(nc.psum_tensor("psWA", [P, 512], F32))
        psWD = st.enter_context(nc.psum_tensor("psWD", [P, 512], F32))

        wqkv = sb("wqkv", [P, KC, 3 * C])
        wproj = sb("wproj", [P, KC, C])
        wq = sb("wq", [P, KC, INNER])
        wk = sb("wk", [P, KC, INNER])
        wv = sb("wv", [P, KC, INNER])
        wo = sb("wo", [P, CH, C])
        rw = sb("rw", [P, KC, E])
        bqkv_b = sb("bqkv_b", [P, 3 * C])
        bproj_b = sb("bproj_b", [P, C])
        bo_b = sb("bo_b", [P, C])
        rb_b = sb("rb_b", [P, E])
        relbias = sb("relbias", [P, WS, WS * H])
        head_row = sb("head_row", [P, H, CTX], BF16)
        half_exp = sb("half_exp", [P, WS])
        eps = sb("eps", [P, WS])

        xw = sb("xw", [P, WS, C])
        tmp1 = sb("tmp1", [P, WS, C])
        products = [xw, tmp1]
        idle = sb("idle", [P, 1])
        st1 = sb("st1", [P, WS, 6])
        mv1 = sb("mv1", [P, WS, 2])
        ve1 = sb("ve1", [P, WS])
        rs1 = sb("rs1", [P, WS])
        xnT = sb("xnT", [P, KC, WS, P])
        qkv = sb("qkv", [P, WS, 3 * C])
        probs = sb("probs", [P, WS, WS * H])
        red = sb("red", [P, WS * H])
        oT = sb("oT", [P, KC, GB, WS, BLK])

        xb = sb("xb", [P, 2, 2, C])
        ctx = sb("ctx", [P, 2, CTXD])
        x1 = sb("x1", [P, 2, C])
        xn = sb("xn", [P, 2, C])
        st2 = sb("st2", [P, 2, 2, 6])
        mv2 = sb("mv2", [P, 2, 2, 2])
        ve2 = sb("ve2", [P, 2, 2])
        rs2 = sb("rs2", [P, 2, 2])
        xT = sb("xT", [P, KC, 2 * P])
        ctxT = sb("ctxT", [P, KC, P])
        qT = sb("qT", [P, CH, 2 * P])
        qTb = sb("qTb", [P, CH, 2 * P], BF16)
        kT = sb("kT", [P, CH, 2, CTX])
        kTb = sb("kTb", [P, CH, 2, CTX], BF16)
        vo = sb("vo", [P, H, 2 * D2])
        nm = sb("nm", [P, 2, H], BF16)
        nmT = sb("nmT", [P, 2 * P], BF16)
        pT = sb("pT", [P, 4, 2 * N])
        rden = sb("rden", [P, 4])
        o2 = sb("o2", [P, 2, 2, 4 * D2])
        xn3 = o2[:, 0]
        b1rows = o2[:, 0, 0, 0:P]
        o2T = sb("o2T", [P, CH, N])

        weights = sem("weights")
        zeros_in = sem("zeros_in")
        pool_step, act_step, vec_step = sem("pool_step"), sem("act_step"), sem("vec_step")
        identities = sem("identities")
        xw_in = sem("xw_in")
        tile_in = [sem("tile_in0"), sem("tile_in1")]
        a_full, a_done = sem("a_full"), sem("a_done")
        d_full, d_done = sem("d_full"), sem("d_done")
        wa_full, wa_done = sem("wa_full"), sem("wa_done")
        wd_full, wd_done = sem("wd_full"), sem("wd_done")
        var1, rstd1, normed1 = sem("var1"), sem("rstd1"), sem("normed1")
        product, consumed = sem("product"), sem("consumed")
        shifted, exped, probs_ready = sem("shifted"), sem("exped"), sem("probs_ready")
        xb_biased, x1_biased = sem("xb_biased"), sem("x1_biased")
        var2, rstd2, normed2 = sem("var2"), sem("rstd2"), sem("normed2")
        var3, rstd3, normed3 = sem("var3"), sem("rstd3"), sem("normed3")
        b1_in, b1_turned, b1_kept = sem("b1_in"), sem("b1_turned"), sem("b1_kept")
        N_WEIGHTS = 13 + WS

        block = st.enter_context(nc.Block())

        def A(name, j, b):
            return at(A_ORDER, A_FIRST, A_BANKS, name, j, b)

        def Dd(name, j, b):
            return at(D_ORDER, D_FIRST, D_BANKS, name, j, b)

        @block.sync
        def _(sp):
            def load_windows(n):
                for i in range(GB):
                    rows = x_flat[bass.ds(n * GB + i, 1), SHIFT * C:SHIFT * C + (BLK - 1) * WS * C]
                    sp.dma_start(xw[i * BLK:(i + 1) * BLK - 1, :, :],
                                 rows.rearrange("a (w f) -> (a w) f", f=WS * C)).then_inc(xw_in, 16)
                seqs = x_flat[bass.ds(n * GB, GB)]
                sp.dma_start(xw[BLK - 1::BLK, 0:SHIFT, :], seqs[:, (N - SHIFT) * C:N * C]).then_inc(xw_in, 16)
                sp.dma_start(xw[BLK - 1::BLK, SHIFT:WS, :], seqs[:, 0:SHIFT * C]).then_inc(xw_in, 16)

            def load_tiles(j, b):
                for half in range(2):
                    sp.dma_start(xb[:, b % 2, half, :], half_of(x, j, half)).then_inc(tile_in[b % 2], 16)
                sp.dma_start(ctx[0:CTX, b % 2, :], ctx_768[bass.ds(j, 1)].rearrange("a k c -> (a k) c"))\
                    .then_inc(tile_in[b % 2], 16)

            load_windows(0)
            sp.dma_start(b1rows, v["b1"].rearrange("e (c p) -> (e c) p", p=P)).then_inc(b1_in, 16)
            sp.dma_start(wqkv[:], v["w_qkv"].rearrange("(k p) n -> p k n", p=P)).then_inc(weights, 16)
            sp.dma_start(bqkv_b[:], v["b_qkv"].partition_broadcast(P)).then_inc(weights, 16)
            for key in range(WS):
                row = 7 * (2 * WS - 1) + (WS - 1) - key
                sp.dma_start(relbias[:, key, :], v["bias_table"][row:row + WS, :].rearrange("a h -> (a h)")
                             .partition_broadcast(P)).then_inc(weights, 16)
            sp.dma_start(wproj[:], v["w_proj"].rearrange("(k p) n -> p k n", p=P)).then_inc(weights, 16)
            sp.dma_start(bproj_b[:], v["b_proj"].partition_broadcast(P)).then_inc(weights, 16)
            load_tiles(0, 0)
            load_tiles(1, 1)
            sp.dma_start(wk[:, 0, :], v["Wk"][0:P, :]).then_inc(weights, 16)
            sp.dma_start(wk[0:CTXD - P, 1, :], v["Wk"][P:CTXD, :]).then_inc(weights, 16)
            sp.dma_start(wv[:, 0, :], v["Wv"][0:P, :]).then_inc(weights, 16)
            sp.dma_start(wv[0:CTXD - P, 1, :], v["Wv"][P:CTXD, :]).then_inc(weights, 16)
            sp.dma_start(wq[:], v["Wq"].rearrange("(k p) n -> p k n", p=P)).then_inc(weights, 16)
            sp.dma_start(wo[:], v["Wo"].rearrange("(k p) n -> p k n", p=P)).then_inc(weights, 16)
            sp.dma_start(bo_b[:], v["bo"].partition_broadcast(P)).then_inc(weights, 16)
            sp.dma_start(rw[:], v["router_w"].rearrange("(k p) n -> p k n", p=P)).then_inc(weights, 16)
            sp.dma_start(rb_b[:], v["router_b"].partition_broadcast(P)).then_inc(weights, 16)
            sp.wait_ge(pool_step, 15)
            for row in range(0, NT * ET, CH * P):
                k = min(CH, (NT * ET - row) // P)
                sp.dma_start(sorted_x[row:row + k * P, :].rearrange("(k p) c -> p k c", p=P), o2T[:, 0:k, :])\
                    .then_inc(zeros_in, 16)

            def turn(g, more):
                if more:
                    sp.wait_ge(consumed, 2 + TMP_ITEMS * (g + 1))
                    load_windows(g + 1)
                for b in range(GB):
                    if not more and b >= GB - 2:
                        continue
                    j = g * GB + b
                    sp.wait_ge(a_full, A("XN2", j, b)[0] + 1)
                    load_tiles(j + 2, b)

            with sp.Fori(0, NG - 1) as g:
                turn(g, True)
            turn(NG - 1, False)

        @block.gpsimd
        def _(pool):
            s = Steps(pool, pool_step)
            s.done(nc.gpsimd.memset(ident[:], 0.0))
            s.done(nc.gpsimd.memset(identb[:], 0.0))
            for m in (ident, identb):
                nc.gpsimd.affine_select(out=m[:], in_=m[:], compare_op=ALU.not_equal, fill=1.0, base=0,
                                        pattern=[[-1, P]], channel_multiplier=1).then_inc(identities, 1)
            s.done(nc.gpsimd.memset(half_exp[:], -0.5))
            s.done(nc.gpsimd.memset(eps[:], EPS))
            s.done(nc.gpsimd.memset(head_row[:], 0.0))
            s.done(nc.gpsimd.affine_select(out=head_row[:], in_=head_row[:], compare_op=ALU.not_equal, fill=1.0,
                                           base=0, pattern=[[-1, H], [0, CTX]], channel_multiplier=1))
            s.done(nc.gpsimd.memset(ctxT[:], 0.0))
            s.done(nc.gpsimd.memset(wk[CTXD - P:P, 1, :], 0.0))
            s.done(nc.gpsimd.memset(wv[CTXD - P:P, 1, :], 0.0))
            s.done(nc.gpsimd.memset(kT[:], 0.0))
            s.done(nc.gpsimd.memset(kTb[:], 0.0))
            s.done(nc.gpsimd.memset(nmT[:], 0.0))
            s.done(nc.gpsimd.memset(pT[:], 0.0))
            s.done(nc.gpsimd.memset(o2T[:], 0.0))
            nc.gpsimd.memset(vo[:], 1.0).then_inc(identities, 1)
            pool.wait_ge(identities, 3)

            def rstd(variance, ve, rs, k, ready, signal, value):
                pool.wait_ge(ready, value)
                s.done(nc.gpsimd.tensor_tensor(ve, variance, eps[:, 0:k], ALU.add))
                then(pool, nc.gpsimd.tensor_tensor(rs, ve, half_exp[:, 0:k], ALU.pow), signal, value)

            def rstd1_of(n):
                rstd(mv1[:, :, 1], ve1[:], rs1[:], WS, var1, rstd1, n + 1)

            def make_product(n, i, query, probabilities):
                item = n * TMP_ITEMS + i
                pool.wait_ge(consumed, item + 1)
                if probabilities:
                    a = qkv[:, :, 2 * C:3 * C].rearrange("p k (h d) -> p k h d", h=H)
                    w = probs[:, :, query * H:(query + 1) * H].unsqueeze(3).to_broadcast([P, WS, H, D1])
                    o = products[i % 2][:].rearrange("p k (h d) -> p k h d", h=H)
                else:
                    a = qkv[:, :, C:2 * C]
                    w = qkv[:, query:query + 1, 0:C].to_broadcast([P, WS, C])
                    o = products[i % 2][:]
                then(pool, nc.gpsimd.tensor_tensor(o, a, w, ALU.mult), product, item + 1)

            def add_projection_bias(j, b, loads):
                pool.wait_ge(tile_in[b % 2], loads)
                then(pool, nc.gpsimd.tensor_tensor(xb[:, b % 2], xb[:, b % 2],
                                                   bproj_b[:].unsqueeze(1).to_broadcast([P, 2, C]), ALU.add),
                     xb_biased, j + 1)

            def norm2(j):
                rstd(mv2[:, 0, :, 1], ve2[:, 0], rs2[:, 0], 2, var2, rstd2, j + 1)

            def norm3(j):
                rstd(mv2[:, 1, :, 1], ve2[:, 1], rs2[:, 1], 2, var3, rstd3, j + 1)

            def bias_x1(j):
                pool.wait_ge(normed2, j + 1)
                then(pool, nc.gpsimd.tensor_tensor(x1[:], x1[:], bo_b[:].unsqueeze(1).to_broadcast([P, 2, C]),
                                                   ALU.add), x1_biased, j + 1)

            pool.wait_ge(weights, 16 * N_WEIGHTS)
            rstd1_of(0)
            pool.wait_ge(wd_done, 1 + WD_ITEMS)
            for i in range(WS):
                make_product(0, i, i, False)
            pool.wait_ge(probs_ready, 1)
            for i in range(WS):
                make_product(0, WS + i, i, True)
            add_projection_bias(0, 0, 48)
            norm2(0)

            def turn(g, more):
                n = g + 1
                for b in range(GB):
                    j = g * GB + b
                    last = not more and b == GB - 1
                    bias_x1(j)
                    if not last:
                        add_projection_bias(j + 1, b + 1, (g * 2 + (b + 1) // 2 + 1) * 48)
                    if more and b == 0:
                        rstd1_of(n)
                    if more and b == 1:
                        pool.wait_ge(wd_done, 1 + WD_ITEMS * (n + 1))
                        for i in range(WS):
                            make_product(n, i, i, False)
                    if more and b == 2:
                        pool.wait_ge(probs_ready, n + 1)
                        for i in range(5):
                            make_product(n, WS + i, i, True)
                    if more and b == 3:
                        for i in range(5, WS):
                            make_product(n, WS + i, i, True)
                    norm3(j)
                    if not last:
                        norm2(j + 1)

            with pool.Fori(0, NG - 1) as g:
                s.loop(g, 9)
                turn(g, True)
                s.turned()
            s.before += 9 * (NG - 1)
            s.turn = s.per_turn = 0
            turn(NG - 1, False)

        @block.scalar
        def _(act):
            copy = ACT.Copy
            act.wait_ge(identities, 3)
            then(act, nc.scalar.activation(rden[:, 0:1], ident[:, 0:1], copy), act_step, 1)
            nc.scalar.activation(rden[:, 1:2], ident[:, 0:1], copy).then_inc(a_done, A_BANKS)
            nc.scalar.activation(rden[:, 2:3], ident[:, 0:1], copy).then_inc(wa_done, 1)

            act.wait_ge(b1_turned, 1)
            nc.scalar.activation(b1T[:].rearrange("p e c -> p (e c)"), psA[:, 0, 0:P], copy).then_inc(b1_kept, 1)

            def window_turned(n, k):
                item = n * WA_ITEMS + k
                act.wait_ge(wa_full, item + 1)
                then(act, nc.scalar.activation(
                    xnT[:, :, 2 * k:2 * k + 2, :].rearrange("p k i w -> p i k w"),
                    psWA[:].rearrange("p (i k w) -> p i k w", i=2, k=KC), copy), wa_done, item + 2)

            def output_turned(n, k):
                item = n * WA_ITEMS + 4 + k
                act.wait_ge(wa_full, item + 1)
                ps = psWA[:].rearrange("p (i k w) -> p i k w", i=2, k=KC)
                for i in range(2):
                    dst = oT[:, :, :, 2 * k + i, :]
                    src = ps[:, i].rearrange("p k (b w) -> p k b w", b=GB)
                    if 2 * k < SHIFT:
                        last = nc.scalar.activation(dst, src, copy)
                    else:
                        nc.scalar.activation(dst[:, :, :, 1:BLK], src[:, :, :, 0:BLK - 1], copy)
                        last = nc.scalar.activation(dst[:, :, :, 0:1], src[:, :, :, BLK - 1:BLK], copy)
                then(act, last, wa_done, item + 2)

            def full(name, j, b):
                item, bank = A(name, j, b)
                act.wait_ge(a_full, item + 1)
                return psA[:, bank, :], item + A_BANKS + 1

            def start_context(j, b):
                ps, value = full("CTX'", j, b)
                nc.scalar.activation(ctxT[:, 0, 0:CTX], ps[:, 0:CTX], copy)
                then(act, nc.scalar.activation(ctxT[0:CTXD - P, 1, 0:CTX], ps[0:CTXD - P, P:P + CTX], copy), a_done, value)
                for half in range(2):
                    ps, value = full(f"K{half}'", j, b)
                    ps = ps.rearrange("p (u k) -> p u k", u=4)
                    us = slice(4 * half, 4 * half + 4)
                    for parity in range(2):
                        rows = slice(parity * D2, (parity + 1) * D2)
                        nc.scalar.activation(kT[rows, us, parity, :], ps[rows, :, 0:CTX], copy)
                        last = nc.scalar.activation(kTb[rows, us, parity, :], ps[rows, :, 0:CTX], copy)
                    then(act, last, a_done, value)

            def output2_turned(m, j, b):
                ps, value = full(f"O{m}", j, b)
                then(act, nc.scalar.activation(o2T[:, 2 * m:2 * m + 2, :].rearrange("p u n -> p (u n)"), ps, copy),
                     a_done, value)

            for k in range(4):
                window_turned(0, k)
            act.wait_ge(shifted, 1)
            then(act, nc.scalar.activation(probs[:], probs[:], ACT.Exp), exped, 1)
            for k in range(4):
                output_turned(0, k)
            start_context(-1, -1)

            def turn(g, more):
                n = g + 1
                for b in range(GB):
                    j = g * GB + b
                    ps, value = full("XN2", j, b)
                    then(act, nc.scalar.activation(xT[:].rearrange("p k n -> p (k n)"), ps, copy), a_done, value)
                    for q in range(4):
                        ps, value = full(f"Q{q}", j, b)
                        nc.scalar.activation(qTb[:, 2 * q:2 * q + 2, :].rearrange("p u n -> p (u n)"), ps, copy)
                        then(act, nc.scalar.activation(qT[:, 2 * q:2 * q + 2, :].rearrange("p u n -> p (u n)"), ps, copy),
                             a_done, value)
                    ps, value = full("NM", j, b)
                    then(act, nc.scalar.activation(nmT[0:H, :], ps[0:H, 0:P].bitcast(BF16), copy), a_done, value)
                    if more and b == 2:
                        act.wait_ge(shifted, n + 1)
                        then(act, nc.scalar.activation(probs[:], probs[:], ACT.Exp), exped, n + 1)
                    for u in range(CH):
                        ps, value = full(f"S{u}", j, b)
                        then(act, nc.scalar.activation(pT[0:CTX, u % 4, :], ps[0:CTX, :], ACT.Exp, scale=D2 ** -0.5),
                             a_done, value)
                        if u == 5:
                            output2_turned(0, j, b)
                    for k in range(4):
                        if more and b == 0:
                            window_turned(n, k)
                        if more and b == 3:
                            output_turned(n, k)
                        if k != 1:
                            output2_turned((1, None, 2, 3)[k], j, b)
                    if more or b < GB - 1:
                        start_context(j, b)
                        ps, value = full("XN3", j, b)
                    else:
                        item, bank = A("CTX'", j, b)
                        act.wait_ge(a_full, item + 1)
                        ps, value = psA[:, bank, :], item + A_BANKS + 1
                    then(act, nc.scalar.activation(xT[:].rearrange("p k n -> p (k n)"), ps, copy), a_done, value)

            with act.Fori(0, NG - 1) as g:
                turn(g, True)
            turn(NG - 1, False)

        @block.vector
        def _(dve):
            s = Steps(dve, vec_step)
            dve.wait_ge(identities, 3)
            nc.vector.memset(red[:, 0:1], 0.0).then_inc(d_done, D_BANKS)
            nc.vector.memset(red[:, 1:2], 0.0).then_inc(wd_done, 1)
            nc.vector.memset(red[:, 2:3], 0.0).then_inc(consumed, 2)
            dve.wait_ge(consumed, 2)
            dve.wait_ge(weights, 16 * N_WEIGHTS)

            def carry_waits():
                nc.vector.memset(idle[:], 0.0)

            def norm1_stats(n):
                dve.wait_ge(xw_in, (n + 1) * 16 * (GB + 2))
                for i in range(WS):
                    ins = nc.vector.bn_stats(st1[:, i, :], xw[:, i, :])
                s.done(ins)
                carry_waits()
                for i in range(WS):
                    ins = nc.vector.bn_aggr(mv1[:, i, :], st1[:, i, :])
                then(dve, ins, var1, n + 1)

            def norm1(n):
                dve.wait_ge(rstd1, n + 1)
                for i in range(WS):
                    ins = nc.vector.tensor_scalar(xw[:, i, :], xw[:, i, :], mv1[:, i, 0:1], rs1[:, i:i + 1],
                                                  ALU.subtract, ALU.mult)
                    if i % 2:
                        then(dve, ins, normed1, n * 4 + i // 2 + 1)

            def window_qkv(n, pair, part):
                item = n * WD_ITEMS + 3 * pair + part
                dve.wait_ge(wd_full, item + 1)
                if part < 2:
                    ins = nc.vector.tensor_tensor(qkv[:, 2 * pair + part, 0:2 * C], psWD[:], bqkv_b[:, 0:2 * C], ALU.add)
                else:
                    ins = nc.vector.tensor_tensor(qkv[:, 2 * pair:2 * pair + 2, 2 * C:3 * C],
                                                  psWD[:].rearrange("p (i c) -> p i c", i=2),
                                                  bqkv_b[:, 2 * C:3 * C].unsqueeze(1).to_broadcast([P, 2, C]), ALU.add)
                then(dve, ins, wd_done, item + 2)

            def sum_scores(n, i):
                item = n * TMP_ITEMS + i
                dve.wait_ge(product, item + 1)
                then(dve, nc.vector.tensor_reduce(probs[:, :, i * H:(i + 1) * H],
                                                  products[i % 2][:].rearrange("p k (h d) -> p k h d", h=H),
                                                  axis=X, op=ALU.add), consumed, item + 3)

            by_key = probs[:].rearrange("p k m -> p m k")

            def window_shift(n):
                s.done(nc.vector.scalar_tensor_tensor(probs[:], probs[:], D1 ** -0.5, relbias[:], ALU.mult, ALU.add))
                s.done(nc.vector.tensor_reduce(red[:], by_key, axis=X, op=ALU.max))
                then(dve, nc.vector.tensor_tensor(probs[:], probs[:],
                                                  red[:].unsqueeze(1).to_broadcast([P, WS, WS * H]), ALU.subtract), shifted, n + 1)

            def window_divide(n):
                dve.wait_ge(exped, n + 1)
                s.done(nc.vector.tensor_reduce(red[:], by_key, axis=X, op=ALU.add))
                s.done(nc.vector.reciprocal(red[:], red[:]))
                then(dve, nc.vector.tensor_tensor(probs[:], probs[:], red[:].unsqueeze(1).to_broadcast([P, WS, WS * H]),
                                                  ALU.mult), probs_ready, n + 1)

            def sum_values(n, i):
                item = n * TMP_ITEMS + WS + i
                t = products[i % 2]
                dve.wait_ge(product, item + 1)
                s.done(nc.vector.tensor_tensor(t[:, 0:4, :], t[:, 0:4, :], t[:, 4:8, :], ALU.add))
                s.done(nc.vector.tensor_tensor(t[:, 0:2, :], t[:, 0:2, :], t[:, 2:4, :], ALU.add))
                then(dve, nc.vector.tensor_tensor(qkv[:, i, 0:C], t[:, 0, :], t[:, 1, :], ALU.add), consumed, item + 3)

            def full(name, j, b):
                item, bank = Dd(name, j, b)
                dve.wait_ge(d_full, item + 1)
                return psD[:, bank, :], item + D_BANKS + 1

            def start_sequence(j, b):
                ps, value = full("PROJ'", j, b)
                dve.wait_ge(xb_biased, j + 2)
                then(dve, nc.vector.tensor_tensor(x1[:].rearrange("p k c -> p (k c)"), ps,
                                                  xb[:, (b + 1) % 2].rearrange("p k c -> p (k c)"), ALU.add), d_done, value)
                for half in range(2):
                    ins = nc.vector.bn_stats(st2[:, 0, half, :], x1[:, half, :])
                s.done(ins)
                carry_waits()
                for half in range(2):
                    ins = nc.vector.bn_aggr(mv2[:, 0, half, :], st2[:, 0, half, :])
                then(dve, ins, var2, j + 2)
                for half in range(2):
                    ps, value = full(f"V{half}'", j, b)
                    then(dve, nc.vector.tensor_copy(vo[:, 8 * half:8 * half + 8, 0:D2],
                                                    ps.rearrange("p (h d) -> p h d", h=8)), d_done, value)

            def norm2(j):
                dve.wait_ge(rstd2, j + 1)
                for half in range(2):
                    ins = nc.vector.tensor_scalar(xn[:, half, :], x1[:, half, :], mv2[:, 0, half, 0:1],
                                                  rs2[:, 0, half:half + 1], ALU.subtract, ALU.mult)
                then(dve, ins, normed2, j + 1)

            norm1_stats(0)
            norm1(0)
            for k in range(WD_ITEMS):
                window_qkv(0, k // 3, k % 3)
            for i in range(WS):
                sum_scores(0, i)
            window_shift(0)
            window_divide(0)
            for i in range(WS):
                sum_values(0, i)
            start_sequence(-1, -1)
            norm2(0)
            dve.wait_ge(zeros_in, 16 * -(-NT * ET // (CH * P)))

            def turn(g, more):
                n = g + 1
                for b in range(GB):
                    j = g * GB + b
                    for t in range(2):
                        for m in range(4):
                            ps, value = full(f"MAX{4 * t + m}", j, b)
                            then(dve, nc.vector.tensor_reduce(
                                nm[:, t, 4 * m:4 * m + 4], ps[:, 0:4 * CTX].rearrange("p (h k) -> p h k", h=4),
                                axis=X, op=ALU.max, negate=True), d_done, value)
                    if more and b == 0:
                        norm1_stats(n)
                    if more and b == 2:
                        window_shift(n)
                    for u in range(CH):
                        ps, value = full(f"PV{u}", j, b)
                        ps = ps.rearrange("p (h c) -> p h c", h=4)
                        if u >= 4 and u % 2 == 0:
                            dve.wait_ge(a_full, A(f"O{u // 2 - 2}", j, b)[0] + 1)
                        s.done(nc.vector.reciprocal(rden[:], ps[:, :, D2]))
                        then(dve, nc.vector.tensor_tensor(
                            o2[:, u // 2 % 2, u % 2, :].rearrange("p (h d) -> p h d", h=4),
                            ps[:, :, 0:D2], rden[:].unsqueeze(2).to_broadcast([P, 4, D2]), ALU.mult), d_done, value)
                        if more and b == 0 and u == 0:
                            norm1(n)
                        if more and b == 0 and u >= 4:
                            for part in range(3):
                                window_qkv(n, u - 4, part)
                        if more and b == 1:
                            sum_scores(n, u)
                        if more and b == 2 and u == 0:
                            window_divide(n)
                        if more and b == 2 and u >= 3:
                            sum_values(n, u - 3)
                        if more and b == 3 and u < 3:
                            sum_values(n, 5 + u)
                    ps, value = full("X2", j, b)
                    dve.wait_ge(x1_biased, j + 1)
                    mine = x2[:, bass.ds(j, 1), :, :].rearrange("p a k c -> p (a k) c")
                    then(dve, nc.vector.tensor_tensor(mine, ps.rearrange("p (k c) -> p k c", k=2), x1[:], ALU.add),
                         d_done, value)
                    carry_waits()
                    for half in range(2):
                        ins = nc.vector.bn_stats(st2[:, 1, half, :], mine[:, half, :])
                    s.done(ins)
                    carry_waits()
                    for half in range(2):
                        ins = nc.vector.bn_aggr(mv2[:, 1, half, :], st2[:, 1, half, :])
                    then(dve, ins, var3, j + 1)
                    last = not more and b == GB - 1
                    if not last:
                        start_sequence(j, b)
                    dve.wait_ge(rstd3, j + 1)
                    for half in range(2):
                        ins = nc.vector.tensor_scalar(xn3[:, half, :], mine[:, half, :], mv2[:, 1, half, 0:1],
                                                      rs2[:, 1, half:half + 1], ALU.subtract, ALU.mult)
                    then(dve, ins, normed3, j + 1)
                    kept = ln3[:, bass.ds(j, 1), :, :].rearrange("p a k m -> p (a k) m")
                    nc.vector.tensor_copy(kept[:, :, 0], mv2[:, 1, :, 0])
                    s.done(nc.vector.tensor_copy(kept[:, :, 1], rs2[:, 1, :]))
                    if not last:
                        norm2(j + 1)
                    item, bank = Dd("PROJ'" if last else "LOG", j, b)
                    dve.wait_ge(d_full, item + 1)
                    then(dve, nc.vector.tensor_tensor(
                        logits[:, bass.ds(j, 1), :, :].rearrange("p a k e -> p (a k) e"),
                        psD[:, bank, 0:2 * E].rearrange("p (k e) -> p k e", k=2),
                        rb_b[:].unsqueeze(1).to_broadcast([P, 2, E]), ALU.add), d_done, item + D_BANKS + 1)

            with dve.Fori(0, NG - 1) as g:
                s.loop(g, 65)
                turn(g, True)
                s.turned()
            s.before += 65 * (NG - 1)
            s.turn = s.per_turn = 0
            turn(NG - 1, False)

        @block.tensor
        def _(pe):
            mm = nc.tensor.matmul
            pe.wait_ge(identities, 3)
            pe.wait_ge(b1_in, 16)
            nc.tensor.transpose(psA[:, 0, 0:P], b1rows, ident[:]).then_inc(b1_turned, 1)
            pe.wait_ge(b1_kept, 1)
            pe.wait_ge(weights, 16 * N_WEIGHTS)

            def free(order, first, banks, done, ps, name, j, b):
                item, bank = at(order, first, banks, name, j, b)
                pe.wait_ge(done, item + 1)
                return ps[:, bank, :]

            def freeA(name, j, b):
                return free(A_ORDER, A_FIRST, A_BANKS, a_done, psA, name, j, b)

            def freeD(name, j, b):
                return free(D_ORDER, D_FIRST, D_BANKS, d_done, psD, name, j, b)

            def take_a(name, j, b):
                pe.wait_ge(a_done, A(name, j, b)[0] + A_BANKS + 1)

            def window_turn(n, k):
                pe.wait_ge(normed1, n * 4 + k + 1)
                pe.wait_ge(wa_done, n * WA_ITEMS + k + 1)
                for i in range(2):
                    for c in range(KC):
                        ins = nc.tensor.transpose(psWA[:, (i * KC + c) * P:(i * KC + c + 1) * P],
                                                  xw[:, 2 * k + i, c * P:(c + 1) * P], ident[:])
                ins.then_inc(wa_full, 1)

            def window_qkv(n, pair, part):
                if part == 0:
                    pe.wait_ge(wa_done, n * WA_ITEMS + pair + 2)
                pe.wait_ge(wd_done, n * WD_ITEMS + 3 * pair + part + 1)
                for i in ([2 * pair + part] if part < 2 else [2 * pair, 2 * pair + 1]):
                    cols = slice(0, 2 * C) if part < 2 else slice(2 * C, 3 * C)
                    dst = psWD[:] if part < 2 else psWD[:, (i % 2) * C:(i % 2 + 1) * C]
                    for c in range(KC):
                        ins = mm(dst, xnT[:, c, i, :], wqkv[:, c, cols], start=c == 0, stop=c == KC - 1)
                ins.then_inc(wd_full, 1)

            def output_turn(n, k):
                pe.wait_ge(consumed, 2 + n * TMP_ITEMS + WS + 2 * k + 2)
                pe.wait_ge(wa_done, n * WA_ITEMS + 4 + k + 1)
                for i in range(2):
                    for c in range(KC):
                        ins = nc.tensor.transpose(psWA[:, (i * KC + c) * P:(i * KC + c + 1) * P],
                                                  qkv[:, 2 * k + i, c * P:(c + 1) * P], ident[:])
                ins.then_inc(wa_full, 1)

            def start_sequence(j, b, loads, group):
                q = (b + 1) % GB
                pe.wait_ge(wa_done, (group + 1) * WA_ITEMS + 1)
                ps = freeD("PROJ'", j, b)
                for half in range(2):
                    for c in range(KC):
                        ins = mm(ps[:, half * C:(half + 1) * C],
                                 oT[:, c, q, 4 * half:4 * half + 4, :].rearrange("p i w -> p (i w)"), wproj[:, c, :],
                                 start=c == 0, stop=c == KC - 1)
                ins.then_inc(d_full, 1)
                ps = freeA("CTX'", j, b)
                pe.wait_ge(tile_in[(b + 1) % 2], loads)
                nc.tensor.transpose(ps[:, 0:CTX], ctx[0:CTX, (b + 1) % 2, 0:P], ident[0:CTX, 0:CTX])
                nc.tensor.transpose(ps[0:CTXD - P, P:P + CTX], ctx[0:CTX, (b + 1) % 2, P:CTXD],
                                    ident[0:CTX, 0:CTX]).then_inc(a_full, 1)
                take_a("CTX'", j, b)
                for half in range(2):
                    ps = freeA(f"K{half}'", j, b)
                    for u in range(4):
                        for c in range(KC):
                            ins = mm(ps[:, u * P:(u + 1) * P], wk[:, c, (4 * half + u) * P:(4 * half + u + 1) * P],
                                     ctxT[:, c, :], start=c == 0, stop=c == KC - 1)
                    ins.then_inc(a_full, 1)
                for half in range(2):
                    ps = freeD(f"V{half}'", j, b)
                    for c in range(KC):
                        ins = mm(ps, ctxT[:, c, :], wv[:, c, half * 512:(half + 1) * 512], start=c == 0, stop=c == KC - 1)
                    ins.then_inc(d_full, 1)

            for k in range(4):
                window_turn(0, k)
            for k in range(WD_ITEMS):
                window_qkv(0, k // 3, k % 3)
            for k in range(4):
                output_turn(0, k)
            start_sequence(-1, -1, 48, 0)

            def turn(g, more):
                n = g + 1
                for b in range(GB):
                    j = g * GB + b
                    pe.wait_ge(normed2, j + 1)
                    ps = freeA("XN2", j, b)
                    for c in range(KC):
                        for half in range(2):
                            ins = nc.tensor.transpose(ps[:, (c * 2 + half) * P:(c * 2 + half + 1) * P],
                                                      xn[:, half, c * P:(c + 1) * P], ident[:])
                    ins.then_inc(a_full, 1)
                    take_a("XN2", j, b)
                    for q in range(4):
                        ps = freeA(f"Q{q}", j, b)
                        for u in range(2):
                            for c in range(KC):
                                ins = mm(ps[:, u * N:(u + 1) * N], wq[:, c, (2 * q + u) * P:(2 * q + u + 1) * P],
                                         xT[:, c, :], start=c == 0, stop=c == KC - 1)
                        ins.then_inc(a_full, 1)
                    for t in range(2):
                        for m in range(4):
                            if t == 0:
                                take_a(f"Q{m}", j, b)
                            ps = freeD(f"MAX{4 * t + m}", j, b)
                            for i in range(2):
                                u = 2 * m + i
                                ins = mm(ps[:, 2 * i * CTX:2 * (i + 1) * CTX], qTb[:, u, t * P:(t + 1) * P],
                                         kTb[:, u].rearrange("p m k -> p (m k)"), start=True, stop=True)
                            ins.then_inc(d_full, 1)
                    ps = freeA("NM", j, b)
                    for t in range(2):
                        pe.wait_ge(d_done, Dd(f"MAX{4 * t + 3}", j, b)[0] + D_BANKS + 1)
                        ins = nc.tensor.transpose(ps[0:H, t * 64:(t + 1) * 64].bitcast(BF16), nm[:, t, :], identb[:])
                    ins.then_inc(a_full, 1)
                    take_a("NM", j, b)

                    def scores(u):
                        ps = freeA(f"S{u}", j, b)
                        for m in range(2):
                            dst = ps[0:CTX, m * N:(m + 1) * N]
                            mm(dst, kT[:, u, m, :], qT[:, u, :], start=True, stop=False)
                            ins = mm(dst, head_row[:, 2 * u + m, :], nmT[:], start=False, stop=True)
                        ins.then_inc(a_full, 1)

                    def values(v):
                        w, t = v // 2, v % 2
                        take_a(f"S{2 * w + 1}", j, b)
                        ps = freeD(f"PV{v}", j, b)
                        for m in range(4):
                            ins = mm(ps[:, m * P:(m + 1) * P],
                                     pT[:, (2 * w + m // 2) % 4, (m % 2) * N + t * P:(m % 2) * N + (t + 1) * P],
                                     vo[:, 4 * w + m, :], start=True, stop=True)
                        ins.then_inc(d_full, 1)

                    def turn_output2(m):
                        pe.wait_ge(d_done, Dd(f"PV{2 * m + 1}", j, b)[0] + D_BANKS + 1)
                        ps = freeA(f"O{m}", j, b)
                        for u in range(2):
                            for t in range(2):
                                ins = nc.tensor.transpose(ps[:, (2 * u + t) * P:(2 * u + t + 1) * P],
                                                          o2[:, m % 2, t, u * P:(u + 1) * P], ident[:])
                        ins.then_inc(a_full, 1)

                    for u in range(4):
                        scores(u)
                    for v in range(8):
                        values(v)
                        if v in (1, 3):
                            scores(v + 3)
                            scores(v + 4)
                        if more and b == 0 and v >= 4:
                            window_turn(n, v - 4)
                            for part in range(3):
                                window_qkv(n, v - 4, part)
                        if more and b == 3 and v >= 4:
                            output_turn(n, v - 4)
                        if v in (2, 4, 6):
                            turn_output2(v // 2 - 1)
                    turn_output2(3)
                    ps = freeD("X2", j, b)
                    pe.wait_ge(a_done, A("O3", j, b)[0] + A_BANKS + 1)
                    for half in range(2):
                        for u in range(CH):
                            ins = mm(ps[:, half * C:(half + 1) * C], o2T[:, u, half * P:(half + 1) * P], wo[:, u, :],
                                     start=u == 0, stop=u == CH - 1)
                    ins.then_inc(d_full, 1)
                    last = not more and b == GB - 1
                    if not last:
                        start_sequence(j, b, (g * 2 + (b + 1) // 2 + 1) * 48, g if b < GB - 1 else g + 1)
                    pe.wait_ge(normed3, j + 1)
                    ps = freeA("CTX'" if last else "XN3", j, b)
                    for c in range(KC):
                        for half in range(2):
                            ins = nc.tensor.transpose(ps[:, (c * 2 + half) * P:(c * 2 + half + 1) * P],
                                                      xn3[:, half, c * P:(c + 1) * P], ident[:])
                    ins.then_inc(a_full, 1)
                    take_a("CTX'" if last else "XN3", j, b)
                    ps = freeD("PROJ'" if last else "LOG", j, b)
                    for half in range(2):
                        for c in range(KC):
                            ins = mm(ps[:, half * E:(half + 1) * E], xT[:, c, half * P:(half + 1) * P], rw[:, c, :],
                                     start=c == 0, stop=c == KC - 1)
                    ins.then_inc(d_full, 1)

            with pe.Fori(0, NG - 1) as g:
                turn(g, True)
            turn(NG - 1, False)


def experts(nc, outer, v):
    ident, x2, logits, ln3, b1T = (v[k] for k in ("ident", "x2", "logits", "ln3", "b1T"))
    sorted_x, sorted_y, out, half_of = v["sorted_x"], v["sorted_y"], v["out"], v["half_of"]
    SLOTS = 8
    HB = 4
    with ExitStack() as st:
        def sb(name, shape, dt=F32):
            return st.enter_context(nc.sbuf_tensor(name, shape, dt))

        def sem(name):
            return st.enter_context(nc.semaphore(name))

        psH = st.enter_context(nc.psum_tensor("psH", [P, HB, 2, ET], F32))
        psY = st.enter_context(nc.psum_tensor("psY", [P, 2, 512], F32))
        psT = st.enter_context(nc.psum_tensor("psT", [P, KC, ET], F32))
        psR = st.enter_context(nc.psum_tensor("psR", [P, 2, TT, E], F32))

        upper = sb("upper", [P, P], BF16)
        ones = sb("ones", [P, P], BF16)
        e_less_8 = sb("e_less_8", [P, E])
        k_tiles = sb("k_tiles", [P, B * N // ET])
        tile_no = sb("tile_no", [P, NT])
        best = sb("best", [P, TT])
        cand = sb("cand", [P, TT, E])
        first = sb("first", [P, TT])
        onehot = sb("onehot", [P, TT, E])
        onehotb = sb("onehotb", [P, TT, E], BF16)
        run = sb("run", [P, 2, TT, E])
        total = sb("total", [P, TT, E])
        where = sb("where", [P, TT, E])
        cmp = sb("cmp", [P, E, B * N // ET])
        ntiles = sb("ntiles", [P, E])
        ends = sb("ends", [P, 2, E])
        base = sb("base", [P, E])
        pos = sb("pos", [P, TT])
        posi = sb("posi", [P, TT], U32)
        passed = sb("passed", [P, NT, E])
        tile_e = sb("tile_e", [P, NT])
        tile_ei = sb("tile_ei", [P, NT], I32)
        b1big = sb("b1big", [P, NT, 2 * HC, E])
        b1s = sb("b1s", [P, NT, 2 * HC])
        slots = sb("slots", [P, SLOTS, C])
        w1s = [sb(f"w1s{i}", [P, KC, 2 * HID]) for i in range(2)]
        w2s = [sb(f"w2s{i}", [P, HC, C]) for i in range(2)]
        b2s = sb("b2s", [P, 2, C])
        xs = sb("xs", [P, 2, 2, C])
        xsT = sb("xsT", [P, KC, ET])
        sig = sb("sig", [P, 2, ET])
        gated = sb("gated", [P, 2, ET])
        ys = sb("ys", [P, 2, 2, C])

        pool_step, vec_step = sem("pool_step2"), sem("vec_step2")
        onehot_ready, counted, located = sem("onehot_ready"), sem("counted"), sem("located")
        normed = sem("normed")
        scattered = [sem(f"scattered{i}") for i in range(SLOTS)]
        gathered = [sem(f"gathered{i}") for i in range(SLOTS)]
        out_stored = [sem(f"out_stored{i}") for i in range(SLOTS)]
        summed = sem("summed")
        w_in = [sem("w_in0"), sem("w_in1")]
        xs_in = [sem("xs_in0"), sem("xs_in1")]
        y_stored = [sem("y_stored0"), sem("y_stored1")]
        t_full, t_done, h_full, sig_done, h_done = (sem(k) for k in ("t_full", "t_done", "h_full", "sig_done", "h_done"))
        y_full, y_done = sem("y_full"), sem("y_done")
        block = st.enter_context(nc.Block())
        PAIRS = (NT - 3) // 2
        ROUTE_STEPS = 40

        def tiles(eng, tile):
            with eng.Fori(0, PAIRS) as k:
                for par in range(2):
                    tile(k * 2 + par, par, k)
            for t in range(2 * PAIRS, NT):
                tile(t, t % 2, t // 2)

        @block.sync
        def _(sp):
            def load_weights(t, par):
                e = sp.value_load(tile_ei[0:1, bass.ds(t, 1)], min_val=0, max_val=E - 1)
                sp.dma_start(w1s[par][:], v["w1"][bass.ds(e, 1)].rearrange("a (k p) n -> p (a k) n", p=P))\
                    .then_inc(w_in[par], 16)
                sp.dma_start(w2s[par][:], v["w2"][bass.ds(e, 1)].rearrange("a (k p) n -> p (a k) n", p=P))\
                    .then_inc(w_in[par], 16)
                return e

            def load_bias(e, par):
                sp.dma_start(b2s[:, par, :], v["b2"][bass.ds(e, 1), :].rearrange("a c -> (a c)").partition_broadcast(P))\
                    .then_inc(w_in[par], 16)

            def rows(ap, t):
                return ap[bass.ds(t * ET, ET), :].rearrange("(k p) c -> p k c", p=P)

            def load_tokens(t, par):
                sp.dma_start(xs[:, par], rows(sorted_x, t)).then_inc(xs_in[par], 16)

            sp.wait_ge(located, 1)
            for t in range(2):
                load_bias(load_weights(t, t), t)
            for i in range(SLOTS):
                sp.wait_ge(scattered[i], 16 * (TT // SLOTS))
            for t in range(2):
                load_tokens(t, t)

            def tile(t, par, turn):
                more = not isinstance(t, int) or t + 2 < NT
                sp.wait_ge(y_full, t + 1)
                if more:
                    e = load_weights(t + 2, par)
                    load_tokens(t + 2, par)
                sp.wait_ge(y_done, t + 2)
                if more:
                    load_bias(e, par)
                sp.dma_start(rows(sorted_y, t), ys[:, par]).then_inc(y_stored[par], 16)

            tiles(sp, tile)
            for t in range(TT):
                sp.wait_ge(summed, t + 1)
                sp.dma_start(half_of(out, t // 2, t % 2), slots[:, t % SLOTS, :]).then_inc(out_stored[t % SLOTS], 16)
            for i in range(SLOTS):
                sp.wait_ge(out_stored[i], 16 * (TT // SLOTS))

        @block.gpsimd
        def _(pool):
            s = Steps(pool, pool_step)
            s.done(nc.gpsimd.memset(upper[:], 1.0))
            s.done(nc.gpsimd.affine_select(out=upper[:], in_=upper[:], compare_op=ALU.is_gt, fill=0.0, base=0,
                                           pattern=[[1, P]], channel_multiplier=-1))
            s.done(nc.gpsimd.memset(ones[:], 1.0))
            for dst, step, first_value in ((e_less_8, 1, -E), (k_tiles, ET, 0), (tile_no, 1, 0)):
                s.done(nc.gpsimd.iota(dst[:], pattern=[[step, dst.shape[1]]], base=first_value, channel_multiplier=0,
                                      allow_small_or_imprecise_dtypes=True))
            for t in range(TT):
                pool.wait_ge(normed, t + 1)
                nc.gpsimd.indirect_dma_start(
                    out=sorted_x[:, :], out_offset=bass.IndirectOffsetOnAxis(ap=posi[:, t:t + 1], axis=0),
                    in_=slots[:, t % SLOTS, :], in_offset=None).then_inc(scattered[t % SLOTS], 16)
            pool.wait_ge(y_stored[0], 16 * ((NT + 1) // 2 + 1))
            pool.wait_ge(y_stored[1], 16 * (NT // 2 + 1))
            for t in range(TT):
                if t >= SLOTS:
                    pool.wait_ge(out_stored[t % SLOTS], 16 * (t // SLOTS))
                nc.gpsimd.indirect_dma_start(
                    out=slots[:, t % SLOTS, :], out_offset=None, in_=sorted_y[:, :],
                    in_offset=bass.IndirectOffsetOnAxis(ap=posi[:, t:t + 1], axis=0)).then_inc(gathered[t % SLOTS], 16)

        @block.vector
        def _(dve):
            s = Steps(dve, vec_step)
            tt, reduce = nc.vector.tensor_tensor, nc.vector.tensor_reduce
            dve.wait_ge(pool_step, 6)
            lg = logits[:].rearrange("p b k e -> p (b k) e")

            def over_tiles(ap):
                return ap.unsqueeze(1).to_broadcast([P, TT, E])

            def over_experts(ap, n=TT):
                return ap.unsqueeze(2).to_broadcast([P, n, E])

            s.done(reduce(best[:], lg, axis=X, op=ALU.max))
            s.done(tt(cand[:], lg, over_experts(best[:]), ALU.is_equal))
            s.done(tt(cand[:], cand[:], over_tiles(e_less_8[:]), ALU.mult))
            s.done(reduce(first[:], cand[:], axis=X, op=ALU.min))
            s.done(tt(onehot[:], over_tiles(e_less_8[:]), over_experts(first[:]), ALU.is_equal))
            then(dve, nc.vector.tensor_copy(onehotb[:], onehot[:]), onehot_ready, 1)
            dve.wait_ge(counted, 1)
            s.done(nc.vector.tensor_copy(total[:], psR[:, 1]))
            s.done(nc.vector.tensor_copy(run[:, 0], psR[:, 1]))
            cur = 0
            for step in (1, 2, 4, 8, 16):
                s.done(nc.vector.tensor_copy(run[:, 1 - cur, 0:step, :], run[:, cur, 0:step, :]))
                s.done(tt(run[:, 1 - cur, step:TT, :], run[:, cur, step:TT, :], run[:, cur, 0:TT - step, :], ALU.add))
                cur = 1 - cur
            nk = B * N // ET
            s.done(tt(cmp[:], run[:, cur, TT - 1, :].unsqueeze(2).to_broadcast([P, E, nk]),
                      k_tiles[:].unsqueeze(1).to_broadcast([P, E, nk]), ALU.is_gt))
            s.done(reduce(ntiles[:], cmp[:], axis=X, op=ALU.add))
            s.done(nc.vector.tensor_copy(ends[:, 0, :], ntiles[:]))
            c = 0
            for step in (1, 2, 4):
                s.done(nc.vector.tensor_copy(ends[:, 1 - c, 0:step], ends[:, c, 0:step]))
                s.done(tt(ends[:, 1 - c, step:E], ends[:, c, step:E], ends[:, c, 0:E - step], ALU.add))
                c = 1 - c
            s.done(tt(passed[:], over_experts(tile_no[:], NT), ends[:, c, :].unsqueeze(1).to_broadcast([P, NT, E]),
                      ALU.is_ge))
            s.done(reduce(tile_e[:], passed[:], axis=X, op=ALU.add))
            s.done(nc.vector.tensor_scalar(tile_e[:], tile_e[:], float(E - 1), None, ALU.min))
            then(dve, nc.vector.tensor_copy(tile_ei[:], tile_e[:]), located, 1)
            s.done(tt(base[:], ends[:, c, :], ntiles[:], ALU.subtract))
            s.done(nc.vector.tensor_scalar(base[:], base[:], float(ET), None, ALU.mult))
            s.done(tt(where[:], run[:, cur], total[:], ALU.subtract))
            s.done(tt(where[:], where[:], psR[:, 0], ALU.add))
            s.done(tt(where[:], where[:], over_tiles(base[:]), ALU.add))
            s.done(tt(where[:], where[:], onehot[:], ALU.mult))
            s.done(reduce(pos[:], where[:], axis=X, op=ALU.add))
            s.done(nc.vector.tensor_copy(posi[:], pos[:]))
            for t in range(TT):
                if t >= SLOTS:
                    dve.wait_ge(scattered[t % SLOTS], 16 * (t // SLOTS))
                ln = ln3[:, t // 2, t % 2, :]
                nc.vector.tensor_scalar(slots[:, t % SLOTS, :], x2[:, t // 2, t % 2, :], ln[:, 0:1], ln[:, 1:2],
                                        ALU.subtract, ALU.mult).then_inc(normed, 1)
            s.done(nc.vector.tensor_scalar(tile_e[:], tile_e[:], -float(E), None, ALU.add))
            s.done(tt(passed[:], over_experts(tile_e[:], NT), e_less_8[:].unsqueeze(1).to_broadcast([P, NT, E]),
                      ALU.is_equal))
            s.done(tt(b1big[:], passed[:].unsqueeze(2).to_broadcast([P, NT, 2 * HC, E]),
                      b1T[:].rearrange("p e c -> p c e").unsqueeze(1).to_broadcast([P, NT, 2 * HC, E]), ALU.mult))
            then(dve, reduce(b1s[:], b1big[:], axis=X, op=ALU.add), h_done, 1)
            nc.vector.memset(cmp[:, 0, 0:1], 0.0).then_inc(y_done, 1)
            nc.vector.memset(cmp[:, 0, 1:2], 0.0).then_inc(h_done, HB - 1)
            for i in range(2):
                nc.vector.memset(cmp[:, 0, 2 + i:3 + i], 0.0).then_inc(y_stored[i], 16)

            def tile(t, par, turn):
                for c in range(HC):
                    item = t * HC + c
                    dve.wait_ge(sig_done, item + 1)
                    then(dve, nc.vector.scalar_tensor_tensor(
                        gated[:, c % 2, :], psH[:, c % HB, 0, :],
                        b1s[:, bass.ds(t, 1), c], sig[:, c % 2, :], ALU.add, ALU.mult), h_done, item + HB + 1)
                dve.wait_ge(y_full, t + 1)
                dve.wait_ge(w_in[par], (turn + 1) * 48)
                dve.wait_ge(y_stored[par], turn * 16 + 16)
                then(dve, tt(ys[:, par], psY[:, :, 0:C], b2s[:, par:par + 1, :].to_broadcast([P, 2, C]), ALU.add),
                     y_done, t + 2)

            tiles(dve, tile)
            for t in range(TT):
                dve.wait_ge(gathered[t % SLOTS], 16 * (t // SLOTS + 1))
                tt(slots[:, t % SLOTS, :], slots[:, t % SLOTS, :], x2[:, t // 2, t % 2, :], ALU.add).then_inc(summed, 1)

        @block.scalar
        def _(act):
            def tile(t, par, turn):
                act.wait_ge(t_full, t + 1)
                then(act, nc.scalar.activation(xsT[:], psT[:], ACT.Copy), t_done, t + 1)
                for c in range(HC):
                    item = t * HC + c
                    act.wait_ge(h_full, item + 1)
                    act.wait_ge(h_done, item + HB - 1)
                    then(act, nc.scalar.activation(sig[:, c % 2, :], psH[:, c % HB, 1, :], ACT.Sigmoid,
                                                   bias=b1s[:, bass.ds(t, 1), HC + c]), sig_done, item + 1)

            act.wait_ge(h_done, HB)
            tiles(act, tile)

        @block.tensor
        def _(pe):
            mm = nc.tensor.matmul
            pe.wait_ge(onehot_ready, 1)
            oh = onehotb[:].rearrange("p t e -> p (t e)")
            mm(psR[:, 0].rearrange("p t e -> p (t e)"), upper[:], oh, start=True, stop=True)
            mm(psR[:, 1].rearrange("p t e -> p (t e)"), ones[:], oh, start=True, stop=True).then_inc(counted, 1)

            def turn_tokens(t, par, turn):
                pe.wait_ge(xs_in[par], (turn + 1) * 16)
                for c in range(KC):
                    for half in range(2):
                        ins = nc.tensor.transpose(psT[:, c, half * P:(half + 1) * P],
                                                  xs[:, par, half, c * P:(c + 1) * P], ident[:])
                ins.then_inc(t_full, 1)

            def down(t, par, c):
                pe.wait_ge(h_done, t * HC + c + HB + 1)
                if c == 0:
                    pe.wait_ge(y_done, t + 1)
                for half in range(2):
                    ins = mm(psY[:, half, 0:C], gated[:, c % 2, half * P:(half + 1) * P], w2s[par][:, c, :],
                             start=c == 0, stop=c == HC - 1)
                if c == HC - 1:
                    ins.then_inc(y_full, 1)

            def tile(t, par, turn):
                pe.wait_ge(w_in[par], (turn + 1) * 48)
                pe.wait_ge(t_done, t + 1)
                for c in range(HC):
                    pe.wait_ge(h_done, t * HC + c + 1)
                    for part in range(2):
                        w = part * HID + c * P
                        for k in range(KC):
                            ins = mm(psH[:, c % HB, part, :], w1s[par][:, k, w:w + P], xsT[:, k, :],
                                     start=k == 0, stop=k == KC - 1)
                    ins.then_inc(h_full, 1)
                    if c >= 1:
                        if c == HC - 1 and not (isinstance(t, int) and t == NT - 1):
                            turn_tokens(t + 1, 1 - par, turn + par)
                        down(t, par, c - 1)
                down(t, par, HC - 1)

            turn_tokens(0, 0, 0)
            tiles(pe, tile)


_NAMES = ["x", "ctx_768", "L0_attn_w_qkv", "L0_attn_b_qkv", "L0_attn_w_proj", "L0_attn_b_proj", "L0_attn_bias_table",
          "L0_xattn_Wq", "L0_xattn_Wk", "L0_xattn_Wv", "L0_xattn_Wo", "L0_xattn_bo", "L0_ffn_router_w",
          "L0_ffn_router_b", "L0_ffn_w1", "L0_ffn_b1", "L0_ffn_w2", "L0_ffn_b2"]


def kernel(**inputs):
    import numpy as np
    import concourse.bacc as bacc
    from concourse.bass_utils import run_bass_kernel_spmd

    nc = bacc.Bacc("TRN2", target_bir_lowering=False, num_devices=1)
    arrays = {f"in_{k}": np.ascontiguousarray(inputs[k]) for k in _NAMES}
    args = [nc.dram_tensor(k, a.shape, mybir.dt.from_np(a.dtype), kind="ExternalInput").ap() for k, a in arrays.items()]
    out = nc.dram_tensor("out", (B, N, C), F32, kind="ExternalOutput").ap()
    decoder_layer(nc, *args, out)
    return run_bass_kernel_spmd(nc, [arrays], core_ids=[0]).results[0]["out"]
```

```python
from contextlib import ExitStack

import concourse.bass as bass
from concourse import mybir

F32 = mybir.dt.float32
BF16 = mybir.dt.bfloat16
I32 = mybir.dt.int32
U32 = mybir.dt.uint32
ALU = mybir.AluOpType
ACT = mybir.ActivationFunctionType
X = mybir.AxisListType.X

P = 128
B, N, C = 16, 256, 256
KC = C // P
WS, SHIFT = 8, 4
H, D1 = 16, 16
D2 = 64
INNER = H * D2
CH = INNER // P
CTX, CTXD = 77, 192
GB = 4
NG = B // GB
BLK = N // WS
E, HID = 8, 1024
HC = HID // P
ET = 256
NT = B * N // ET + E - 1
TT = B * N // P
EPS = 1e-5

A_ORDER = (["XN2"] + [f"Q{n}" for n in range(4)] + ["NM", "S0", "S1", "S2", "S3", "S4", "S5", "O0", "S6", "S7"]
           + ["O1", "O2", "CTX'", "O3", "K0'", "K1'", "XN3"])
D_ORDER = ["V1"] + [f"MAX{n}" for n in range(8)] + [f"PV{v}" for v in range(8)] + ["X2", "PROJ'", "V0'", "LOG"]
A_FIRST = ["CTX'", "K0'", "K1'"]
D_FIRST = ["PROJ'", "V0'"]
A_BANKS, D_BANKS = 4, 2
assert GB * len(A_ORDER) % A_BANKS == 0 and GB * len(D_ORDER) % D_BANKS == 0
WA_ITEMS, WD_ITEMS = 8, 12
TMP_ITEMS = 2 * WS
QKV_PARTS = {v: [(k // 3, k % 3) for k in ks] for v, ks in
             {2: [0], 3: [1, 2], 4: [3, 4], 5: [5, 6], 6: [7, 8], 7: [9, 10, 11]}.items()}
POOL_FIRST = (1, 4, 7)


def at(order, first, banks, name, j, b):
    if isinstance(j, int) and j < 0:
        return first.index(name), first.index(name) % banks
    k = len(first) + order.index(name)
    return j * len(order) + k, (b * len(order) + k) % banks


class Steps:

    def __init__(self, eng, sem):
        self.eng, self.sem, self.before, self.per_turn, self.turn, self.n = eng, sem, 0, 0, 0, 0

    def loop(self, turn, per_turn):
        self.before, self.n, self.turn, self.per_turn = self.before + self.n, 0, turn, per_turn

    def turned(self):
        assert self.n == self.per_turn, f"{self.sem}: {self.n} steps in a turn"
        self.n = 0

    def done(self, ins):
        ins.then_inc(self.sem, 1)
        self.n += 1
        self.eng.wait_ge(self.sem, self.turn * self.per_turn + (self.before + self.n))


def then(eng, ins, sem, value):
    ins.then_inc(sem, 1)
    eng.wait_ge(sem, value)


def decoder_layer(nc, x, ctx_768, w_qkv, b_qkv, w_proj, b_proj, bias_table, Wq, Wk, Wv, Wo, bo,
                  router_w, router_b, w1, b1, w2, b2, out):
    sorted_x = nc.dram_tensor("sorted_x", (NT * ET, C), F32, kind="Internal").ap()
    sorted_y = nc.dram_tensor("sorted_y", (NT * ET, C), F32, kind="Internal").ap()
    x_flat = x.rearrange("b n c -> b (n c)")

    def half_of(ap, j, half):
        rows = ap[bass.ds(j, 1)].rearrange("a (k r) c -> r (a k) c", r=WS)
        return rows[SHIFT:WS] if half == 0 else rows[0:SHIFT]

    with ExitStack() as whole:
        def keep(name, shape, dt=F32):
            return whole.enter_context(nc.sbuf_tensor(name, shape, dt))

        ident = keep("ident", [P, P])
        identb = keep("identb", [P, P], BF16)
        x2 = keep("x2", [P, B, 2, C])
        logits = keep("logits", [P, B, 2, E])
        ln3 = keep("ln3", [P, B, 2, 2])
        b1T = keep("b1T", [P, E, 2 * HC])

        trunk(nc, whole, locals())
        experts(nc, whole, locals())


def trunk(nc, outer, v):
    x, x_flat, ctx_768, half_of = v["x"], v["x_flat"], v["ctx_768"], v["half_of"]
    ident, identb, x2, logits, ln3, b1T = (v[k] for k in ("ident", "identb", "x2", "logits", "ln3", "b1T"))
    sorted_x = v["sorted_x"]
    with ExitStack() as st:
        def sb(name, shape, dt=F32):
            return st.enter_context(nc.sbuf_tensor(name, shape, dt))

        def sem(name):
            return st.enter_context(nc.semaphore(name))

        psA = st.enter_context(nc.psum_tensor("psA", [P, A_BANKS, 512], F32))
        psD = st.enter_context(nc.psum_tensor("psD", [P, D_BANKS, 512], F32))
        psW = st.enter_context(nc.psum_tensor("psW", [P, 2, 512], F32))

        wqkv = sb("wqkv", [P, KC, 3 * C])
        wproj = sb("wproj", [P, KC, C])
        wq = sb("wq", [P, KC, INNER])
        wk = sb("wk", [P, KC, INNER])
        wv = sb("wv", [P, KC, INNER])
        wo = sb("wo", [P, CH, C])
        rw = sb("rw", [P, KC, E])
        bqkv_b = sb("bqkv_b", [P, 3 * C])
        bproj_b = sb("bproj_b", [P, C])
        bo_b = sb("bo_b", [P, C])
        rb_b = sb("rb_b", [P, E])
        relbias = sb("relbias", [P, WS, WS * H])
        head_row = sb("head_row", [P, H, CTX], BF16)
        half_exp = sb("half_exp", [P, WS])
        eps = sb("eps", [P, WS])

        xw = sb("xw", [P, WS, C])
        tmp1 = sb("tmp1", [P, WS, C])
        products = [xw, tmp1]
        idle = sb("idle", [P, 1])
        st1 = sb("st1", [P, WS, 6])
        mv1 = sb("mv1", [P, WS, 2])
        ve1 = sb("ve1", [P, WS])
        rs1 = sb("rs1", [P, WS])
        xnT = sb("xnT", [P, KC, WS, P])
        qkv = sb("qkv", [P, WS, 3 * C])
        probs = sb("probs", [P, WS, WS * H])
        red = sb("red", [P, WS * H])
        oT = sb("oT", [P, KC, GB, WS, BLK])

        xb = sb("xb", [P, 2, 2, C])
        ctx = sb("ctx", [P, 2, CTXD])
        x1 = sb("x1", [P, 2, C])
        xn = sb("xn", [P, 2, C])
        st2 = sb("st2", [P, 2, 2, 6])
        mv2 = sb("mv2", [P, 2, 2, 2])
        ve2 = sb("ve2", [P, 2, 2])
        rs2 = sb("rs2", [P, 2, 2])
        xT = sb("xT", [P, KC, 2 * P])
        ctxT = sb("ctxT", [P, KC, P])
        qT = sb("qT", [P, CH, 2 * P])
        qTb = sb("qTb", [P, CH, 2 * P], BF16)
        kT = sb("kT", [P, CH, 2, CTX])
        kTb = sb("kTb", [P, CH, 2, CTX], BF16)
        vo = sb("vo", [P, H, 2 * D2])
        nm = sb("nm", [P, 2, H], BF16)
        nmT = sb("nmT", [P, 2 * P], BF16)
        pT = sb("pT", [P, 4, 2 * N])
        rden = sb("rden", [P, 4])
        o2 = sb("o2", [P, 2, 2, 4 * D2])
        xn3 = o2[:, 0]
        b1rows = o2[:, 0, 0, 0:P]
        o2T = sb("o2T", [P, CH, N])

        weights = sem("weights")
        zeros_in = sem("zeros_in")
        pool_step, act_step, vec_step = sem("pool_step"), sem("act_step"), sem("vec_step")
        identities = sem("identities")
        xw_in = sem("xw_in")
        tile_in = [sem("tile_in0"), sem("tile_in1")]
        a_full, a_done = sem("a_full"), sem("a_done")
        d_full, d_done = sem("d_full"), sem("d_done")
        wa_full, wa_done = sem("wa_full"), sem("wa_done")
        wd_full, wd_done = sem("wd_full"), sem("wd_done")
        var1, rstd1, normed1 = sem("var1"), sem("rstd1"), sem("normed1")
        product, consumed = sem("product"), sem("consumed")
        shifted, exped, probs_ready = sem("shifted"), sem("exped"), sem("probs_ready")
        xb_biased, x1_biased = sem("xb_biased"), sem("x1_biased")
        var2, rstd2, normed2 = sem("var2"), sem("rstd2"), sem("normed2")
        var3, rstd3, normed3 = sem("var3"), sem("rstd3"), sem("normed3")
        b1_in, b1_turned, b1_kept = sem("b1_in"), sem("b1_turned"), sem("b1_kept")
        N_WEIGHTS = 13 + WS

        block = st.enter_context(nc.Block())

        def A(name, j, b):
            return at(A_ORDER, A_FIRST, A_BANKS, name, j, b)

        def Dd(name, j, b):
            return at(D_ORDER, D_FIRST, D_BANKS, name, j, b)

        def product_count(n, i):
            if isinstance(n, int) and n == 0:
                return (i // WS) * len(POOL_FIRST) + POOL_FIRST.index(i % WS) + 1
            return (n - 1) * TMP_ITEMS + (2 * len(POOL_FIRST) + i + 1)

        def make_product(eng, tensor_tensor, n, i, query, probabilities, done):
            item = n * TMP_ITEMS + i
            eng.wait_ge(consumed, item + 1)
            if probabilities:
                a = qkv[:, :, 2 * C:3 * C].rearrange("p k (h d) -> p k h d", h=H)
                w = probs[:, :, query * H:(query + 1) * H].unsqueeze(3).to_broadcast([P, WS, H, D1])
                o = products[i % 2][:].rearrange("p k (h d) -> p k h d", h=H)
            else:
                a = qkv[:, :, C:2 * C]
                w = qkv[:, query:query + 1, 0:C].to_broadcast([P, WS, C])
                o = products[i % 2][:]
            done(tensor_tensor(o, a, w, ALU.mult))

        @block.sync
        def _(sp):
            def load_windows(n):
                for i in range(GB):
                    rows = x_flat[bass.ds(n * GB + i, 1), SHIFT * C:SHIFT * C + (BLK - 1) * WS * C]
                    sp.dma_start(xw[i * BLK:(i + 1) * BLK - 1, :, :],
                                 rows.rearrange("a (w f) -> (a w) f", f=WS * C)).then_inc(xw_in, 16)
                seqs = x_flat[bass.ds(n * GB, GB)]
                sp.dma_start(xw[BLK - 1::BLK, 0:SHIFT, :], seqs[:, (N - SHIFT) * C:N * C]).then_inc(xw_in, 16)
                sp.dma_start(xw[BLK - 1::BLK, SHIFT:WS, :], seqs[:, 0:SHIFT * C]).then_inc(xw_in, 16)

            def load_tiles(j, b):
                for half in range(2):
                    sp.dma_start(xb[:, b % 2, half, :], half_of(x, j, half)).then_inc(tile_in[b % 2], 16)
                sp.dma_start(ctx[0:CTX, b % 2, :], ctx_768[bass.ds(j, 1)].rearrange("a k c -> (a k) c"))\
                    .then_inc(tile_in[b % 2], 16)

            load_windows(0)
            sp.dma_start(b1rows, v["b1"].rearrange("e (c p) -> (e c) p", p=P)).then_inc(b1_in, 16)
            sp.dma_start(wqkv[:], v["w_qkv"].rearrange("(k p) n -> p k n", p=P)).then_inc(weights, 16)
            sp.dma_start(bqkv_b[:], v["b_qkv"].partition_broadcast(P)).then_inc(weights, 16)
            for key in range(WS):
                row = 7 * (2 * WS - 1) + (WS - 1) - key
                sp.dma_start(relbias[:, key, :], v["bias_table"][row:row + WS, :].rearrange("a h -> (a h)")
                             .partition_broadcast(P)).then_inc(weights, 16)
            sp.dma_start(wproj[:], v["w_proj"].rearrange("(k p) n -> p k n", p=P)).then_inc(weights, 16)
            sp.dma_start(bproj_b[:], v["b_proj"].partition_broadcast(P)).then_inc(weights, 16)
            load_tiles(0, 0)
            load_tiles(1, 1)
            sp.dma_start(wk[:, 0, :], v["Wk"][0:P, :]).then_inc(weights, 16)
            sp.dma_start(wk[0:CTXD - P, 1, :], v["Wk"][P:CTXD, :]).then_inc(weights, 16)
            sp.dma_start(wv[:, 0, :], v["Wv"][0:P, :]).then_inc(weights, 16)
            sp.dma_start(wv[0:CTXD - P, 1, :], v["Wv"][P:CTXD, :]).then_inc(weights, 16)
            sp.dma_start(wq[:], v["Wq"].rearrange("(k p) n -> p k n", p=P)).then_inc(weights, 16)
            sp.dma_start(wo[:], v["Wo"].rearrange("(k p) n -> p k n", p=P)).then_inc(weights, 16)
            sp.dma_start(bo_b[:], v["bo"].partition_broadcast(P)).then_inc(weights, 16)
            sp.dma_start(rw[:], v["router_w"].rearrange("(k p) n -> p k n", p=P)).then_inc(weights, 16)
            sp.dma_start(rb_b[:], v["router_b"].partition_broadcast(P)).then_inc(weights, 16)
            sp.wait_ge(pool_step, 15)
            for row in range(0, NT * ET, CH * P):
                k = min(CH, (NT * ET - row) // P)
                sp.dma_start(sorted_x[row:row + k * P, :].rearrange("(k p) c -> p k c", p=P), o2T[:, 0:k, :])\
                    .then_inc(zeros_in, 16)

            def turn(g, more):
                if more:
                    sp.wait_ge(consumed, 2 + TMP_ITEMS * (g + 1))
                    load_windows(g + 1)
                for b in range(GB):
                    if not more and b >= GB - 2:
                        continue
                    j = g * GB + b
                    sp.wait_ge(a_full, A("XN2", j, b)[0] + 1)
                    load_tiles(j + 2, b)

            with sp.Fori(0, NG - 1) as g:
                turn(g, True)
            turn(NG - 1, False)

        @block.gpsimd
        def _(pool):
            s = Steps(pool, pool_step)
            s.done(nc.gpsimd.memset(ident[:], 0.0))
            s.done(nc.gpsimd.memset(identb[:], 0.0))
            for m in (ident, identb):
                nc.gpsimd.affine_select(out=m[:], in_=m[:], compare_op=ALU.not_equal, fill=1.0, base=0,
                                        pattern=[[-1, P]], channel_multiplier=1).then_inc(identities, 1)
            s.done(nc.gpsimd.memset(half_exp[:], -0.5))
            s.done(nc.gpsimd.memset(eps[:], EPS))
            s.done(nc.gpsimd.memset(head_row[:], 0.0))
            s.done(nc.gpsimd.affine_select(out=head_row[:], in_=head_row[:], compare_op=ALU.not_equal, fill=1.0,
                                           base=0, pattern=[[-1, H], [0, CTX]], channel_multiplier=1))
            s.done(nc.gpsimd.memset(ctxT[:], 0.0))
            s.done(nc.gpsimd.memset(wk[CTXD - P:P, 1, :], 0.0))
            s.done(nc.gpsimd.memset(wv[CTXD - P:P, 1, :], 0.0))
            s.done(nc.gpsimd.memset(kT[:], 0.0))
            s.done(nc.gpsimd.memset(kTb[:], 0.0))
            s.done(nc.gpsimd.memset(nmT[:], 0.0))
            s.done(nc.gpsimd.memset(pT[:], 0.0))
            s.done(nc.gpsimd.memset(o2T[:], 0.0))
            nc.gpsimd.memset(vo[:], 1.0).then_inc(identities, 1)
            pool.wait_ge(identities, 3)

            def rstd(variance, ve, rs, k, ready, signal, value):
                pool.wait_ge(ready, value)
                s.done(nc.gpsimd.tensor_tensor(ve, variance, eps[:, 0:k], ALU.add))
                then(pool, nc.gpsimd.tensor_tensor(rs, ve, half_exp[:, 0:k], ALU.pow), signal, value)

            def rstd1_of(n):
                rstd(mv1[:, :, 1], ve1[:], rs1[:], WS, var1, rstd1, n + 1)

            def product_of(n, i, query, probabilities):
                make_product(pool, nc.gpsimd.tensor_tensor, n, i, query, probabilities,
                             lambda ins: then(pool, ins, product, product_count(n, i)))

            def add_projection_bias(j, b, loads):
                pool.wait_ge(tile_in[b % 2], loads)
                then(pool, nc.gpsimd.tensor_tensor(xb[:, b % 2], xb[:, b % 2],
                                                   bproj_b[:].unsqueeze(1).to_broadcast([P, 2, C]), ALU.add),
                     xb_biased, j + 1)

            def norm2(j):
                rstd(mv2[:, 0, :, 1], ve2[:, 0], rs2[:, 0], 2, var2, rstd2, j + 1)

            def norm3(j):
                rstd(mv2[:, 1, :, 1], ve2[:, 1], rs2[:, 1], 2, var3, rstd3, j + 1)

            def bias_x1(j):
                pool.wait_ge(normed2, j + 1)
                then(pool, nc.gpsimd.tensor_tensor(x1[:], x1[:], bo_b[:].unsqueeze(1).to_broadcast([P, 2, C]),
                                                   ALU.add), x1_biased, j + 1)

            pool.wait_ge(weights, 16 * N_WEIGHTS)
            rstd1_of(0)
            pool.wait_ge(wd_done, 1 + WD_ITEMS)
            for i in POOL_FIRST:
                product_of(0, i, i, False)
            pool.wait_ge(probs_ready, 1)
            for i in POOL_FIRST:
                product_of(0, WS + i, i, True)
            add_projection_bias(0, 0, 48)
            norm2(0)

            def turn(g, more):
                n = g + 1
                for b in range(GB):
                    j = g * GB + b
                    last = not more and b == GB - 1
                    bias_x1(j)
                    if not last:
                        add_projection_bias(j + 1, b + 1, (g * 2 + (b + 1) // 2 + 1) * 48)
                    if more and b == 0:
                        rstd1_of(n)
                    if more and b == 1:
                        pool.wait_ge(wd_done, 1 + WD_ITEMS * (n + 1))
                        for i in range(6):
                            product_of(n, i, i, False)
                    if more and b == 2:
                        for i in range(6, WS):
                            product_of(n, i, i, False)
                        pool.wait_ge(probs_ready, n + 1)
                        for i in range(3):
                            product_of(n, WS + i, i, True)
                    if more and b == 3:
                        for i in range(3, WS):
                            product_of(n, WS + i, i, True)
                    norm3(j)
                    if not last:
                        norm2(j + 1)

            with pool.Fori(0, NG - 1) as g:
                s.loop(g, 9)
                turn(g, True)
                s.turned()
            s.before += 9 * (NG - 1)
            s.turn = s.per_turn = 0
            turn(NG - 1, False)

        @block.scalar
        def _(act):
            copy = ACT.Copy
            act.wait_ge(identities, 3)
            then(act, nc.scalar.activation(rden[:, 0:1], ident[:, 0:1], copy), act_step, 1)
            nc.scalar.activation(rden[:, 1:2], ident[:, 0:1], copy).then_inc(a_done, A_BANKS)
            nc.scalar.activation(rden[:, 2:3], ident[:, 0:1], copy).then_inc(wa_done, 2)

            act.wait_ge(b1_turned, 1)
            nc.scalar.activation(b1T[:].rearrange("p e c -> p (e c)"), psA[:, 0, 0:P], copy).then_inc(b1_kept, 1)

            def window_turned(n, k):
                item = n * WA_ITEMS + k
                act.wait_ge(wa_full, item + 1)
                src = psW[:, k % 2, :]
                then(act, nc.scalar.activation(
                    xnT[:, :, 2 * k:2 * k + 2, :].rearrange("p k i w -> p i k w"),
                    src.rearrange("p (i k w) -> p i k w", i=2, k=KC), copy), wa_done, item + 3)

            def output_turned(n, k):
                item = n * WA_ITEMS + 4 + k
                act.wait_ge(wa_full, item + 1)
                ps = psW[:, k % 2, :].rearrange("p (i k w) -> p i k w", i=2, k=KC)
                for i in range(2):
                    dst = oT[:, :, :, 2 * k + i, :]
                    src = ps[:, i].rearrange("p k (b w) -> p k b w", b=GB)
                    if 2 * k < SHIFT:
                        last = nc.scalar.activation(dst, src, copy)
                    else:
                        nc.scalar.activation(dst[:, :, :, 1:BLK], src[:, :, :, 0:BLK - 1], copy)
                        last = nc.scalar.activation(dst[:, :, :, 0:1], src[:, :, :, BLK - 1:BLK], copy)
                then(act, last, wa_done, item + 3)

            def full(name, j, b):
                item, bank = A(name, j, b)
                act.wait_ge(a_full, item + 1)
                return psA[:, bank, :], item + A_BANKS + 1

            def turn_context(j, b):
                ps, value = full("CTX'", j, b)
                nc.scalar.activation(ctxT[:, 0, 0:CTX], ps[:, 0:CTX], copy)
                then(act, nc.scalar.activation(ctxT[0:CTXD - P, 1, 0:CTX], ps[0:CTXD - P, P:P + CTX], copy), a_done, value)

            def keys(j, b):
                for half in range(2):
                    ps, value = full(f"K{half}'", j, b)
                    ps = ps.rearrange("p (u k) -> p u k", u=4)
                    us = slice(4 * half, 4 * half + 4)
                    for parity in range(2):
                        rows = slice(parity * D2, (parity + 1) * D2)
                        nc.scalar.activation(kT[rows, us, parity, :], ps[rows, :, 0:CTX], copy)
                        last = nc.scalar.activation(kTb[rows, us, parity, :], ps[rows, :, 0:CTX], copy)
                    then(act, last, a_done, value)

            def output2_turned(m, j, b):
                ps, value = full(f"O{m}" if m != "CTX'" else m, j, b)
                m = 3 if m == "CTX'" else m
                then(act, nc.scalar.activation(o2T[:, 2 * m:2 * m + 2, :].rearrange("p u n -> p (u n)"), ps, copy),
                     a_done, value)

            for k in range(4):
                window_turned(0, k)
            act.wait_ge(shifted, 1)
            then(act, nc.scalar.activation(probs[:], probs[:], ACT.Exp), exped, 1)
            turn_context(-1, -1)
            keys(-1, -1)
            for k in range(4):
                output_turned(0, k)

            def turn(g, more):
                n = g + 1
                for b in range(GB):
                    j = g * GB + b
                    ps, value = full("XN2", j, b)
                    then(act, nc.scalar.activation(xT[:].rearrange("p k n -> p (k n)"), ps, copy), a_done, value)
                    for q in range(4):
                        ps, value = full(f"Q{q}", j, b)
                        nc.scalar.activation(qTb[:, 2 * q:2 * q + 2, :].rearrange("p u n -> p (u n)"), ps, copy)
                        then(act, nc.scalar.activation(qT[:, 2 * q:2 * q + 2, :].rearrange("p u n -> p (u n)"), ps, copy),
                             a_done, value)
                    ps, value = full("NM", j, b)
                    then(act, nc.scalar.activation(nmT[0:H, :], ps[0:H, 0:P].bitcast(BF16), copy), a_done, value)
                    if more and b == 2:
                        act.wait_ge(shifted, n + 1)
                        then(act, nc.scalar.activation(probs[:], probs[:], ACT.Exp), exped, n + 1)
                    for u in range(CH):
                        ps, value = full(f"S{u}", j, b)
                        then(act, nc.scalar.activation(pT[0:CTX, u % 4, :], ps[0:CTX, :], ACT.Exp, scale=D2 ** -0.5),
                             a_done, value)
                        if more and b == 0 and u in (3, 5):
                            window_turned(n, u - 3)
                            window_turned(n, u - 2)
                        if u == 5:
                            output2_turned(0, j, b)
                    last = not more and b == GB - 1
                    for k in range(4):
                        if more and b == 3:
                            output_turned(n, k)
                        if k in (0, 2):
                            output2_turned(1 + k // 2, j, b)
                    if not last:
                        turn_context(j, b)
                        output2_turned(3, j, b)
                        keys(j, b)
                        ps, value = full("XN3", j, b)
                    else:
                        output2_turned("CTX'", j, b)
                        ps, value = full("O3", j, b)
                    then(act, nc.scalar.activation(xT[:].rearrange("p k n -> p (k n)"), ps, copy), a_done, value)

            with act.Fori(0, NG - 1) as g:
                turn(g, True)
            turn(NG - 1, False)

        @block.vector
        def _(dve):
            s = Steps(dve, vec_step)
            dve.wait_ge(identities, 3)
            nc.vector.memset(red[:, 0:1], 0.0).then_inc(d_done, D_BANKS)
            nc.vector.memset(red[:, 1:2], 0.0).then_inc(wd_done, 1)
            nc.vector.memset(red[:, 2:3], 0.0).then_inc(consumed, 2)
            dve.wait_ge(consumed, 2)
            dve.wait_ge(weights, 16 * N_WEIGHTS)

            def carry_waits():
                nc.vector.memset(idle[:], 0.0)

            def norm1_stats(n):
                dve.wait_ge(xw_in, (n + 1) * 16 * (GB + 2))
                for i in range(WS):
                    ins = nc.vector.bn_stats(st1[:, i, :], xw[:, i, :])
                s.done(ins)
                carry_waits()
                for i in range(WS):
                    ins = nc.vector.bn_aggr(mv1[:, i, :], st1[:, i, :])
                then(dve, ins, var1, n + 1)

            def norm1(n):
                dve.wait_ge(rstd1, n + 1)
                for i in range(WS):
                    ins = nc.vector.tensor_scalar(xw[:, i, :], xw[:, i, :], mv1[:, i, 0:1], rs1[:, i:i + 1],
                                                  ALU.subtract, ALU.mult)
                    if i % 2:
                        then(dve, ins, normed1, n * 4 + i // 2 + 1)

            def window_qkv(n, pair, part):
                item = n * WD_ITEMS + 3 * pair + part
                dve.wait_ge(wd_full, item + 1)
                ps = psW[:, (3 * pair + part) % 2, :]
                if part < 2:
                    ins = nc.vector.tensor_tensor(qkv[:, 2 * pair + part, 0:2 * C], ps, bqkv_b[:, 0:2 * C], ALU.add)
                else:
                    ins = nc.vector.tensor_tensor(qkv[:, 2 * pair:2 * pair + 2, 2 * C:3 * C],
                                                  ps.rearrange("p (i c) -> p i c", i=2),
                                                  bqkv_b[:, 2 * C:3 * C].unsqueeze(1).to_broadcast([P, 2, C]), ALU.add)
                then(dve, ins, wd_done, item + 2)

            def sum_scores(n, i):
                item = n * TMP_ITEMS + i
                if not isinstance(n, int) or i in POOL_FIRST:
                    dve.wait_ge(product, product_count(n, i))
                then(dve, nc.vector.tensor_reduce(probs[:, :, i * H:(i + 1) * H],
                                                  products[i % 2][:].rearrange("p k (h d) -> p k h d", h=H),
                                                  axis=X, op=ALU.add), consumed, item + 3)

            by_key = probs[:].rearrange("p k m -> p m k")

            def window_shift(n):
                s.done(nc.vector.scalar_tensor_tensor(probs[:], probs[:], D1 ** -0.5, relbias[:], ALU.mult, ALU.add))
                s.done(nc.vector.tensor_reduce(red[:], by_key, axis=X, op=ALU.max))
                then(dve, nc.vector.tensor_tensor(probs[:], probs[:],
                                                  red[:].unsqueeze(1).to_broadcast([P, WS, WS * H]), ALU.subtract), shifted, n + 1)

            def window_divide(n):
                dve.wait_ge(exped, n + 1)
                s.done(nc.vector.tensor_reduce(red[:], by_key, axis=X, op=ALU.add))
                s.done(nc.vector.reciprocal(red[:], red[:]))
                then(dve, nc.vector.tensor_tensor(probs[:], probs[:], red[:].unsqueeze(1).to_broadcast([P, WS, WS * H]),
                                                  ALU.mult), probs_ready, n + 1)

            def sum_values(n, i):
                item = n * TMP_ITEMS + WS + i
                t = products[i % 2]
                if not isinstance(n, int) or i in POOL_FIRST:
                    dve.wait_ge(product, product_count(n, WS + i))
                s.done(nc.vector.tensor_tensor(t[:, 0:4, :], t[:, 0:4, :], t[:, 4:8, :], ALU.add))
                s.done(nc.vector.tensor_tensor(t[:, 0:2, :], t[:, 0:2, :], t[:, 2:4, :], ALU.add))
                then(dve, nc.vector.tensor_tensor(qkv[:, i, 0:C], t[:, 0, :], t[:, 1, :], ALU.add), consumed, item + 3)

            def full(name, j, b):
                item, bank = Dd(name, j, b)
                dve.wait_ge(d_full, item + 1)
                return psD[:, bank, :], item + D_BANKS + 1

            def start_sequence(j, b):
                ps, value = full("PROJ'", j, b)
                dve.wait_ge(xb_biased, j + 2)
                then(dve, nc.vector.tensor_tensor(x1[:].rearrange("p k c -> p (k c)"), ps,
                                                  xb[:, (b + 1) % 2].rearrange("p k c -> p (k c)"), ALU.add), d_done, value)
                for half in range(2):
                    ins = nc.vector.bn_stats(st2[:, 0, half, :], x1[:, half, :])
                s.done(ins)
                carry_waits()
                for half in range(2):
                    ins = nc.vector.bn_aggr(mv2[:, 0, half, :], st2[:, 0, half, :])
                then(dve, ins, var2, j + 2)

            def keep_values(half, name, j, b):
                ps, value = full(name, j, b)
                then(dve, nc.vector.tensor_copy(vo[:, 8 * half:8 * half + 8, 0:D2],
                                                ps.rearrange("p (h d) -> p h d", h=8)), d_done, value)

            def norm2(j):
                dve.wait_ge(rstd2, j + 1)
                for half in range(2):
                    ins = nc.vector.tensor_scalar(xn[:, half, :], x1[:, half, :], mv2[:, 0, half, 0:1],
                                                  rs2[:, 0, half:half + 1], ALU.subtract, ALU.mult)
                then(dve, ins, normed2, j + 1)

            norm1_stats(0)
            norm1(0)
            for k in range(WD_ITEMS):
                window_qkv(0, k // 3, k % 3)
            for i in range(WS):
                if i not in POOL_FIRST:
                    make_product(dve, nc.vector.tensor_tensor, 0, i, i, False, s.done)
                sum_scores(0, i)
            window_shift(0)
            window_divide(0)
            for i in range(WS):
                if i not in POOL_FIRST:
                    make_product(dve, nc.vector.tensor_tensor, 0, WS + i, i, True, s.done)
                sum_values(0, i)
            start_sequence(-1, -1)
            norm2(0)
            keep_values(0, "V0'", -1, -1)
            dve.wait_ge(zeros_in, 16 * -(-NT * ET // (CH * P)))

            def turn(g, more):
                n = g + 1
                for b in range(GB):
                    j = g * GB + b
                    keep_values(1, "V1", j, b)
                    for m in range(4):
                        for t in range(2):
                            ps, value = full(f"MAX{2 * m + t}", j, b)
                            then(dve, nc.vector.tensor_reduce(
                                nm[:, t, 4 * m:4 * m + 4], ps[:, 0:4 * CTX].rearrange("p (h k) -> p h k", h=4),
                                axis=X, op=ALU.max, negate=True), d_done, value)
                    if more and b == 0:
                        norm1_stats(n)
                    if more and b == 1:
                        sum_scores(n, 0)
                        sum_scores(n, 1)
                    if more and b == 2:
                        sum_scores(n, 6)
                        sum_scores(n, 7)
                        window_shift(n)
                    if more and b == 3:
                        sum_values(n, 2)
                        sum_values(n, 3)
                    for u in range(CH):
                        ps, value = full(f"PV{u}", j, b)
                        ps = ps.rearrange("p (h c) -> p h c", h=4)
                        if u >= 4 and u % 2 == 0:
                            dve.wait_ge(a_full, A(f"O{u // 2 - 2}", j, b)[0] + 1)
                        s.done(nc.vector.reciprocal(rden[:], ps[:, :, D2]))
                        then(dve, nc.vector.tensor_tensor(
                            o2[:, u // 2 % 2, u % 2, :].rearrange("p (h d) -> p h d", h=4),
                            ps[:, :, 0:D2], rden[:].unsqueeze(2).to_broadcast([P, 4, D2]), ALU.mult), d_done, value)
                        if more and b == 0 and u == 0:
                            norm1(n)
                        if more and b == 0 and u >= 2:
                            for part in QKV_PARTS[u]:
                                window_qkv(n, *part)
                        if more and b == 1 and u % 2 == 1:
                            sum_scores(n, 2 + u // 2)
                        if more and b == 2 and u == 1:
                            window_divide(n)
                        if more and b == 2 and u in (5, 7):
                            sum_values(n, (u - 5) // 2)
                        if more and b == 3 and u in (0, 2, 4, 5):
                            sum_values(n, {0: 4, 2: 5, 4: 6, 5: 7}[u])
                    ps, value = full("X2", j, b)
                    dve.wait_ge(x1_biased, j + 1)
                    mine = x2[:, bass.ds(j, 1), :, :].rearrange("p a k c -> p (a k) c")
                    then(dve, nc.vector.tensor_tensor(mine, ps.rearrange("p (k c) -> p k c", k=2), x1[:], ALU.add),
                         d_done, value)
                    carry_waits()
                    for half in range(2):
                        ins = nc.vector.bn_stats(st2[:, 1, half, :], mine[:, half, :])
                    s.done(ins)
                    carry_waits()
                    for half in range(2):
                        ins = nc.vector.bn_aggr(mv2[:, 1, half, :], st2[:, 1, half, :])
                    then(dve, ins, var3, j + 1)
                    last = not more and b == GB - 1
                    if not last:
                        start_sequence(j, b)
                    dve.wait_ge(rstd3, j + 1)
                    for half in range(2):
                        ins = nc.vector.tensor_scalar(xn3[:, half, :], mine[:, half, :], mv2[:, 1, half, 0:1],
                                                      rs2[:, 1, half:half + 1], ALU.subtract, ALU.mult)
                    then(dve, ins, normed3, j + 1)
                    kept = ln3[:, bass.ds(j, 1), :, :].rearrange("p a k m -> p (a k) m")
                    nc.vector.tensor_copy(kept[:, :, 0], mv2[:, 1, :, 0])
                    s.done(nc.vector.tensor_copy(kept[:, :, 1], rs2[:, 1, :]))
                    if not last:
                        norm2(j + 1)
                        keep_values(0, "V0'", j, b)
                    item, bank = Dd("PROJ'" if last else "LOG", j, b)
                    dve.wait_ge(d_full, item + 1)
                    then(dve, nc.vector.tensor_tensor(
                        logits[:, bass.ds(j, 1), :, :].rearrange("p a k e -> p (a k) e"),
                        psD[:, bank, 0:2 * E].rearrange("p (k e) -> p k e", k=2),
                        rb_b[:].unsqueeze(1).to_broadcast([P, 2, E]), ALU.add), d_done, item + D_BANKS + 1)

            with dve.Fori(0, NG - 1) as g:
                s.loop(g, 65)
                turn(g, True)
                s.turned()
            s.before += 65 * (NG - 1)
            s.turn = s.per_turn = 0
            turn(NG - 1, False)

        @block.tensor
        def _(pe):
            mm = nc.tensor.matmul
            pe.wait_ge(identities, 3)
            pe.wait_ge(b1_in, 16)
            nc.tensor.transpose(psA[:, 0, 0:P], b1rows, ident[:]).then_inc(b1_turned, 1)
            pe.wait_ge(b1_kept, 1)
            pe.wait_ge(weights, 16 * N_WEIGHTS)

            def free(order, first, banks, done, ps, name, j, b):
                item, bank = at(order, first, banks, name, j, b)
                pe.wait_ge(done, item + 1)
                return ps[:, bank, :]

            def freeA(name, j, b):
                return free(A_ORDER, A_FIRST, A_BANKS, a_done, psA, name, j, b)

            def freeD(name, j, b):
                return free(D_ORDER, D_FIRST, D_BANKS, d_done, psD, name, j, b)

            def take_a(name, j, b):
                pe.wait_ge(a_done, A(name, j, b)[0] + A_BANKS + 1)

            def window_turn(n, k):
                pe.wait_ge(normed1, n * 4 + k + 1)
                pe.wait_ge(wa_done, n * WA_ITEMS + k + 1)
                for i in range(2):
                    for c in range(KC):
                        ins = nc.tensor.transpose(psW[:, k % 2, (i * KC + c) * P:(i * KC + c + 1) * P],
                                                  xw[:, 2 * k + i, c * P:(c + 1) * P], ident[:])
                ins.then_inc(wa_full, 1)

            def window_qkv(n, pair, part):
                k = 3 * pair + part
                if part == 0:
                    pe.wait_ge(wa_done, n * WA_ITEMS + pair + 3)
                if k < 2:
                    pe.wait_ge(wa_done, n * WA_ITEMS + k + 5)
                else:
                    pe.wait_ge(wd_done, n * WD_ITEMS + k)
                for i in ([2 * pair + part] if part < 2 else [2 * pair, 2 * pair + 1]):
                    cols = slice(0, 2 * C) if part < 2 else slice(2 * C, 3 * C)
                    dst = psW[:, k % 2, :] if part < 2 else psW[:, k % 2, (i % 2) * C:(i % 2 + 1) * C]
                    for c in range(KC):
                        ins = mm(dst, xnT[:, c, i, :], wqkv[:, c, cols], start=c == 0, stop=c == KC - 1)
                ins.then_inc(wd_full, 1)

            def output_turn(n, k):
                pe.wait_ge(consumed, 2 + n * TMP_ITEMS + WS + 2 * k + 2)
                if k < 2:
                    pe.wait_ge(wd_done, (n + 1) * WD_ITEMS + k)
                else:
                    pe.wait_ge(wa_done, n * WA_ITEMS + 4 + k + 1)
                for i in range(2):
                    for c in range(KC):
                        ins = nc.tensor.transpose(psW[:, k % 2, (i * KC + c) * P:(i * KC + c + 1) * P],
                                                  qkv[:, 2 * k + i, c * P:(c + 1) * P], ident[:])
                ins.then_inc(wa_full, 1)

            def project(j, b, group):
                q = (b + 1) % GB
                pe.wait_ge(wa_done, (group + 1) * WA_ITEMS + 2)
                ps = freeD("PROJ'", j, b)
                for half in range(2):
                    for c in range(KC):
                        ins = mm(ps[:, half * C:(half + 1) * C],
                                 oT[:, c, q, 4 * half:4 * half + 4, :].rearrange("p i w -> p (i w)"), wproj[:, c, :],
                                 start=c == 0, stop=c == KC - 1)
                ins.then_inc(d_full, 1)

            def turn_context(j, b, loads):
                ps = freeA("CTX'", j, b)
                pe.wait_ge(tile_in[(b + 1) % 2], loads)
                nc.tensor.transpose(ps[:, 0:CTX], ctx[0:CTX, (b + 1) % 2, 0:P], ident[0:CTX, 0:CTX])
                nc.tensor.transpose(ps[0:CTXD - P, P:P + CTX], ctx[0:CTX, (b + 1) % 2, P:CTXD],
                                    ident[0:CTX, 0:CTX]).then_inc(a_full, 1)

            def keys(j, b):
                take_a("CTX'", j, b)
                for half in range(2):
                    ps = freeA(f"K{half}'", j, b)
                    for u in range(4):
                        for c in range(KC):
                            ins = mm(ps[:, u * P:(u + 1) * P], wk[:, c, (4 * half + u) * P:(4 * half + u + 1) * P],
                                     ctxT[:, c, :], start=c == 0, stop=c == KC - 1)
                    ins.then_inc(a_full, 1)

            def context_values(half, name, j, b):
                ps = freeD(name, j, b)
                for c in range(KC):
                    ins = mm(ps, ctxT[:, c, :], wv[:, c, half * 512:(half + 1) * 512], start=c == 0, stop=c == KC - 1)
                ins.then_inc(d_full, 1)

            for k in range(4):
                window_turn(0, k)
            for k in range(WD_ITEMS):
                window_qkv(0, k // 3, k % 3)
            turn_context(-1, -1, 48)
            keys(-1, -1)
            for k in range(4):
                output_turn(0, k)
            project(-1, -1, 0)
            context_values(0, "V0'", -1, -1)

            def turn(g, more):
                n = g + 1
                for b in range(GB):
                    j = g * GB + b
                    pe.wait_ge(normed2, j + 1)
                    ps = freeA("XN2", j, b)
                    for c in range(KC):
                        for half in range(2):
                            ins = nc.tensor.transpose(ps[:, (c * 2 + half) * P:(c * 2 + half + 1) * P],
                                                      xn[:, half, c * P:(c + 1) * P], ident[:])
                    ins.then_inc(a_full, 1)
                    context_values(1, "V1", j, b)

                    def queries(q):
                        if q == 0:
                            take_a("XN2", j, b)
                        ps = freeA(f"Q{q}", j, b)
                        for u in range(2):
                            for c in range(KC):
                                ins = mm(ps[:, u * N:(u + 1) * N], wq[:, c, (2 * q + u) * P:(2 * q + u + 1) * P],
                                         xT[:, c, :], start=c == 0, stop=c == KC - 1)
                        ins.then_inc(a_full, 1)

                    def scores_for_max(m):
                        take_a(f"Q{m}", j, b)
                        for t in range(2):
                            ps = freeD(f"MAX{2 * m + t}", j, b)
                            for i in range(2):
                                u = 2 * m + i
                                ins = mm(ps[:, 2 * i * CTX:2 * (i + 1) * CTX], qTb[:, u, t * P:(t + 1) * P],
                                         kTb[:, u].rearrange("p m k -> p (m k)"), start=True, stop=True)
                            ins.then_inc(d_full, 1)

                    def score_products(u, m):
                        ps = freeA(f"S{u}", j, b)
                        mm(ps[0:CTX, m * N:(m + 1) * N], kT[:, u, m, :], qT[:, u, :], start=True, stop=False)

                    def score_shift(u, m):
                        ps = psA[:, A(f"S{u}", j, b)[1], :]
                        ins = mm(ps[0:CTX, m * N:(m + 1) * N], head_row[:, 2 * u + m, :], nmT[:], start=False, stop=True)
                        if m == 1:
                            ins.then_inc(a_full, 1)

                    def scores(u):
                        for m in range(2):
                            score_products(u, m)
                            score_shift(u, m)

                    def values(v):
                        w, t = v // 2, v % 2
                        take_a(f"S{2 * w + 1}", j, b)
                        ps = freeD(f"PV{v}", j, b)
                        for m in range(4):
                            ins = mm(ps[:, m * P:(m + 1) * P],
                                     pT[:, (2 * w + m // 2) % 4, (m % 2) * N + t * P:(m % 2) * N + (t + 1) * P],
                                     vo[:, 4 * w + m, :], start=True, stop=True)
                        ins.then_inc(d_full, 1)

                    def turn_output2(m, name=None):
                        pe.wait_ge(d_done, Dd(f"PV{2 * m + 1}", j, b)[0] + D_BANKS + 1)
                        ps = freeA(name or f"O{m}", j, b)
                        for u in range(2):
                            for t in range(2):
                                ins = nc.tensor.transpose(ps[:, (2 * u + t) * P:(2 * u + t + 1) * P],
                                                          o2[:, m % 2, t, u * P:(u + 1) * P], ident[:])
                        ins.then_inc(a_full, 1)

                    queries(0)
                    for q in range(1, 4):
                        queries(q)
                        scores_for_max(q - 1)
                    score_products(0, 0)
                    scores_for_max(3)
                    score_products(1, 0)
                    ps = freeA("NM", j, b)
                    for t in range(2):
                        pe.wait_ge(d_done, Dd(f"MAX{6 + t}", j, b)[0] + D_BANKS + 1)
                        ins = nc.tensor.transpose(ps[0:H, t * 64:(t + 1) * 64].bitcast(BF16), nm[:, t, :], identb[:])
                    ins.then_inc(a_full, 1)
                    take_a("NM", j, b)
                    for u in range(2):
                        score_shift(u, 0)
                        score_products(u, 1)
                        score_shift(u, 1)
                    scores(2)
                    scores(3)
                    for v in range(8):
                        values(v)
                        if more and b == 0 and v > 2:
                            window_qkv(n, *QKV_PARTS[v][0])
                        if more and b == 0 and v in (1, 2):
                            window_turn(n, 2 * v - 2)
                            window_turn(n, 2 * v - 1)
                        if v in (1, 3):
                            scores(v + 3)
                            scores(v + 4)
                        if more and b == 3 and v >= 4:
                            output_turn(n, v - 4)
                        if v in (2, 4, 6):
                            turn_output2(v // 2 - 1)
                        if more and b == 0 and v >= 2:
                            for part in QKV_PARTS[v][v > 2:]:
                                window_qkv(n, *part)
                    last = not more and b == GB - 1
                    if not last:
                        turn_context(j, b, (g * 2 + (b + 1) // 2 + 1) * 48)
                    turn_output2(3, "CTX'" if last else "O3")
                    ps = freeD("X2", j, b)
                    for half in range(2):
                        for u in range(CH):
                            if half == 0 and u % 2 == 0:
                                take_a("CTX'" if last and u == 6 else f"O{u // 2}", j, b)
                            ins = mm(ps[:, half * C:(half + 1) * C], o2T[:, u, half * P:(half + 1) * P], wo[:, u, :],
                                     start=u == 0, stop=u == CH - 1)
                    ins.then_inc(d_full, 1)
                    if not last:
                        project(j, b, g if b < GB - 1 else g + 1)
                        keys(j, b)
                    pe.wait_ge(normed3, j + 1)
                    ps = freeA("O3" if last else "XN3", j, b)
                    for c in range(KC):
                        for half in range(2):
                            ins = nc.tensor.transpose(ps[:, (c * 2 + half) * P:(c * 2 + half + 1) * P],
                                                      xn3[:, half, c * P:(c + 1) * P], ident[:])
                    ins.then_inc(a_full, 1)
                    if not last:
                        context_values(0, "V0'", j, b)
                    take_a("O3" if last else "XN3", j, b)
                    ps = freeD("PROJ'" if last else "LOG", j, b)
                    for half in range(2):
                        for c in range(KC):
                            ins = mm(ps[:, half * E:(half + 1) * E], xT[:, c, half * P:(half + 1) * P], rw[:, c, :],
                                     start=c == 0, stop=c == KC - 1)
                    ins.then_inc(d_full, 1)

            with pe.Fori(0, NG - 1) as g:
                turn(g, True)
            turn(NG - 1, False)


def experts(nc, outer, v):
    ident, x2, logits, ln3, b1T = (v[k] for k in ("ident", "x2", "logits", "ln3", "b1T"))
    sorted_x, sorted_y, out, half_of = v["sorted_x"], v["sorted_y"], v["out"], v["half_of"]
    SLOTS = 8
    HB = 4
    with ExitStack() as st:
        def sb(name, shape, dt=F32):
            return st.enter_context(nc.sbuf_tensor(name, shape, dt))

        def sem(name):
            return st.enter_context(nc.semaphore(name))

        psH = st.enter_context(nc.psum_tensor("psH", [P, HB, 2, ET], F32))
        psY = st.enter_context(nc.psum_tensor("psY", [P, 2, 512], F32))
        psT = st.enter_context(nc.psum_tensor("psT", [P, KC, ET], F32))
        psR = st.enter_context(nc.psum_tensor("psR", [P, 2, TT, E], F32))

        upper = sb("upper", [P, P], BF16)
        ones = sb("ones", [P, P], BF16)
        e_less_8 = sb("e_less_8", [P, E])
        k_tiles = sb("k_tiles", [P, B * N // ET])
        tile_no = sb("tile_no", [P, NT])
        best = sb("best", [P, TT])
        cand = sb("cand", [P, TT, E])
        first = sb("first", [P, TT])
        onehot = sb("onehot", [P, TT, E])
        onehotb = sb("onehotb", [P, TT, E], BF16)
        run = sb("run", [P, 2, TT, E])
        total = sb("total", [P, TT, E])
        where = sb("where", [P, TT, E])
        cmp = sb("cmp", [P, E, B * N // ET])
        ntiles = sb("ntiles", [P, E])
        ends = sb("ends", [P, 2, E])
        base = sb("base", [P, E])
        pos = sb("pos", [P, TT])
        posi = sb("posi", [P, TT], U32)
        passed = sb("passed", [P, NT, E])
        tile_e = sb("tile_e", [P, NT])
        tile_ei = sb("tile_ei", [P, NT], I32)
        b1big = sb("b1big", [P, NT, 2 * HC, E])
        b1s = sb("b1s", [P, NT, 2 * HC])
        slots = sb("slots", [P, SLOTS, C])
        w1s = [sb(f"w1s{i}", [P, KC, 2 * HID]) for i in range(2)]
        w2s = [sb(f"w2s{i}", [P, HC, C]) for i in range(2)]
        b2s = sb("b2s", [P, 2, C])
        xs = sb("xs", [P, 2, 2, C])
        xsT = sb("xsT", [P, KC, ET])
        sig = sb("sig", [P, 2, ET])
        gated = sb("gated", [P, 2, ET])
        ys = sb("ys", [P, 2, 2, C])

        pool_step, vec_step = sem("pool_step2"), sem("vec_step2")
        onehot_ready, counted, located = sem("onehot_ready"), sem("counted"), sem("located")
        normed = sem("normed")
        scattered = [sem(f"scattered{i}") for i in range(SLOTS)]
        gathered = [sem(f"gathered{i}") for i in range(SLOTS)]
        out_stored = [sem(f"out_stored{i}") for i in range(SLOTS)]
        summed = sem("summed")
        w_in = [sem("w_in0"), sem("w_in1")]
        xs_in = [sem("xs_in0"), sem("xs_in1")]
        y_stored = [sem("y_stored0"), sem("y_stored1")]
        t_full, t_done, h_full, sig_done, h_done = (sem(k) for k in ("t_full", "t_done", "h_full", "sig_done", "h_done"))
        y_full, y_done = sem("y_full"), sem("y_done")
        block = st.enter_context(nc.Block())
        PAIRS = (NT - 3) // 2
        ROUTE_STEPS = 40

        def tiles(eng, tile):
            with eng.Fori(0, PAIRS) as k:
                for par in range(2):
                    tile(k * 2 + par, par, k)
            for t in range(2 * PAIRS, NT):
                tile(t, t % 2, t // 2)

        @block.sync
        def _(sp):
            def load_weights(t, par):
                e = sp.value_load(tile_ei[0:1, bass.ds(t, 1)], min_val=0, max_val=E - 1)
                sp.dma_start(w1s[par][:], v["w1"][bass.ds(e, 1)].rearrange("a (k p) n -> p (a k) n", p=P))\
                    .then_inc(w_in[par], 16)
                sp.dma_start(w2s[par][:], v["w2"][bass.ds(e, 1)].rearrange("a (k p) n -> p (a k) n", p=P))\
                    .then_inc(w_in[par], 16)
                return e

            def load_bias(e, par):
                sp.dma_start(b2s[:, par, :], v["b2"][bass.ds(e, 1), :].rearrange("a c -> (a c)").partition_broadcast(P))\
                    .then_inc(w_in[par], 16)

            def rows(ap, t):
                return ap[bass.ds(t * ET, ET), :].rearrange("(k p) c -> p k c", p=P)

            def load_tokens(t, par):
                sp.dma_start(xs[:, par], rows(sorted_x, t)).then_inc(xs_in[par], 16)

            sp.wait_ge(located, 1)
            for t in range(2):
                load_bias(load_weights(t, t), t)
            for i in range(SLOTS):
                sp.wait_ge(scattered[i], 16 * (TT // SLOTS))
            for t in range(2):
                load_tokens(t, t)

            def tile(t, par, turn):
                more = not isinstance(t, int) or t + 2 < NT
                sp.wait_ge(y_full, t + 1)
                if more:
                    e = load_weights(t + 2, par)
                    load_tokens(t + 2, par)
                sp.wait_ge(y_done, t + 2)
                if more:
                    load_bias(e, par)
                sp.dma_start(rows(sorted_y, t), ys[:, par]).then_inc(y_stored[par], 16)

            tiles(sp, tile)
            for t in range(TT):
                sp.wait_ge(summed, t + 1)
                sp.dma_start(half_of(out, t // 2, t % 2), slots[:, t % SLOTS, :]).then_inc(out_stored[t % SLOTS], 16)
            for i in range(SLOTS):
                sp.wait_ge(out_stored[i], 16 * (TT // SLOTS))

        @block.gpsimd
        def _(pool):
            s = Steps(pool, pool_step)
            s.done(nc.gpsimd.memset(upper[:], 1.0))
            s.done(nc.gpsimd.affine_select(out=upper[:], in_=upper[:], compare_op=ALU.is_gt, fill=0.0, base=0,
                                           pattern=[[1, P]], channel_multiplier=-1))
            s.done(nc.gpsimd.memset(ones[:], 1.0))
            for dst, step, first_value in ((e_less_8, 1, -E), (k_tiles, ET, 0), (tile_no, 1, 0)):
                s.done(nc.gpsimd.iota(dst[:], pattern=[[step, dst.shape[1]]], base=first_value, channel_multiplier=0,
                                      allow_small_or_imprecise_dtypes=True))
            for t in range(TT):
                pool.wait_ge(normed, t + 1)
                nc.gpsimd.indirect_dma_start(
                    out=sorted_x[:, :], out_offset=bass.IndirectOffsetOnAxis(ap=posi[:, t:t + 1], axis=0),
                    in_=slots[:, t % SLOTS, :], in_offset=None).then_inc(scattered[t % SLOTS], 16)
            pool.wait_ge(y_stored[0], 16 * ((NT + 1) // 2 + 1))
            pool.wait_ge(y_stored[1], 16 * (NT // 2 + 1))
            for t in range(TT):
                if t >= SLOTS:
                    pool.wait_ge(out_stored[t % SLOTS], 16 * (t // SLOTS))
                nc.gpsimd.indirect_dma_start(
                    out=slots[:, t % SLOTS, :], out_offset=None, in_=sorted_y[:, :],
                    in_offset=bass.IndirectOffsetOnAxis(ap=posi[:, t:t + 1], axis=0)).then_inc(gathered[t % SLOTS], 16)

        @block.vector
        def _(dve):
            s = Steps(dve, vec_step)
            tt, reduce = nc.vector.tensor_tensor, nc.vector.tensor_reduce
            dve.wait_ge(pool_step, 6)
            lg = logits[:].rearrange("p b k e -> p (b k) e")

            def over_tiles(ap):
                return ap.unsqueeze(1).to_broadcast([P, TT, E])

            def over_experts(ap, n=TT):
                return ap.unsqueeze(2).to_broadcast([P, n, E])

            s.done(reduce(best[:], lg, axis=X, op=ALU.max))
            s.done(tt(cand[:], lg, over_experts(best[:]), ALU.is_equal))
            s.done(tt(cand[:], cand[:], over_tiles(e_less_8[:]), ALU.mult))
            s.done(reduce(first[:], cand[:], axis=X, op=ALU.min))
            s.done(tt(onehot[:], over_tiles(e_less_8[:]), over_experts(first[:]), ALU.is_equal))
            then(dve, nc.vector.tensor_copy(onehotb[:], onehot[:]), onehot_ready, 1)
            dve.wait_ge(counted, 1)
            s.done(nc.vector.tensor_copy(total[:], psR[:, 1]))
            s.done(nc.vector.tensor_copy(run[:, 0], psR[:, 1]))
            cur = 0
            for step in (1, 2, 4, 8, 16):
                s.done(nc.vector.tensor_copy(run[:, 1 - cur, 0:step, :], run[:, cur, 0:step, :]))
                s.done(tt(run[:, 1 - cur, step:TT, :], run[:, cur, step:TT, :], run[:, cur, 0:TT - step, :], ALU.add))
                cur = 1 - cur
            nk = B * N // ET
            s.done(tt(cmp[:], run[:, cur, TT - 1, :].unsqueeze(2).to_broadcast([P, E, nk]),
                      k_tiles[:].unsqueeze(1).to_broadcast([P, E, nk]), ALU.is_gt))
            s.done(reduce(ntiles[:], cmp[:], axis=X, op=ALU.add))
            s.done(nc.vector.tensor_copy(ends[:, 0, :], ntiles[:]))
            c = 0
            for step in (1, 2, 4):
                s.done(nc.vector.tensor_copy(ends[:, 1 - c, 0:step], ends[:, c, 0:step]))
                s.done(tt(ends[:, 1 - c, step:E], ends[:, c, step:E], ends[:, c, 0:E - step], ALU.add))
                c = 1 - c
            s.done(tt(passed[:], over_experts(tile_no[:], NT), ends[:, c, :].unsqueeze(1).to_broadcast([P, NT, E]),
                      ALU.is_ge))
            s.done(reduce(tile_e[:], passed[:], axis=X, op=ALU.add))
            s.done(nc.vector.tensor_scalar(tile_e[:], tile_e[:], float(E - 1), None, ALU.min))
            then(dve, nc.vector.tensor_copy(tile_ei[:], tile_e[:]), located, 1)
            s.done(tt(base[:], ends[:, c, :], ntiles[:], ALU.subtract))
            s.done(nc.vector.tensor_scalar(base[:], base[:], float(ET), None, ALU.mult))
            s.done(tt(where[:], run[:, cur], total[:], ALU.subtract))
            s.done(tt(where[:], where[:], psR[:, 0], ALU.add))
            s.done(tt(where[:], where[:], over_tiles(base[:]), ALU.add))
            s.done(tt(where[:], where[:], onehot[:], ALU.mult))
            s.done(reduce(pos[:], where[:], axis=X, op=ALU.add))
            s.done(nc.vector.tensor_copy(posi[:], pos[:]))
            for t in range(TT):
                if t >= SLOTS:
                    dve.wait_ge(scattered[t % SLOTS], 16 * (t // SLOTS))
                ln = ln3[:, t // 2, t % 2, :]
                nc.vector.tensor_scalar(slots[:, t % SLOTS, :], x2[:, t // 2, t % 2, :], ln[:, 0:1], ln[:, 1:2],
                                        ALU.subtract, ALU.mult).then_inc(normed, 1)
            s.done(nc.vector.tensor_scalar(tile_e[:], tile_e[:], -float(E), None, ALU.add))
            s.done(tt(passed[:], over_experts(tile_e[:], NT), e_less_8[:].unsqueeze(1).to_broadcast([P, NT, E]),
                      ALU.is_equal))
            s.done(tt(b1big[:], passed[:].unsqueeze(2).to_broadcast([P, NT, 2 * HC, E]),
                      b1T[:].rearrange("p e c -> p c e").unsqueeze(1).to_broadcast([P, NT, 2 * HC, E]), ALU.mult))
            then(dve, reduce(b1s[:], b1big[:], axis=X, op=ALU.add), h_done, 1)
            nc.vector.memset(cmp[:, 0, 0:1], 0.0).then_inc(y_done, 1)
            nc.vector.memset(cmp[:, 0, 1:2], 0.0).then_inc(h_done, HB - 1)
            for i in range(2):
                nc.vector.memset(cmp[:, 0, 2 + i:3 + i], 0.0).then_inc(y_stored[i], 16)

            def tile(t, par, turn):
                for c in range(HC):
                    item = t * HC + c
                    dve.wait_ge(sig_done, item + 1)
                    then(dve, nc.vector.scalar_tensor_tensor(
                        gated[:, c % 2, :], psH[:, c % HB, 0, :],
                        b1s[:, bass.ds(t, 1), c], sig[:, c % 2, :], ALU.add, ALU.mult), h_done, item + HB + 1)
                dve.wait_ge(y_full, t + 1)
                dve.wait_ge(w_in[par], (turn + 1) * 48)
                dve.wait_ge(y_stored[par], turn * 16 + 16)
                then(dve, tt(ys[:, par], psY[:, :, 0:C], b2s[:, par:par + 1, :].to_broadcast([P, 2, C]), ALU.add),
                     y_done, t + 2)

            tiles(dve, tile)
            for t in range(TT):
                dve.wait_ge(gathered[t % SLOTS], 16 * (t // SLOTS + 1))
                tt(slots[:, t % SLOTS, :], slots[:, t % SLOTS, :], x2[:, t // 2, t % 2, :], ALU.add).then_inc(summed, 1)

        @block.scalar
        def _(act):
            def tile(t, par, turn):
                act.wait_ge(t_full, t + 1)
                then(act, nc.scalar.activation(xsT[:], psT[:], ACT.Copy), t_done, t + 1)
                for c in range(HC):
                    item = t * HC + c
                    act.wait_ge(h_full, item + 1)
                    act.wait_ge(h_done, item + HB - 1)
                    then(act, nc.scalar.activation(sig[:, c % 2, :], psH[:, c % HB, 1, :], ACT.Sigmoid,
                                                   bias=b1s[:, bass.ds(t, 1), HC + c]), sig_done, item + 1)

            act.wait_ge(h_done, HB)
            tiles(act, tile)

        @block.tensor
        def _(pe):
            mm = nc.tensor.matmul
            pe.wait_ge(onehot_ready, 1)
            oh = onehotb[:].rearrange("p t e -> p (t e)")
            mm(psR[:, 0].rearrange("p t e -> p (t e)"), upper[:], oh, start=True, stop=True)
            mm(psR[:, 1].rearrange("p t e -> p (t e)"), ones[:], oh, start=True, stop=True).then_inc(counted, 1)

            def turn_tokens(t, par, turn):
                pe.wait_ge(xs_in[par], (turn + 1) * 16)
                for c in range(KC):
                    for half in range(2):
                        ins = nc.tensor.transpose(psT[:, c, half * P:(half + 1) * P],
                                                  xs[:, par, half, c * P:(c + 1) * P], ident[:])
                ins.then_inc(t_full, 1)

            def down(t, par, c):
                pe.wait_ge(h_done, t * HC + c + HB + 1)
                if c == 0:
                    pe.wait_ge(y_done, t + 1)
                for half in range(2):
                    ins = mm(psY[:, half, 0:C], gated[:, c % 2, half * P:(half + 1) * P], w2s[par][:, c, :],
                             start=c == 0, stop=c == HC - 1)
                if c == HC - 1:
                    ins.then_inc(y_full, 1)

            def tile(t, par, turn):
                pe.wait_ge(w_in[par], (turn + 1) * 48)
                pe.wait_ge(t_done, t + 1)
                for c in range(HC):
                    pe.wait_ge(h_done, t * HC + c + 1)
                    for part in range(2):
                        w = part * HID + c * P
                        for k in range(KC):
                            ins = mm(psH[:, c % HB, part, :], w1s[par][:, k, w:w + P], xsT[:, k, :],
                                     start=k == 0, stop=k == KC - 1)
                    ins.then_inc(h_full, 1)
                    if c >= 1:
                        if c == HC - 1 and not (isinstance(t, int) and t == NT - 1):
                            turn_tokens(t + 1, 1 - par, turn + par)
                        down(t, par, c - 1)
                down(t, par, HC - 1)

            turn_tokens(0, 0, 0)
            tiles(pe, tile)


_NAMES = ["x", "ctx_768", "L0_attn_w_qkv", "L0_attn_b_qkv", "L0_attn_w_proj", "L0_attn_b_proj", "L0_attn_bias_table",
          "L0_xattn_Wq", "L0_xattn_Wk", "L0_xattn_Wv", "L0_xattn_Wo", "L0_xattn_bo", "L0_ffn_router_w",
          "L0_ffn_router_b", "L0_ffn_w1", "L0_ffn_b1", "L0_ffn_w2", "L0_ffn_b2"]


def kernel(**inputs):
    import numpy as np
    import concourse.bacc as bacc
    from concourse.bass_utils import run_bass_kernel_spmd

    nc = bacc.Bacc("TRN2", target_bir_lowering=False, num_devices=1)
    arrays = {f"in_{k}": np.ascontiguousarray(inputs[k]) for k in _NAMES}
    args = [nc.dram_tensor(k, a.shape, mybir.dt.from_np(a.dtype), kind="ExternalInput").ap() for k, a in arrays.items()]
    out = nc.dram_tensor("out", (B, N, C), F32, kind="ExternalOutput").ap()
    decoder_layer(nc, *args, out)
    return run_bass_kernel_spmd(nc, [arrays], core_ids=[0]).results[0]["out"]
```

```python
from contextlib import ExitStack

import concourse.bass as bass
from concourse import mybir

F32 = mybir.dt.float32
F32R = mybir.dt.float32r
BF16 = mybir.dt.bfloat16
I32 = mybir.dt.int32
U32 = mybir.dt.uint32
ALU = mybir.AluOpType
ACT = mybir.ActivationFunctionType
X = mybir.AxisListType.X

P = 128
B, N, C = 16, 256, 256
KC = C // P
WS, SHIFT = 8, 4
H, D1 = 16, 16
D2 = 64
INNER = H * D2
CH = INNER // P
CTX, CTXD = 77, 192
GB = 4
NG = B // GB
BLK = N // WS
E, HID = 8, 1024
HC = HID // P
ET = 256
NT = B * N // ET + E - 1
TT = B * N // P
SCATTERED = 2 * 16
REGION = B * N + ET
EPS = 1e-5

A_ORDER = ([f"Q{n}" for n in range(4)] + ["NM", "S0", "S1", "S2", "S3", "S4", "S5", "O0", "S6", "S7"]
           + ["O1", "O2", "CTX'", "O3", "K0'", "K1'", "XN3", "XN2'"])
D_ORDER = [f"MAX{n}" for n in range(8)] + [f"PV{v}" for v in range(8)] + ["X2", "PROJ'", "V0'", "LOG", "V1'", "RANK"]
A_FIRST = ["CTX'", "K0'", "K1'", "XN2'"]
D_FIRST = ["V0'", "V1'", "PROJ'"]
A_BANKS, D_BANKS = 4, 2
assert GB * len(A_ORDER) % A_BANKS == 0 and GB * len(D_ORDER) % D_BANKS == 0
WA_ITEMS, WD_ITEMS = 8, 12
TMP_ITEMS = 2 * WS
POOL_STEPS, VEC_STEPS = 9, 105
QKV_PARTS = {v: [(k // 3, k % 3) for k in ks] for v, ks in
             {2: [0], 3: [1, 2], 4: [3, 4], 5: [5, 6], 6: [7, 8], 7: [9, 10, 11]}.items()}
POOL_FIRST = (1, 3, 5, 7)


def at(order, first, banks, name, j, b):
    if isinstance(j, int) and j < 0:
        return first.index(name), first.index(name) % banks
    k = len(first) + order.index(name)
    return j * len(order) + k, (b * len(order) + k) % banks


class Steps:

    def __init__(self, eng, sem):
        self.eng, self.sem, self.before, self.per_turn, self.turn, self.n = eng, sem, 0, 0, 0, 0

    def loop(self, turn, per_turn):
        self.before, self.n, self.turn, self.per_turn = self.before + self.n, 0, turn, per_turn

    def after_loop(self, turns):
        self.before, self.turn, self.per_turn = self.before + turns * self.per_turn, 0, 0

    def turned(self):
        assert self.n == self.per_turn, f"{self.sem}: {self.n} steps in a turn"
        self.n = 0

    def done(self, ins):
        ins.then_inc(self.sem, 1)
        self.n += 1
        self.eng.wait_ge(self.sem, self.turn * self.per_turn + (self.before + self.n))


def then(eng, ins, sem, value):
    ins.then_inc(sem, 1)
    eng.wait_ge(sem, value)


def decoder_layer(nc, x, ctx_768, w_qkv, b_qkv, w_proj, b_proj, bias_table, Wq, Wk, Wv, Wo, bo,
                  router_w, router_b, w1, b1, w2, b2, out):
    sorted_x = nc.dram_tensor("sorted_x", (E * REGION, C), F32, kind="Internal").ap()
    sorted_y = nc.dram_tensor("sorted_y", (NT * ET, C), F32, kind="Internal").ap()

    def half_of(ap, j, half):
        rows = ap[bass.ds(j, 1)].rearrange("a (k r) c -> r (a k) c", r=WS)
        return rows[SHIFT:WS] if half == 0 else rows[0:SHIFT]

    with ExitStack() as whole:
        def keep(name, shape, dt=F32):
            return whole.enter_context(nc.sbuf_tensor(name, shape, dt))

        ident = keep("ident", [P, P])
        identb = keep("identb", [P, P], BF16)
        x2 = keep("x2", [P, B, 2, C])
        first = keep("first", [P, B, 2])
        place = keep("place", [P, B, 2])
        counts = keep("counts", [P, E])
        e_less_8 = keep("e_less_8", [P, E])
        b1T = keep("b1T", [P, E, 2 * HC])

        scattered = whole.enter_context(nc.semaphore("scattered"))
        trunk(nc, x, ctx_768, w_qkv, b_qkv, w_proj, b_proj, bias_table, Wq, Wk, Wv, Wo, bo, router_w, router_b, b1,
              half_of, sorted_x, scattered, ident, identb, x2, first, place, counts, e_less_8, b1T)
        experts(nc, w1, w2, b2, out, half_of, sorted_x, sorted_y, scattered, ident, x2, first, place, counts,
                e_less_8, b1T)


def trunk(nc, x, ctx_768, w_qkv, b_qkv, w_proj, b_proj, bias_table, Wq, Wk, Wv, Wo, bo, router_w, router_b, b1,
          half_of, sorted_x, scattered, ident, identb, x2, first, place, counts, e_less_8, b1T):
    x_flat = x.rearrange("b n c -> b (n c)")
    with ExitStack() as st:
        def sb(name, shape, dt=F32):
            return st.enter_context(nc.sbuf_tensor(name, shape, dt))

        def sem(name):
            return st.enter_context(nc.semaphore(name))

        psA = st.enter_context(nc.psum_tensor("psA", [P, A_BANKS, 512], F32))
        psD = st.enter_context(nc.psum_tensor("psD", [P, D_BANKS, 512], F32))
        psW = st.enter_context(nc.psum_tensor("psW", [P, 2, 512], F32))

        wqkv = sb("wqkv", [P, KC, 3 * C])
        wproj = sb("wproj", [P, KC, C])
        wq = sb("wq", [P, KC, INNER])
        wk = sb("wk", [P, KC, INNER])
        wv = sb("wv", [P, KC, INNER])
        wo = sb("wo", [P, CH, C])
        rw = sb("rw", [P, KC, E])
        bqkv_b = sb("bqkv_b", [P, 3 * C])
        bproj_b = sb("bproj_b", [P, C])
        bo_b = sb("bo_b", [P, C])
        rb_b = sb("rb_b", [P, E])
        relbias = sb("relbias", [P, WS, WS * H])
        head_row = sb("head_row", [P, H, CTX], BF16)
        half_exp = sb("half_exp", [P, WS])
        eps = sb("eps", [P, WS])

        xw = sb("xw", [P, WS, C])
        tmp1 = sb("tmp1", [P, WS, C])
        products = [xw, tmp1]
        idle = sb("idle", [P, 1])
        idle2 = sb("idle2", [P, 1])
        st1 = sb("st1", [P, WS, 6])
        mv1 = sb("mv1", [P, WS, 2])
        ve1 = sb("ve1", [P, WS])
        rs1 = sb("rs1", [P, WS])
        xnT = sb("xnT", [P, KC, WS, P])
        qkv = sb("qkv", [P, WS, 3 * C])
        probs = sb("probs", [P, WS, WS * H])
        red = sb("red", [P, WS * H])
        oT = sb("oT", [P, KC, GB, WS, BLK])

        xb = sb("xb", [P, 2, 2, C])
        ctx = sb("ctx", [P, 2, CTXD])
        x1 = sb("x1", [P, 2, C])
        xn = sb("xn", [P, 2, C])
        st2 = sb("st2", [P, 2, 2, 6])
        mv2 = sb("mv2", [P, 2, 2, 2])
        ve2 = sb("ve2", [P, 2, 2])
        rs2 = sb("rs2", [P, 2, 2])
        xT = sb("xT", [P, KC, 2 * P])
        ctxT = sb("ctxT", [P, KC, P])
        qT = sb("qT", [P, CH, 2 * P])
        qTb = sb("qTb", [P, CH, 2 * P], BF16)
        kT = sb("kT", [P, CH, 2, CTX])
        kTb = sb("kTb", [P, CH, 2, CTX], BF16)
        vo = sb("vo", [P, H, 2 * D2])
        nm = sb("nm", [P, 2, H], BF16)
        nmT = sb("nmT", [P, 2 * P], BF16)
        pT = sb("pT", [P, 4, 2 * N])
        rden = sb("rden", [P, 4])
        o2 = sb("o2", [P, 2, 2, 4 * D2])
        xn3 = o2[:, 0]
        b1rows = o2[:, 0, 0, 0:P]
        o2T = sb("o2T", [P, CH, N])

        upper = sb("upper", [P, P], BF16)
        ones = sb("ones", [P, P], BF16)
        region_row = sb("region_row", [P, E])
        lg = sb("lg", [P, 2, E])
        best = sb("best", [P, 2])
        cand = sb("cand", [P, 2, E])
        onehot = sb("onehot", [P, 2, E])
        onehotb = sb("onehotb", [P, 2, E], BF16)
        rank = sb("rank", [P, 2, E])
        row = sb("row", [P, 2])
        rowi = sb("rowi", [P, 2], U32)

        weights = sem("weights")
        onehot_ready, routed = sem("onehot_ready"), sem("routed")
        pool_step, act_step, vec_step = sem("pool_step"), sem("act_step"), sem("vec_step")
        constants = sem("constants")
        xw_in = sem("xw_in")
        tile_in = [sem("tile_in0"), sem("tile_in1")]
        a_full, a_done = sem("a_full"), sem("a_done")
        d_full, d_done = sem("d_full"), sem("d_done")
        wa_full, wa_done = sem("wa_full"), sem("wa_done")
        wd_full, wd_done = sem("wd_full"), sem("wd_done")
        var1, rstd1, normed1 = sem("var1"), sem("rstd1"), sem("normed1")
        product, consumed = sem("product"), sem("consumed")
        shifted, exped, probs_ready = sem("shifted"), sem("exped"), sem("probs_ready")
        xb_biased, x1_biased = sem("xb_biased"), sem("x1_biased")
        var2, rstd2, normed2 = sem("var2"), sem("rstd2"), sem("normed2")
        var3, rstd3, normed3 = sem("var3"), sem("rstd3"), sem("normed3")
        b1_in, b1_turned, b1_kept = sem("b1_in"), sem("b1_turned"), sem("b1_kept")
        qkv_weights = sem("qkv_weights")
        N_WEIGHTS = 11 + WS

        block = st.enter_context(nc.Block())

        def A(name, j, b):
            return at(A_ORDER, A_FIRST, A_BANKS, name, j, b)

        def Dd(name, j, b):
            return at(D_ORDER, D_FIRST, D_BANKS, name, j, b)

        def product_count(n, i):
            if isinstance(n, int) and n == 0:
                return (i // WS) * len(POOL_FIRST) + POOL_FIRST.index(i % WS) + 1
            return (n - 1) * TMP_ITEMS + (2 * len(POOL_FIRST) + i + 1)

        def make_product(eng, tensor_tensor, n, i, query, probabilities, done):
            item = n * TMP_ITEMS + i
            eng.wait_ge(consumed, item + 1)
            if probabilities:
                a = qkv[:, :, 2 * C:3 * C].rearrange("p k (h d) -> p k h d", h=H)
                w = probs[:, :, query * H:(query + 1) * H].unsqueeze(3).to_broadcast([P, WS, H, D1])
                o = products[i % 2][:].rearrange("p k (h d) -> p k h d", h=H)
            else:
                a = qkv[:, :, C:2 * C]
                w = qkv[:, query:query + 1, 0:C].to_broadcast([P, WS, C])
                o = products[i % 2][:]
            done(tensor_tensor(o, a, w, ALU.mult))

        @block.sync
        def _(sp):
            def load_windows(n):
                for i in range(GB):
                    rows = x_flat[bass.ds(n * GB + i, 1), SHIFT * C:SHIFT * C + (BLK - 1) * WS * C]
                    sp.dma_start(xw[i * BLK:(i + 1) * BLK - 1, :, :],
                                 rows.rearrange("a (w f) -> (a w) f", f=WS * C)).then_inc(xw_in, 16)
                seqs = x_flat[bass.ds(n * GB, GB)]
                sp.dma_start(xw[BLK - 1::BLK, 0:SHIFT, :], seqs[:, (N - SHIFT) * C:N * C]).then_inc(xw_in, 16)
                sp.dma_start(xw[BLK - 1::BLK, SHIFT:WS, :], seqs[:, 0:SHIFT * C]).then_inc(xw_in, 16)

            def load_tiles(j, b):
                for half in range(2):
                    sp.dma_start(xb[:, b % 2, half, :], half_of(x, j, half)).then_inc(tile_in[b % 2], 16)
                sp.dma_start(ctx[0:CTX, b % 2, :], ctx_768[bass.ds(j, 1)].rearrange("a k c -> (a k) c"))\
                    .then_inc(tile_in[b % 2], 16)

            load_windows(0)
            sp.dma_start(wqkv[:], w_qkv.rearrange("(k p) n -> p k n", p=P)).then_inc(qkv_weights, 16)
            sp.dma_start(bqkv_b[:], b_qkv.partition_broadcast(P)).then_inc(qkv_weights, 16)
            sp.dma_start(b1rows, b1.rearrange("e (c p) -> (e c) p", p=P)).then_inc(b1_in, 16)
            for key in range(WS):
                row = 7 * (2 * WS - 1) + (WS - 1) - key
                sp.dma_start(relbias[:, key, :], bias_table[row:row + WS, :].rearrange("a h -> (a h)")
                             .partition_broadcast(P)).then_inc(weights, 16)
            sp.dma_start(wproj[:], w_proj.rearrange("(k p) n -> p k n", p=P)).then_inc(weights, 16)
            sp.dma_start(bproj_b[:], b_proj.partition_broadcast(P)).then_inc(weights, 16)
            load_tiles(0, 0)
            load_tiles(1, 1)
            sp.dma_start(wk[:, 0, :], Wk[0:P, :]).then_inc(weights, 16)
            sp.dma_start(wk[0:CTXD - P, 1, :], Wk[P:CTXD, :]).then_inc(weights, 16)
            sp.dma_start(wv[:, 0, :], Wv[0:P, :]).then_inc(weights, 16)
            sp.dma_start(wv[0:CTXD - P, 1, :], Wv[P:CTXD, :]).then_inc(weights, 16)
            sp.dma_start(wq[:], Wq.rearrange("(k p) n -> p k n", p=P)).then_inc(weights, 16)
            sp.dma_start(wo[:], Wo.rearrange("(k p) n -> p k n", p=P)).then_inc(weights, 16)
            sp.dma_start(bo_b[:], bo.partition_broadcast(P)).then_inc(weights, 16)
            sp.dma_start(rw[:], router_w.rearrange("(k p) n -> p k n", p=P)).then_inc(weights, 16)
            sp.dma_start(rb_b[:], router_b.partition_broadcast(P)).then_inc(weights, 16)
            def turn(g, more):
                if more:
                    sp.wait_ge(consumed, 2 + TMP_ITEMS * (g + 1))
                    load_windows(g + 1)
                for b in range(GB):
                    if not more and b >= GB - 2:
                        continue
                    j = g * GB + b
                    sp.wait_ge(a_full, A("Q0", j, b)[0] + 1)
                    load_tiles(j + 2, b)

            with sp.Fori(0, NG - 1) as g:
                turn(g, True)
            turn(NG - 1, False)

        @block.gpsimd
        def _(pool):
            s = Steps(pool, pool_step)

            def rstd(variance, ve, rs, k, ready, signal, value):
                pool.wait_ge(ready, value)
                s.done(nc.gpsimd.tensor_tensor(ve, variance, eps[:, 0:k], ALU.add))
                then(pool, nc.gpsimd.tensor_tensor(rs, ve, half_exp[:, 0:k], ALU.pow), signal, value)

            def rstd1_of(n):
                rstd(mv1[:, :, 1], ve1[:], rs1[:], WS, var1, rstd1, n + 1)

            s.done(nc.gpsimd.memset(ident[:], 0.0))
            s.done(nc.gpsimd.memset(identb[:], 0.0))
            for m in (ident, identb):
                nc.gpsimd.affine_select(out=m[:], in_=m[:], compare_op=ALU.not_equal, fill=1.0, base=0,
                                        pattern=[[-1, P]], channel_multiplier=1).then_inc(constants, 1)
            s.done(nc.gpsimd.memset(half_exp[:], -0.5))
            s.done(nc.gpsimd.memset(eps[:], EPS))
            s.done(nc.gpsimd.memset(head_row[:], 0.0))
            s.done(nc.gpsimd.affine_select(out=head_row[:], in_=head_row[:], compare_op=ALU.not_equal, fill=1.0,
                                           base=0, pattern=[[-1, H], [0, CTX]], channel_multiplier=1))
            s.done(nc.gpsimd.memset(ctxT[:], 0.0))
            s.done(nc.gpsimd.memset(wk[CTXD - P:P, 1, :], 0.0))
            s.done(nc.gpsimd.memset(wv[CTXD - P:P, 1, :], 0.0))
            rstd1_of(0)
            s.done(nc.gpsimd.memset(kT[:], 0.0))
            s.done(nc.gpsimd.memset(kTb[:], 0.0))
            s.done(nc.gpsimd.memset(nmT[:], 0.0))
            s.done(nc.gpsimd.memset(pT[:], 0.0))
            s.done(nc.gpsimd.memset(upper[:], 1.0))
            s.done(nc.gpsimd.affine_select(out=upper[:], in_=upper[:], compare_op=ALU.is_gt, fill=0.0, base=0,
                                           pattern=[[1, P]], channel_multiplier=-1))
            s.done(nc.gpsimd.memset(ones[:], 1.0))
            for dst, step, first_value in ((e_less_8, 1, -E), (region_row, REGION, 0)):
                s.done(nc.gpsimd.iota(dst[:], pattern=[[step, E]], base=first_value, channel_multiplier=0,
                                      allow_small_or_imprecise_dtypes=True))
            s.done(nc.gpsimd.memset(counts[:], 0.0))
            for i in range(2):
                nc.gpsimd.dma_start(lg[0:1, i, :], router_b.unsqueeze(0)).then_inc(scattered, 16)
            nc.gpsimd.memset(vo[:], 1.0).then_inc(constants, 1)
            pool.wait_ge(constants, 3)

            def product_of(n, i, query, probabilities):
                make_product(pool, nc.gpsimd.tensor_tensor, n, i, query, probabilities,
                             lambda ins: then(pool, ins, product, product_count(n, i)))

            def add_projection_bias(j, b, loads):
                pool.wait_ge(tile_in[b % 2], loads)
                then(pool, nc.gpsimd.tensor_tensor(xb[:, b % 2], xb[:, b % 2],
                                                   bproj_b[:].unsqueeze(1).to_broadcast([P, 2, C]), ALU.add),
                     xb_biased, j + 1)

            def norm2(j):
                rstd(mv2[:, 0, :, 1], ve2[:, 0], rs2[:, 0], 2, var2, rstd2, j + 1)

            def norm3(j):
                rstd(mv2[:, 1, :, 1], ve2[:, 1], rs2[:, 1], 2, var3, rstd3, j + 1)

            def bias_x1(j):
                pool.wait_ge(normed2, j + 1)
                then(pool, nc.gpsimd.tensor_tensor(x1[:], x1[:], bo_b[:].unsqueeze(1).to_broadcast([P, 2, C]),
                                                   ALU.add), x1_biased, j + 1)

            pool.wait_ge(weights, 16 * N_WEIGHTS)
            pool.wait_ge(wd_done, 1 + WD_ITEMS)
            for i in POOL_FIRST:
                product_of(0, i, i, False)
            pool.wait_ge(probs_ready, 1)
            for i in POOL_FIRST:
                product_of(0, WS + i, i, True)
            add_projection_bias(0, 0, 48)
            norm2(0)

            def turn(g, more):
                n = g + 1
                for b in range(GB):
                    j = g * GB + b
                    last = not more and b == GB - 1
                    bias_x1(j)
                    if not last:
                        add_projection_bias(j + 1, b + 1, (g * 2 + (b + 1) // 2 + 1) * 48)
                    if more and b == 0:
                        rstd1_of(n)
                    if more and b == 1:
                        for i in range(1, 6):
                            product_of(n, i, i, False)
                    if more and b == 2:
                        for i in range(7, WS):
                            product_of(n, i, i, False)
                        pool.wait_ge(probs_ready, n + 1)
                        for i in range(2):
                            product_of(n, WS + i, i, True)
                    if more and b == 3:
                        for i in range(2, WS):
                            product_of(n, WS + i, i, True)
                    norm3(j)
                    if not last:
                        norm2(j + 1)
                    if more and b == 0:
                        pool.wait_ge(wd_done, 1 + WD_ITEMS * (n + 1))
                        product_of(n, 0, 0, False)
                    if more and b == 1:
                        product_of(n, 6, 6, False)
                    pool.wait_ge(routed, j + 1)
                    nc.gpsimd.tensor_tensor(idle2[:], eps[:, 0:1], eps[:, 0:1], ALU.add)
                    for half in range(2):
                        nc.gpsimd.indirect_dma_start(
                            out=sorted_x[:, :], out_offset=bass.IndirectOffsetOnAxis(ap=rowi[:, half:half + 1], axis=0),
                            in_=xn3[:, half, :], in_offset=None).then_inc(scattered, 16)

            with pool.Fori(0, NG - 1) as g:
                s.loop(g, POOL_STEPS)
                turn(g, True)
                s.turned()
            s.after_loop(NG - 1)
            turn(NG - 1, False)

        @block.scalar
        def _(act):
            copy = ACT.Copy
            act.wait_ge(constants, 2)
            then(act, nc.scalar.activation(rden[:, 0:1], ident[:, 0:1], copy), act_step, 1)
            nc.scalar.activation(rden[:, 1:2], ident[:, 0:1], copy).then_inc(a_done, A_BANKS)
            nc.scalar.activation(rden[:, 2:3], ident[:, 0:1], copy).then_inc(wa_done, 2)

            def window_turned(n, k):
                item = n * WA_ITEMS + k
                act.wait_ge(wa_full, item + 1)
                src = psW[:, k % 2, :]
                then(act, nc.scalar.activation(
                    xnT[:, :, 2 * k:2 * k + 2, :].rearrange("p k i w -> p i k w"),
                    src.rearrange("p (i k w) -> p i k w", i=2, k=KC), copy), wa_done, item + 3)

            def output_turned(n, k):
                item = n * WA_ITEMS + 4 + k
                act.wait_ge(wa_full, item + 1)
                ps = psW[:, k % 2, :].rearrange("p (i k w) -> p i k w", i=2, k=KC)
                for i in range(2):
                    dst = oT[:, :, :, 2 * k + i, :]
                    src = ps[:, i].rearrange("p k (b w) -> p k b w", b=GB)
                    if 2 * k < SHIFT:
                        last = nc.scalar.activation(dst, src, copy)
                    else:
                        nc.scalar.activation(dst[:, :, :, 1:BLK], src[:, :, :, 0:BLK - 1], copy)
                        last = nc.scalar.activation(dst[:, :, :, 0:1], src[:, :, :, BLK - 1:BLK], copy)
                then(act, last, wa_done, item + 3)

            def full(name, j, b):
                item, bank = A(name, j, b)
                act.wait_ge(a_full, item + 1)
                return psA[:, bank, :], item + A_BANKS + 1

            def normed_turned(name, j, b):
                ps, value = full(name, j, b)
                then(act, nc.scalar.activation(xT[:].rearrange("p k n -> p (k n)"), ps, copy), a_done, value)

            def turn_context(j, b):
                ps, value = full("CTX'", j, b)
                nc.scalar.activation(ctxT[:, 0, 0:CTX], ps[:, 0:CTX], copy)
                then(act, nc.scalar.activation(ctxT[0:CTXD - P, 1, 0:CTX], ps[0:CTXD - P, P:P + CTX], copy), a_done, value)

            def keys(half, j, b):
                ps, value = full(f"K{half}'", j, b)
                ps = ps.rearrange("p (u k) -> p u k", u=4)
                us = slice(4 * half, 4 * half + 4)
                for parity in range(2):
                    rows = slice(parity * D2, (parity + 1) * D2)
                    nc.scalar.activation(kT[rows, us, parity, :], ps[rows, :, 0:CTX], copy)
                    last = nc.scalar.activation(kTb[rows, us, parity, :], ps[rows, :, 0:CTX], copy)
                then(act, last, a_done, value)

            def output2_turned(m, j, b):
                ps, value = full(f"O{m}" if m != "CTX'" else m, j, b)
                m = 3 if m == "CTX'" else m
                then(act, nc.scalar.activation(o2T[:, 2 * m:2 * m + 2, :].rearrange("p u n -> p (u n)"), ps, copy),
                     a_done, value)

            for k in range(4):
                window_turned(0, k)
            act.wait_ge(b1_turned, 1)
            nc.scalar.activation(b1T[:].rearrange("p e c -> p (e c)"), psA[:, 0, 0:P], copy).then_inc(b1_kept, 1)
            act.wait_ge(constants, 3)
            turn_context(-1, -1)
            keys(0, -1, -1)
            keys(1, -1, -1)
            act.wait_ge(shifted, 1)
            then(act, nc.scalar.activation(probs[:], probs[:], ACT.Exp), exped, 1)
            for k in range(4):
                output_turned(0, k)
            normed_turned("XN2'", -1, -1)

            def turn(g, more):
                n = g + 1
                for b in range(GB):
                    j = g * GB + b
                    for q in range(4):
                        ps, value = full(f"Q{q}", j, b)
                        nc.scalar.activation(qTb[:, 2 * q:2 * q + 2, :].rearrange("p u n -> p (u n)"), ps, copy)
                        then(act, nc.scalar.activation(qT[:, 2 * q:2 * q + 2, :].rearrange("p u n -> p (u n)"), ps, copy),
                             a_done, value)
                    ps, value = full("NM", j, b)
                    then(act, nc.scalar.activation(nmT[0:H, :], ps[0:H, 0:P].bitcast(BF16), copy), a_done, value)
                    for u in range(CH):
                        ps, value = full(f"S{u}", j, b)
                        then(act, nc.scalar.activation(pT[0:CTX, u % 4, :], ps[0:CTX, :], ACT.Exp, scale=D2 ** -0.5),
                             a_done, value)
                        if more and b == 2 and u == 3:
                            act.wait_ge(shifted, n + 1)
                            then(act, nc.scalar.activation(probs[:], probs[:], ACT.Exp), exped, n + 1)
                        if more and b == 0 and u in (3, 5):
                            window_turned(n, u - 3)
                            window_turned(n, u - 2)
                        if u == 5:
                            output2_turned(0, j, b)
                    last = not more and b == GB - 1
                    for k in range(4):
                        if more and b == 3:
                            output_turned(n, k)
                        if k in (0, 2):
                            output2_turned(1 + k // 2, j, b)
                    if not last:
                        turn_context(j, b)
                        output2_turned(3, j, b)
                        keys(0, j, b)
                        keys(1, j, b)
                        normed_turned("XN3", j, b)
                        normed_turned("XN2'", j, b)
                    else:
                        output2_turned("CTX'", j, b)
                        normed_turned("O3", j, b)

            with act.Fori(0, NG - 1) as g:
                turn(g, True)
            turn(NG - 1, False)

        @block.vector
        def _(dve):
            s = Steps(dve, vec_step)
            nc.vector.memset(red[:, 0:1], 0.0).then_inc(d_done, D_BANKS)
            nc.vector.memset(red[:, 1:2], 0.0).then_inc(wd_done, 1)
            nc.vector.memset(red[:, 2:3], 0.0).then_inc(consumed, 2)
            dve.wait_ge(consumed, 2)

            def carry_waits():
                nc.vector.memset(idle[:], 0.0)

            def norm1_stats(n):
                dve.wait_ge(xw_in, (n + 1) * 16 * (GB + 2))
                for i in range(WS):
                    ins = nc.vector.bn_stats(st1[:, i, :], xw[:, i, :])
                s.done(ins)
                carry_waits()
                for i in range(WS):
                    ins = nc.vector.bn_aggr(mv1[:, i, :], st1[:, i, :])
                then(dve, ins, var1, n + 1)

            def norm1(n):
                dve.wait_ge(rstd1, n + 1)
                for i in range(WS):
                    ins = nc.vector.tensor_scalar(xw[:, i, :], xw[:, i, :], mv1[:, i, 0:1], rs1[:, i:i + 1],
                                                  ALU.subtract, ALU.mult)
                    if i % 2:
                        then(dve, ins, normed1, n * 4 + i // 2 + 1)

            def window_qkv(n, pair, part):
                item = n * WD_ITEMS + 3 * pair + part
                dve.wait_ge(wd_full, item + 1)
                ps = psW[:, (3 * pair + part) % 2, :]
                if part < 2:
                    ins = nc.vector.tensor_tensor(qkv[:, 2 * pair + part, 0:2 * C], ps, bqkv_b[:, 0:2 * C], ALU.add)
                else:
                    ins = nc.vector.tensor_tensor(qkv[:, 2 * pair:2 * pair + 2, 2 * C:3 * C],
                                                  ps.rearrange("p (i c) -> p i c", i=2),
                                                  bqkv_b[:, 2 * C:3 * C].unsqueeze(1).to_broadcast([P, 2, C]), ALU.add)
                then(dve, ins, wd_done, item + 2)

            def sum_scores(n, i):
                item = n * TMP_ITEMS + i
                if not isinstance(n, int) or i in POOL_FIRST:
                    dve.wait_ge(product, product_count(n, i))
                then(dve, nc.vector.tensor_reduce(probs[:, :, i * H:(i + 1) * H],
                                                  products[i % 2][:].rearrange("p k (h d) -> p k h d", h=H),
                                                  axis=X, op=ALU.add), consumed, item + 3)

            by_key = probs[:].rearrange("p k m -> p m k")

            def window_shift(n):
                s.done(nc.vector.scalar_tensor_tensor(probs[:], probs[:], D1 ** -0.5, relbias[:], ALU.mult, ALU.add))
                s.done(nc.vector.tensor_reduce(red[:], by_key, axis=X, op=ALU.max))
                then(dve, nc.vector.tensor_tensor(probs[:], probs[:],
                                                  red[:].unsqueeze(1).to_broadcast([P, WS, WS * H]), ALU.subtract), shifted, n + 1)

            def window_divide(n):
                dve.wait_ge(exped, n + 1)
                s.done(nc.vector.tensor_reduce(red[:], by_key, axis=X, op=ALU.add))
                s.done(nc.vector.reciprocal(red[:], red[:]))
                then(dve, nc.vector.tensor_tensor(probs[:], probs[:], red[:].unsqueeze(1).to_broadcast([P, WS, WS * H]),
                                                  ALU.mult), probs_ready, n + 1)

            def sum_values(n, i):
                item = n * TMP_ITEMS + WS + i
                t = products[i % 2]
                if not isinstance(n, int) or i in POOL_FIRST:
                    dve.wait_ge(product, product_count(n, WS + i))
                s.done(nc.vector.tensor_tensor(t[:, 0:4, :], t[:, 0:4, :], t[:, 4:8, :], ALU.add))
                s.done(nc.vector.tensor_tensor(t[:, 0:2, :], t[:, 0:2, :], t[:, 2:4, :], ALU.add))
                then(dve, nc.vector.tensor_tensor(qkv[:, i, 0:C], t[:, 0, :], t[:, 1, :], ALU.add), consumed, item + 3)

            def full(name, j, b):
                item, bank = Dd(name, j, b)
                dve.wait_ge(d_full, item + 1)
                return psD[:, bank, :], item + D_BANKS + 1

            def start_sequence(j, b):
                ps, value = full("PROJ'", j, b)
                dve.wait_ge(xb_biased, j + 2)
                then(dve, nc.vector.tensor_tensor(x1[:].rearrange("p k c -> p (k c)"), ps,
                                                  xb[:, (b + 1) % 2].rearrange("p k c -> p (k c)"), ALU.add), d_done, value)
                for half in range(2):
                    ins = nc.vector.bn_stats(st2[:, 0, half, :], x1[:, half, :])
                s.done(ins)
                carry_waits()
                for half in range(2):
                    ins = nc.vector.bn_aggr(mv2[:, 0, half, :], st2[:, 0, half, :])
                then(dve, ins, var2, j + 2)

            def keep_values(half, name, j, b):
                ps, value = full(name, j, b)
                then(dve, nc.vector.tensor_copy(vo[:, 8 * half:8 * half + 8, 0:D2],
                                                ps.rearrange("p (h d) -> p h d", h=8)), d_done, value)

            def norm2(j):
                dve.wait_ge(rstd2, j + 1)
                for half in range(2):
                    ins = nc.vector.tensor_scalar(xn[:, half, :], x1[:, half, :], mv2[:, 0, half, 0:1],
                                                  rs2[:, 0, half:half + 1], ALU.subtract, ALU.mult)
                then(dve, ins, normed2, j + 1)

            norm1_stats(0)
            norm1(0)
            dve.wait_ge(qkv_weights, 32)
            for k in range(WD_ITEMS):
                window_qkv(0, k // 3, k % 3)
            dve.wait_ge(constants, 3)
            dve.wait_ge(weights, 16 * N_WEIGHTS)
            for i in range(WS):
                if i not in POOL_FIRST:
                    make_product(dve, nc.vector.tensor_tensor, 0, i, i, False, s.done)
                sum_scores(0, i)
            window_shift(0)
            keep_values(0, "V0'", -1, -1)
            keep_values(1, "V1'", -1, -1)
            window_divide(0)
            for i in range(WS):
                if i not in POOL_FIRST:
                    make_product(dve, nc.vector.tensor_tensor, 0, WS + i, i, True, s.done)
                sum_values(0, i)
            start_sequence(-1, -1)
            norm2(0)

            def turn(g, more):
                n = g + 1
                for b in range(GB):
                    j = g * GB + b
                    if more and b == 2:
                        sum_scores(n, 5)
                    if more and b == 3:
                        sum_values(n, 0)
                        sum_values(n, 1)
                    for m in range(4):
                        for t in range(2):
                            ps, value = full(f"MAX{2 * m + t}", j, b)
                            then(dve, nc.vector.tensor_reduce(
                                nm[:, t, 4 * m:4 * m + 4], ps[:, 0:4 * CTX].rearrange("p (h k) -> p h k", h=4),
                                axis=X, op=ALU.max, negate=True), d_done, value)
                    if more and b == 0:
                        norm1_stats(n)
                    if more and b == 1:
                        sum_scores(n, 0)
                        sum_scores(n, 1)
                    if more and b == 2:
                        sum_scores(n, 6)
                        sum_scores(n, 7)
                        window_shift(n)
                    if more and b == 3:
                        sum_values(n, 2)
                        sum_values(n, 3)
                    for u in range(CH):
                        ps, value = full(f"PV{u}", j, b)
                        ps = ps.rearrange("p (h c) -> p h c", h=4)
                        if u >= 4 and u % 2 == 0:
                            dve.wait_ge(a_full, A(f"O{u // 2 - 2}", j, b)[0] + 1)
                        s.done(nc.vector.reciprocal(rden[:], ps[:, :, D2]))
                        if u == 0:
                            dve.wait_ge(scattered, j * SCATTERED + SCATTERED)
                        then(dve, nc.vector.tensor_tensor(
                            o2[:, u // 2 % 2, u % 2, :].rearrange("p (h d) -> p h d", h=4),
                            ps[:, :, 0:D2], rden[:].unsqueeze(2).to_broadcast([P, 4, D2]), ALU.mult), d_done, value)
                        if more and b == 0 and u == 0:
                            norm1(n)
                        if more and b == 0 and u >= 2:
                            for part in QKV_PARTS[u]:
                                window_qkv(n, *part)
                        if more and b == 1 and u in (1, 3, 5):
                            sum_scores(n, 2 + u // 2)
                        if more and b == 2 and u == 2:
                            window_divide(n)
                        if more and b == 3 and u in (1, 3, 4, 6):
                            sum_values(n, {1: 4, 3: 5, 4: 6, 6: 7}[u])
                    ps, value = full("X2", j, b)
                    dve.wait_ge(x1_biased, j + 1)
                    mine = x2[:, bass.ds(j, 1), :, :].rearrange("p a k c -> p (a k) c")
                    then(dve, nc.vector.tensor_tensor(mine, ps.rearrange("p (k c) -> p k c", k=2), x1[:], ALU.add),
                         d_done, value)
                    carry_waits()
                    for half in range(2):
                        ins = nc.vector.bn_stats(st2[:, 1, half, :], mine[:, half, :])
                    s.done(ins)
                    carry_waits()
                    for half in range(2):
                        ins = nc.vector.bn_aggr(mv2[:, 1, half, :], st2[:, 1, half, :])
                    then(dve, ins, var3, j + 1)
                    last = not more and b == GB - 1
                    if not last:
                        start_sequence(j, b)
                    dve.wait_ge(rstd3, j + 1)
                    for half in range(2):
                        ins = nc.vector.tensor_scalar(xn3[:, half, :], mine[:, half, :], mv2[:, 1, half, 0:1],
                                                      rs2[:, 1, half:half + 1], ALU.subtract, ALU.mult)
                    then(dve, ins, normed3, j + 1)
                    if not last:
                        norm2(j + 1)
                        keep_values(0, "V0'", j, b)
                    item, bank = Dd("PROJ'" if last else "LOG", j, b)
                    dve.wait_ge(d_full, item + 1)
                    tt, reduce = nc.vector.tensor_tensor, nc.vector.tensor_reduce
                    then(dve, tt(lg[:], psD[:, bank, 0:2 * E].rearrange("p (k e) -> p k e", k=2),
                                 rb_b[:].unsqueeze(1).to_broadcast([P, 2, E]), ALU.add), d_done, item + D_BANKS + 1)
                    over_experts = [P, 2, E]
                    mine = first[:, bass.ds(j, 1), :].rearrange("p a k -> p (a k)")
                    s.done(reduce(best[:], lg[:], axis=X, op=ALU.max))
                    s.done(tt(cand[:], lg[:], best[:].unsqueeze(2).to_broadcast(over_experts), ALU.is_equal))
                    s.done(tt(cand[:], cand[:], e_less_8[:].unsqueeze(1).to_broadcast(over_experts), ALU.mult))
                    s.done(reduce(mine, cand[:], axis=X, op=ALU.min))
                    s.done(tt(onehot[:], e_less_8[:].unsqueeze(1).to_broadcast(over_experts),
                              mine.unsqueeze(2).to_broadcast(over_experts), ALU.is_equal))
                    then(dve, nc.vector.tensor_copy(onehotb[:], onehot[:]), onehot_ready, j + 1)
                    if not last:
                        keep_values(1, "V1'", j, b)
                    item, bank = Dd("V0'" if last else "RANK", j, b)
                    dve.wait_ge(d_full, item + 1)
                    s.done(tt(rank[:], psD[:, bank, 0:2 * E].rearrange("p (k e) -> p k e", k=2),
                              counts[:].unsqueeze(1).to_broadcast(over_experts), ALU.add))
                    then(dve, tt(counts[:], counts[:], psD[:, bank, 2 * E:3 * E], ALU.add), d_done, item + D_BANKS + 1)
                    s.done(tt(cand[:], rank[:], onehot[:], ALU.mult))
                    s.done(reduce(place[:, bass.ds(j, 1), :].rearrange("p a k -> p (a k)"), cand[:], axis=X, op=ALU.add))
                    s.done(tt(rank[:], rank[:], region_row[:].unsqueeze(1).to_broadcast(over_experts), ALU.add))
                    s.done(tt(rank[:], rank[:], onehot[:], ALU.mult))
                    s.done(reduce(row[:], rank[:], axis=X, op=ALU.add))
                    then(dve, nc.vector.tensor_copy(rowi[:], row[:]), routed, j + 1)

            with dve.Fori(0, NG - 1) as g:
                s.loop(g, VEC_STEPS)
                turn(g, True)
                s.turned()
            s.after_loop(NG - 1)
            turn(NG - 1, False)

        @block.tensor
        def _(pe):
            mm = nc.tensor.matmul
            pe.wait_ge(constants, 2)

            def free(order, first, banks, done, ps, name, j, b):
                item, bank = at(order, first, banks, name, j, b)
                pe.wait_ge(done, item + 1)
                return ps[:, bank, :]

            def freeA(name, j, b):
                return free(A_ORDER, A_FIRST, A_BANKS, a_done, psA, name, j, b)

            def freeD(name, j, b):
                return free(D_ORDER, D_FIRST, D_BANKS, d_done, psD, name, j, b)

            def take_a(name, j, b):
                pe.wait_ge(a_done, A(name, j, b)[0] + A_BANKS + 1)

            def window_turn(n, k):
                pe.wait_ge(normed1, n * 4 + k + 1)
                pe.wait_ge(wa_done, n * WA_ITEMS + k + 1)
                for i in range(2):
                    for c in range(KC):
                        ins = nc.tensor.transpose(psW[:, k % 2, (i * KC + c) * P:(i * KC + c + 1) * P],
                                                  xw[:, 2 * k + i, c * P:(c + 1) * P], ident[:])
                ins.then_inc(wa_full, 1)

            def window_qkv(n, pair, part):
                k = 3 * pair + part
                if part == 0:
                    pe.wait_ge(wa_done, n * WA_ITEMS + pair + 3)
                if k < 2:
                    pe.wait_ge(wa_done, n * WA_ITEMS + k + 5)
                else:
                    pe.wait_ge(wd_done, n * WD_ITEMS + k)
                for i in ([2 * pair + part] if part < 2 else [2 * pair, 2 * pair + 1]):
                    cols = slice(0, 2 * C) if part < 2 else slice(2 * C, 3 * C)
                    dst = psW[:, k % 2, :] if part < 2 else psW[:, k % 2, (i % 2) * C:(i % 2 + 1) * C]
                    for c in range(KC):
                        ins = mm(dst, xnT[:, c, i, :], wqkv[:, c, cols], start=c == 0, stop=c == KC - 1)
                ins.then_inc(wd_full, 1)

            def output_turn(n, k):
                pe.wait_ge(consumed, 2 + n * TMP_ITEMS + WS + 2 * k + 2)
                if k < 2:
                    pe.wait_ge(wd_done, (n + 1) * WD_ITEMS + k)
                else:
                    pe.wait_ge(wa_done, n * WA_ITEMS + 4 + k + 1)
                for i in range(2):
                    for c in range(KC):
                        ins = nc.tensor.transpose(psW[:, k % 2, (i * KC + c) * P:(i * KC + c + 1) * P],
                                                  qkv[:, 2 * k + i, c * P:(c + 1) * P], ident[:])
                ins.then_inc(wa_full, 1)

            def project(j, b, group):
                q = (b + 1) % GB
                pe.wait_ge(wa_done, (group + 1) * WA_ITEMS + 2)
                ps = freeD("PROJ'", j, b)
                for half in range(2):
                    for c in range(KC):
                        ins = mm(ps[:, half * C:(half + 1) * C],
                                 oT[:, c, q, 4 * half:4 * half + 4, :].rearrange("p i w -> p (i w)"), wproj[:, c, :],
                                 start=c == 0, stop=c == KC - 1)
                ins.then_inc(d_full, 1)

            def turn_context(j, b, loads):
                ps = freeA("CTX'", j, b)
                pe.wait_ge(tile_in[(b + 1) % 2], loads)
                nc.tensor.transpose(ps[:, 0:CTX], ctx[0:CTX, (b + 1) % 2, 0:P], ident[0:CTX, 0:CTX])
                nc.tensor.transpose(ps[0:CTXD - P, P:P + CTX], ctx[0:CTX, (b + 1) % 2, P:CTXD],
                                    ident[0:CTX, 0:CTX]).then_inc(a_full, 1)

            def keys(half, j, b):
                if half == 0:
                    take_a("CTX'", j, b)
                ps = freeA(f"K{half}'", j, b)
                for u in range(4):
                    for c in range(KC):
                        ins = mm(ps[:, u * P:(u + 1) * P], wk[:, c, (4 * half + u) * P:(4 * half + u + 1) * P],
                                 ctxT[:, c, :], start=c == 0, stop=c == KC - 1)
                ins.then_inc(a_full, 1)

            def context_values(half, name, j, b):
                ps = freeD(name, j, b)
                for c in range(KC):
                    ins = mm(ps, ctxT[:, c, :], wv[:, c, half * 512:(half + 1) * 512], start=c == 0, stop=c == KC - 1)
                ins.then_inc(d_full, 1)

            def turn_normed(src, name, j, b, ready, value):
                pe.wait_ge(ready, value)
                ps = freeA(name, j, b)
                for c in range(KC):
                    for half in range(2):
                        ins = nc.tensor.transpose(ps[:, (c * 2 + half) * P:(c * 2 + half + 1) * P],
                                                  src[:, half, c * P:(c + 1) * P], ident[:])
                ins.then_inc(a_full, 1)

            for k in range(4):
                window_turn(0, k)
            pe.wait_ge(b1_in, 16)
            nc.tensor.transpose(psA[:, 0, 0:P], b1rows, ident[:]).then_inc(b1_turned, 1)
            pe.wait_ge(qkv_weights, 32)
            for k in range(WD_ITEMS):
                window_qkv(0, k // 3, k % 3)
            pe.wait_ge(b1_kept, 1)
            pe.wait_ge(constants, 3)
            pe.wait_ge(weights, 16 * N_WEIGHTS)
            turn_context(-1, -1, 48)
            keys(0, -1, -1)
            keys(1, -1, -1)
            context_values(0, "V0'", -1, -1)
            context_values(1, "V1'", -1, -1)
            for k in range(4):
                output_turn(0, k)
            project(-1, -1, 0)
            turn_normed(xn, "XN2'", -1, -1, normed2, 1)

            def turn(g, more):
                n = g + 1
                for b in range(GB):
                    j = g * GB + b
                    def queries(q):
                        if q == 0:
                            pe.wait_ge(a_done, A_BANKS + A("Q0", j, b)[0])
                        ps = freeA(f"Q{q}", j, b)
                        for u in range(2):
                            for c in range(KC):
                                ins = mm(ps[:, u * N:(u + 1) * N], wq[:, c, (2 * q + u) * P:(2 * q + u + 1) * P],
                                         xT[:, c, :], start=c == 0, stop=c == KC - 1)
                        ins.then_inc(a_full, 1)

                    def scores_for_max(m):
                        take_a(f"Q{m}", j, b)
                        for t in range(2):
                            ps = freeD(f"MAX{2 * m + t}", j, b)
                            for i in range(2):
                                u = 2 * m + i
                                ins = mm(ps[:, 2 * i * CTX:2 * (i + 1) * CTX], qTb[:, u, t * P:(t + 1) * P],
                                         kTb[:, u].rearrange("p m k -> p (m k)"), start=True, stop=True)
                            ins.then_inc(d_full, 1)

                    def score_products(u, m):
                        ps = freeA(f"S{u}", j, b)
                        mm(ps[0:CTX, m * N:(m + 1) * N], kT[:, u, m, :], qT[:, u, :], start=True, stop=False)

                    def score_shift(u, m):
                        ps = psA[:, A(f"S{u}", j, b)[1], :]
                        ins = mm(ps[0:CTX, m * N:(m + 1) * N], head_row[:, 2 * u + m, :], nmT[:], start=False, stop=True)
                        if m == 1:
                            ins.then_inc(a_full, 1)

                    def scores(u):
                        for m in range(2):
                            score_products(u, m)
                            score_shift(u, m)

                    def values(v):
                        w, t = v // 2, v % 2
                        take_a(f"S{2 * w + 1}", j, b)
                        ps = freeD(f"PV{v}", j, b)
                        for m in range(4):
                            ins = mm(ps[:, m * P:(m + 1) * P],
                                     pT[:, (2 * w + m // 2) % 4, (m % 2) * N + t * P:(m % 2) * N + (t + 1) * P],
                                     vo[:, 4 * w + m, :], start=True, stop=True)
                        ins.then_inc(d_full, 1)

                    def turn_output2(m, name=None):
                        pe.wait_ge(d_done, Dd(f"PV{2 * m + 1}", j, b)[0] + D_BANKS + 1)
                        ps = freeA(name or f"O{m}", j, b)
                        for u in range(2):
                            for t in range(2):
                                ins = nc.tensor.transpose(ps[:, (2 * u + t) * P:(2 * u + t + 1) * P],
                                                          o2[:, m % 2, t, u * P:(u + 1) * P], ident[:])
                        ins.then_inc(a_full, 1)

                    queries(0)
                    for q in range(1, 4):
                        queries(q)
                        scores_for_max(q - 1)
                    score_products(0, 0)
                    scores_for_max(3)
                    score_products(1, 0)
                    ps = freeA("NM", j, b)
                    for t in range(2):
                        pe.wait_ge(d_done, Dd(f"MAX{6 + t}", j, b)[0] + D_BANKS + 1)
                        ins = nc.tensor.transpose(ps[0:H, t * 64:(t + 1) * 64].bitcast(BF16), nm[:, t, :], identb[:])
                    ins.then_inc(a_full, 1)
                    take_a("NM", j, b)
                    for u in range(2):
                        score_shift(u, 0)
                        score_products(u, 1)
                        score_shift(u, 1)
                    scores(2)
                    scores(3)
                    for v in range(8):
                        values(v)
                        if more and b == 0 and v > 2:
                            window_qkv(n, *QKV_PARTS[v][0])
                        if more and b == 0 and v in (1, 2):
                            window_turn(n, 2 * v - 2)
                            window_turn(n, 2 * v - 1)
                        if v in (1, 3):
                            scores(v + 3)
                            scores(v + 4)
                        if more and b == 3 and v >= 4:
                            output_turn(n, v - 4)
                        if v in (2, 4, 6):
                            turn_output2(v // 2 - 1)
                        if more and b == 0 and v >= 2:
                            for part in QKV_PARTS[v][v > 2:]:
                                window_qkv(n, *part)
                    last = not more and b == GB - 1
                    if not last:
                        turn_context(j, b, (g * 2 + (b + 1) // 2 + 1) * 48)
                    turn_output2(3, "CTX'" if last else "O3")
                    ps = freeD("X2", j, b)
                    for half in range(2):
                        for u in range(CH):
                            if half == 0 and u % 2 == 0:
                                take_a("CTX'" if last and u == 6 else f"O{u // 2}", j, b)
                            ins = mm(ps[:, half * C:(half + 1) * C], o2T[:, u, half * P:(half + 1) * P], wo[:, u, :],
                                     start=u == 0, stop=u == CH - 1)
                    ins.then_inc(d_full, 1)
                    if not last:
                        project(j, b, g if b < GB - 1 else g + 1)
                        keys(0, j, b)
                        keys(1, j, b)
                    turn_normed(xn3, "O3" if last else "XN3", j, b, normed3, j + 1)
                    if not last:
                        context_values(0, "V0'", j, b)
                    take_a("O3" if last else "XN3", j, b)
                    ps = freeD("PROJ'" if last else "LOG", j, b)
                    for half in range(2):
                        for c in range(KC):
                            ins = mm(ps[:, half * E:(half + 1) * E], xT[:, c, half * P:(half + 1) * P], rw[:, c, :],
                                     start=c == 0, stop=c == KC - 1)
                    ins.then_inc(d_full, 1)
                    if not last:
                        turn_normed(xn, "XN2'", j, b, normed2, j + 2)
                        context_values(1, "V1'", j, b)
                    pe.wait_ge(onehot_ready, j + 1)
                    ps = freeD("V0'" if last else "RANK", j, b)
                    mm(ps[:, 0:E], upper[:], onehotb[:, 0], start=True, stop=True)
                    mm(ps[:, E:2 * E], upper[:], onehotb[:, 1], start=True, stop=False)
                    mm(ps[:, E:2 * E], ones[:], onehotb[:, 0], start=False, stop=True)
                    for half in range(2):
                        ins = mm(ps[:, 2 * E:3 * E], ones[:], onehotb[:, half], start=half == 0, stop=half == 1)
                    ins.then_inc(d_full, 1)

            with pe.Fori(0, NG - 1) as g:
                turn(g, True)
            turn(NG - 1, False)


def experts(nc, w1, w2, b2, out, half_of, sorted_x, sorted_y, scattered, ident, x2, first, place, counts,
            e_less_8, b1T):
    SLOTS = 8
    PAIR = 2
    PAIRS_HID = HC // PAIR
    W2_POOL = 6
    PIECES = 3
    with ExitStack() as st:
        def sb(name, shape, dt=F32):
            return st.enter_context(nc.sbuf_tensor(name, shape, dt))

        def sem(name):
            return st.enter_context(nc.semaphore(name))

        psH = st.enter_context(nc.psum_tensor("psH", [P, 2 * PAIR, 2, ET], F32))
        psY = st.enter_context(nc.psum_tensor("psY", [P, 2, 512], F32))
        psT = st.enter_context(nc.psum_tensor("psT", [P, KC, ET], F32))

        k_tiles = sb("k_tiles", [P, B * N // ET])
        tile_no = sb("tile_no", [P, NT])
        region_row = sb("region_row2", [P, E])
        tail_row = sb("tail_row", [P, E])
        tail_rowi = sb("tail_rowi", [P, E], I32)
        cmp = sb("cmp", [P, E, B * N // ET])
        ntiles = sb("ntiles", [P, E])
        ends = sb("ends", [P, 2, E])
        before = sb("before", [P, E])
        shift_row = sb("shift_row", [P, E])
        passed = sb("passed", [P, NT, E])
        tile_e = sb("tile_e", [P, NT])
        tile_ei = sb("tile_ei", [P, NT], I32)
        tile_row = sb("tile_row", [P, NT])
        tile_rowi = sb("tile_rowi", [P, NT], I32)
        where = sb("where", [P, TT, E])
        pos = sb("pos", [P, TT])
        posi = sb("posi", [P, TT], U32)
        b1s = sb("b1s", [P, NT, 2 * HC])
        slots = sb("slots", [P, SLOTS, C])
        staged = sb("staged", [P, PIECES, HC * C])
        whigh = [sb(f"whigh{i}", [P, PIECES, HC * C], F32R) for i in range(2)]
        wlow = [sb(f"wlow{i}", [P, PIECES, HC * C], F32R) for i in range(2)]
        b2s = sb("b2s", [P, 2, C])
        xs = sb("xs", [P, 2, 2, C])
        xhigh = sb("xhigh", [P, 2, KC, ET], F32R)
        xlow = sb("xlow", [P, 2, KC, ET], F32R)
        work = sb("work", [P, 3, PAIR, ET])
        sig = work[:, 0:2]
        gated = work[:, 2]
        b1big = work[:].rearrange("p a c t -> p (a c t)")[:, 0:NT * HC * E]\
            .rearrange("p (t c e) -> p t c e", t=NT, c=HC)
        ghigh = sb("ghigh", [P, 2, PAIR, ET], F32R)
        glow = sb("glow", [P, 2, PAIR, ET], F32R)
        ys = sb("ys", [P, 2, 2, C])

        pool_step, vec_step = sem("pool_step2"), sem("vec_step2")
        located, tails_located, tails_in, posed = sem("located"), sem("tails_located"), sem("tails_in"), sem("posed")
        gathered = [sem(f"gathered{i}") for i in range(SLOTS)]
        out_stored = [sem(f"out_stored{i}") for i in range(SLOTS)]
        summed = sem("summed")
        w_in = [sem(f"w_in{i}") for i in range(PIECES)]
        w_high = [sem(f"w_high{i}") for i in range(PIECES)]
        w_split = [sem(f"w_split{i}") for i in range(PIECES)]
        b2_in = [sem("b2_in0"), sem("b2_in1")]
        xs_in = [sem("xs_in0"), sem("xs_in1")]
        y_stored = [sem("y_stored0"), sem("y_stored1")]
        x_turned, x_high, x_split = sem("x_turned"), sem("x_high"), sem("x_split")
        h_full, sig_done, h_done, g_high, g_split = (sem(k) for k in ("h_full", "sig_done", "h_done", "g_high", "g_split"))
        y_full, y_done, y_ready = sem("y_full"), sem("y_done"), sem("y_ready")
        block = st.enter_context(nc.Block())
        TURNS = (NT - 5) // 2

        def tiles(eng, tile):
            with eng.Fori(0, TURNS) as k:
                for par in range(2):
                    tile(k * 2 + par, par, k)
            for t in range(2 * TURNS, NT):
                tile(t, t % 2, t // 2)

        def exists(t):
            return not isinstance(t, int) or t < NT

        @block.sync
        def _(sp):
            def expert(t):
                return sp.value_load(tile_ei[0:1, bass.ds(t, 1)], min_val=0, max_val=E - 1)

            def load_piece(t, e, i, wait=True):
                if wait:
                    sp.wait_ge(w_split[i], t * (2 if i == KC else 1))
                if i < KC:
                    src = w1[bass.ds(e, 1), i * P:(i + 1) * P, :].rearrange("a p n -> p (a n)")
                    sp.dma_start(staged[:, i, :], src).then_inc(w_in[i], 16)
                else:
                    src = w2[bass.ds(e, 1)].rearrange("a (k p) n -> p (a k) n", p=P)
                    sp.dma_start(staged[:, i, :].rearrange("p (k n) -> p k n", k=HC), src).then_inc(w_in[i], 16)

            def load_bias(e, par):
                sp.dma_start(b2s[:, par, :], b2[bass.ds(e, 1), :].rearrange("a c -> (a c)").partition_broadcast(P))\
                    .then_inc(b2_in[par], 16)

            def rows(ap, t):
                return ap[bass.ds(t * ET, ET), :].rearrange("(k p) c -> p k c", p=P)

            def load_tokens(t, par):
                row = sp.value_load(tile_rowi[0:1, bass.ds(t, 1)], min_val=0, max_val=E * REGION - ET)
                sp.dma_start(xs[:, par], sorted_x[bass.ds(row, ET), :].rearrange("(k p) c -> p k c", p=P))\
                    .then_inc(xs_in[par], 16)

            sp.wait_ge(pool_step, 4)
            sp.wait_ge(tails_located, 1)
            for i in range(E):
                row = sp.value_load(tail_rowi[0:1, i:i + 1], min_val=0, max_val=E * REGION - ET)
                sp.dma_start(sorted_x[bass.ds(row, ET), :].rearrange("(k p) c -> p k c", p=P), slots[:, 0:2, :])\
                    .then_inc(tails_in, 16)
            sp.wait_ge(located, 1)
            e = expert(0)
            for i in range(KC):
                load_piece(0, e, i, wait=False)
            sp.wait_ge(located, 2)
            sp.wait_ge(scattered, SCATTERED * (B + 1))
            sp.wait_ge(tails_in, 16 * E)
            for t in range(2):
                load_tokens(t, t)
            load_piece(0, e, KC, wait=False)
            load_bias(e, 0)
            load_bias(expert(1), 1)
            e = expert(1)
            for i in range(PIECES):
                load_piece(1, e, i)
            sp.wait_ge(x_turned, 1)
            load_tokens(2, 0)
            e = expert(2)
            for i in range(KC):
                load_piece(2, e, i)
            sp.wait_ge(x_turned, 2)
            load_tokens(3, 1)

            def tile(t, par, turn):
                if exists(t + 2):
                    e = expert(t + 2)
                    load_piece(t + 2, e, KC)
                sp.wait_ge(y_ready, t + 1)
                sp.dma_start(rows(sorted_y, t), ys[:, par]).then_inc(y_stored[par], 16)
                if exists(t + 2):
                    load_bias(e, par)
                if exists(t + 3):
                    e = expert(t + 3)
                    for i in range(KC):
                        load_piece(t + 3, e, i)
                if exists(t + 4):
                    sp.wait_ge(x_turned, t + 3)
                    load_tokens(t + 4, par)

            tiles(sp, tile)
            for t in range(TT):
                sp.wait_ge(summed, t + 1)
                sp.dma_start(half_of(out, t // 2, t % 2), slots[:, t % SLOTS, :]).then_inc(out_stored[t % SLOTS], 16)
            for i in range(SLOTS):
                sp.wait_ge(out_stored[i], 16 * (TT // SLOTS))

        @block.gpsimd
        def _(pool):
            s = Steps(pool, pool_step)
            for dst, step in ((k_tiles, ET), (tile_no, 1), (region_row, REGION)):
                s.done(nc.gpsimd.iota(dst[:], pattern=[[step, dst.shape[1]]], base=0, channel_multiplier=0,
                                      allow_small_or_imprecise_dtypes=True))
            s.done(nc.gpsimd.memset(slots[:, 0:2, :], 0.0))

            def low_parts(t, par):
                for i, cols in ((1, slice(0, HC * C)), (2, slice(0, W2_POOL * C))):
                    if i == 1 and isinstance(t, int) and t == 0:
                        continue
                    pool.wait_ge(w_high[i], t + 1)
                    nc.gpsimd.tensor_tensor(wlow[par][:, i, cols], staged[:, i, cols],
                                            whigh[par][:, i, cols].bitcast(F32), ALU.subtract).then_inc(w_split[i], 1)

            low_parts(0, 0)

            def tile(t, par, turn):
                if exists(t + 1):
                    low_parts(t + 1, 1 - par)
                pool.wait_ge(y_done, t + 2)
                pool.wait_ge(b2_in[par], (turn + 1) * 16)
                nc.gpsimd.tensor_tensor(ys[:, par], ys[:, par], b2s[:, par:par + 1, :].to_broadcast([P, 2, C]),
                                        ALU.add).then_inc(y_ready, 1)

            tiles(pool, tile)
            pool.wait_ge(y_stored[0], 16 * ((NT + 1) // 2 + 1))
            pool.wait_ge(y_stored[1], 16 * (NT // 2 + 1))
            pool.wait_ge(posed, 1)
            pool.wait_ge(tails_in, 16 * E)
            for t in range(TT):
                if t >= SLOTS:
                    pool.wait_ge(out_stored[t % SLOTS], 16 * (t // SLOTS))
                nc.gpsimd.indirect_dma_start(
                    out=slots[:, t % SLOTS, :], out_offset=None, in_=sorted_y[:, :],
                    in_offset=bass.IndirectOffsetOnAxis(ap=posi[:, t:t + 1], axis=0)).then_inc(gathered[t % SLOTS], 16)

        @block.vector
        def _(dve):
            s = Steps(dve, vec_step)
            tt, reduce = nc.vector.tensor_tensor, nc.vector.tensor_reduce
            dve.wait_ge(pool_step, 4)

            def over_experts(ap, n=TT):
                return ap.unsqueeze(2).to_broadcast([P, n, E])

            def over(ap, n=TT):
                return ap.unsqueeze(1).to_broadcast([P, n, E])

            s.done(tt(tail_row[:], region_row[:], counts[:], ALU.add))
            then(dve, nc.vector.tensor_copy(tail_rowi[:], tail_row[:]), tails_located, 1)
            nk = B * N // ET
            s.done(tt(cmp[:], counts[:].unsqueeze(2).to_broadcast([P, E, nk]),
                      k_tiles[:].unsqueeze(1).to_broadcast([P, E, nk]), ALU.is_gt))
            s.done(reduce(ntiles[:], cmp[:], axis=X, op=ALU.add))
            s.done(nc.vector.tensor_copy(ends[:, 0, :], ntiles[:]))
            c = 0
            for step in (1, 2, 4):
                s.done(nc.vector.tensor_copy(ends[:, 1 - c, 0:step], ends[:, c, 0:step]))
                s.done(tt(ends[:, 1 - c, step:E], ends[:, c, step:E], ends[:, c, 0:E - step], ALU.add))
                c = 1 - c
            s.done(tt(passed[:], over_experts(tile_no[:], NT), over(ends[:, c, :], NT), ALU.is_ge))
            s.done(reduce(tile_e[:], passed[:], axis=X, op=ALU.add))
            s.done(nc.vector.tensor_scalar(tile_e[:], tile_e[:], float(E - 1), None, ALU.min))
            then(dve, nc.vector.tensor_copy(tile_ei[:], tile_e[:]), located, 1)
            s.done(nc.vector.tensor_scalar(tile_e[:], tile_e[:], -float(E), None, ALU.add))
            s.done(tt(passed[:], over_experts(tile_e[:], NT), over(e_less_8[:], NT), ALU.is_equal))
            s.done(tt(before[:], ends[:, c, :], ntiles[:], ALU.subtract))
            s.done(nc.vector.tensor_scalar(before[:], before[:], float(ET), None, ALU.mult))
            s.done(tt(shift_row[:], region_row[:], before[:], ALU.subtract))
            s.done(tt(where[:, 0:NT], passed[:], over(shift_row[:], NT), ALU.mult))
            s.done(reduce(tile_row[:], where[:, 0:NT], axis=X, op=ALU.add))
            s.done(nc.vector.scalar_tensor_tensor(tile_row[:], tile_no[:], float(ET), tile_row[:], ALU.mult, ALU.add))
            s.done(nc.vector.tensor_scalar(tile_row[:], tile_row[:], tail_row[:, E - 1:E], None, ALU.min))
            then(dve, nc.vector.tensor_copy(tile_rowi[:], tile_row[:]), located, 2)
            s.done(tt(where[:], over(e_less_8[:]), over_experts(first[:].rearrange("p b k -> p (b k)")), ALU.is_equal))
            s.done(tt(where[:], where[:], over(before[:]), ALU.mult))
            s.done(reduce(pos[:], where[:], axis=X, op=ALU.add))
            s.done(tt(pos[:], pos[:], place[:].rearrange("p b k -> p (b k)"), ALU.add))
            then(dve, nc.vector.tensor_copy(posi[:], pos[:]), posed, 1)
            for part in range(2):
                cols = slice(part * HC, (part + 1) * HC)
                s.done(tt(b1big, passed[:].unsqueeze(2).to_broadcast([P, NT, HC, E]),
                          b1T[:, :, cols].rearrange("p e c -> p c e").unsqueeze(1).to_broadcast([P, NT, HC, E]), ALU.mult))
                s.done(reduce(b1s[:, :, cols], b1big, axis=X, op=ALU.add))
            nc.vector.memset(cmp[:, 0, 0:1], 0.0).then_inc(y_done, 1)
            nc.vector.memset(cmp[:, 0, 1:2], 0.0).then_inc(h_done, 2)
            for i in range(2):
                nc.vector.memset(cmp[:, 0, 2 + i:3 + i], 0.0).then_inc(y_stored[i], 16)

            def low_part(t, par, i=0):
                dve.wait_ge(w_high[i], t + 1)
                tt(wlow[par][:, i, :], staged[:, i, :], whigh[par][:, i, :].bitcast(F32), ALU.subtract)\
                    .then_inc(w_split[i], 1)

            def low_part2(t, par):
                cols = slice(W2_POOL * C, HC * C)
                dve.wait_ge(w_high[2], t + 1)
                tt(wlow[par][:, 2, cols], staged[:, 2, cols], whigh[par][:, 2, cols].bitcast(F32), ALU.subtract)\
                    .then_inc(w_split[2], 1)

            def low_tokens(t, par):
                dve.wait_ge(x_high, t + 1)
                tt(xlow[:, par], psT[:], xhigh[:, par].bitcast(F32), ALU.subtract).then_inc(x_split, 1)

            def gate(t, q):
                item = t * PAIRS_HID + q
                dve.wait_ge(sig_done, item + 1)
                for c in range(PAIR):
                    ins = nc.vector.scalar_tensor_tensor(
                        gated[:, c, :], psH[:, q % 2 * PAIR + c, 0, :], b1s[:, bass.ds(t, 1), q * PAIR + c],
                        sig[:, q % 2, c, :], ALU.add, ALU.mult)
                then(dve, ins, h_done, item + 3)
                then(dve, nc.vector.tensor_copy(ghigh[:, q % 2], gated), g_high, item + 1)
                then(dve, tt(glow[:, q % 2], gated, ghigh[:, q % 2].bitcast(F32), ALU.subtract), g_split, item + 1)

            def tile(t, par, turn):
                for q in range(1, PAIRS_HID):
                    gate(t, q)
                    if q == 1 and exists(t + 1):
                        low_part(t + 1, 1 - par)
                    if q == 2 and exists(t + 1):
                        low_tokens(t + 1, 1 - par)
                    if q == 3 and exists(t + 1):
                        low_part2(t + 1, 1 - par)
                if exists(t + 1):
                    gate(t + 1, 0)

            low_part(0, 0)
            low_part(0, 0, 1)
            low_tokens(0, 0)
            low_part2(0, 0)
            gate(0, 0)
            tiles(dve, tile)
            for t in range(TT):
                dve.wait_ge(gathered[t % SLOTS], 16 * (t // SLOTS + 1))
                tt(slots[:, t % SLOTS, :], slots[:, t % SLOTS, :], x2[:, t // 2, t % 2, :], ALU.add).then_inc(summed, 1)

        @block.scalar
        def _(act):
            def high_part(t, par, i):
                act.wait_ge(w_in[i], 16 * (t + 1))
                nc.scalar.activation(whigh[par][:, i, :], staged[:, i, :], ACT.Copy).then_inc(w_high[i], 1)

            def high_tokens(t, par):
                act.wait_ge(x_turned, t + 1)
                nc.scalar.activation(xhigh[:, par], psT[:], ACT.Copy).then_inc(x_high, 1)

            def sigmoids(t, q):
                item = t * PAIRS_HID + q
                act.wait_ge(h_full, item + 1)
                act.wait_ge(h_done, item + 1)
                for c in range(PAIR):
                    ins = nc.scalar.activation(sig[:, q % 2, c, :], psH[:, q % 2 * PAIR + c, 1, :], ACT.Sigmoid,
                                               bias=b1s[:, bass.ds(t, 1), HC + q * PAIR + c])
                then(act, ins, sig_done, item + 1)

            def tile(t, par, turn):
                for q in range(1, PAIRS_HID):
                    if exists(t + 1):
                        high_part(t + 1, 1 - par, q - 1)
                    if q == 3 and exists(t + 1):
                        high_tokens(t + 1, 1 - par)
                    sigmoids(t, q)
                if exists(t + 1):
                    sigmoids(t + 1, 0)
                act.wait_ge(y_full, t + 2)
                act.wait_ge(y_stored[par], turn * 16 + 16)
                then(act, nc.scalar.activation(ys[:, par], psY[:, :, 0:C], ACT.Copy), y_done, t + 2)

            for i in range(KC):
                high_part(0, 0, i)
            high_tokens(0, 0)
            high_part(0, 0, KC)
            act.wait_ge(h_done, 2)
            sigmoids(0, 0)
            tiles(act, tile)

        @block.tensor
        def _(pe):
            mm = nc.tensor.matmul
            nc.tensor.transpose(psT[:, 0, 0:P], ident[:], ident[:]).then_inc(x_split, 1)
            nc.tensor.transpose(psT[:, 0, P:2 * P], ident[:], ident[:]).then_inc(y_full, 1)

            def turn_tokens(t, par, turn):
                pe.wait_ge(xs_in[par], (turn + 1) * 16)
                pe.wait_ge(x_split, t + 1)
                for c in range(KC):
                    for half in range(2):
                        ins = nc.tensor.transpose(psT[:, c, half * P:(half + 1) * P],
                                                  xs[:, par, half, c * P:(c + 1) * P], ident[:])
                ins.then_inc(x_turned, 1)

            def hidden(t, par, q):
                if q == 0:
                    pe.wait_ge(x_split, t + 2)
                    pe.wait_ge(w_split[0], t + 1)
                    pe.wait_ge(w_split[1], t + 1)
                pe.wait_ge(h_done, t * PAIRS_HID + q + 1)
                for c in range(PAIR):
                    for part in range(2):
                        w = part * HID + (q * PAIR + c) * P
                        passes = [(lhs[par][:, k, w:w + P], rhs[:, par, k, :]) for k in range(KC)
                                  for lhs, rhs in ((whigh, xhigh), (whigh, xlow), (wlow, xhigh))]
                        for i, (lhs, rhs) in enumerate(passes):
                            ins = mm(psH[:, q % 2 * PAIR + c, part, :], lhs, rhs, start=i == 0, stop=i == len(passes) - 1)
                ins.then_inc(h_full, 1)

            def down(t, par, q):
                pe.wait_ge(g_split, t * PAIRS_HID + q + 1)
                if q == 0:
                    pe.wait_ge(w_split[KC], t * 2 + 2)
                    pe.wait_ge(y_done, t + 1)
                for c in range(PAIR):
                    k = q * PAIR + c
                    for half in range(2):
                        for i, (lhs, rhs) in enumerate(((ghigh, whigh), (ghigh, wlow), (glow, whigh))):
                            ins = mm(psY[:, half, 0:C], lhs[:, q % 2, c, half * P:(half + 1) * P],
                                     rhs[par][:, KC, k * C:(k + 1) * C],
                                     start=k == 0 and i == 0, stop=k == HC - 1 and i == 2)
                if q == PAIRS_HID - 1:
                    ins.then_inc(y_full, 1)

            def tile(t, par, turn):
                for q in range(1, PAIRS_HID):
                    hidden(t, par, q)
                    if q == 2 and exists(t + 1):
                        turn_tokens(t + 1, 1 - par, turn + par)
                    down(t, par, q - 1)
                if exists(t + 1):
                    hidden(t + 1, 1 - par, 0)
                down(t, par, PAIRS_HID - 1)

            turn_tokens(0, 0, 0)
            hidden(0, 0, 0)
            tiles(pe, tile)


_NAMES = ["x", "ctx_768", "L0_attn_w_qkv", "L0_attn_b_qkv", "L0_attn_w_proj", "L0_attn_b_proj", "L0_attn_bias_table",
          "L0_xattn_Wq", "L0_xattn_Wk", "L0_xattn_Wv", "L0_xattn_Wo", "L0_xattn_bo", "L0_ffn_router_w",
          "L0_ffn_router_b", "L0_ffn_w1", "L0_ffn_b1", "L0_ffn_w2", "L0_ffn_b2"]


def kernel(**inputs):
    import numpy as np
    import concourse.bacc as bacc
    from concourse.bass_utils import run_bass_kernel_spmd

    nc = bacc.Bacc("TRN2", target_bir_lowering=False, num_devices=1)
    arrays = {f"in_{k}": np.ascontiguousarray(inputs[k]) for k in _NAMES}
    args = [nc.dram_tensor(k, a.shape, mybir.dt.from_np(a.dtype), kind="ExternalInput").ap() for k, a in arrays.items()]
    out = nc.dram_tensor("out", (B, N, C), F32, kind="ExternalOutput").ap()
    decoder_layer(nc, *args, out)
    return run_bass_kernel_spmd(nc, [arrays], core_ids=[0]).results[0]["out"]
```
